# Optimizing a Trainium2 kernel written in Bass

```python
import numpy as np
import jax
import jax.numpy as jnp

def _softmax(x, axis=-1):
    return jax.nn.softmax(x, axis=axis)

def _gelu(x):
    return jax.nn.gelu(x, approximate=True)

def _silu(x):
    return jax.nn.silu(x)

def _sigmoid(x):
    return jax.nn.sigmoid(x)

def _layernorm(x, axis=-1, eps=1e-05):
    m = jnp.mean(x, axis=axis, keepdims=True)
    v = jnp.var(x, axis=axis, keepdims=True)
    return (x - m) / jnp.sqrt(v + eps)

def _scatter_add(tgt, idx, src, axis=0):
    return tgt.at[idx].add(src)

def _segment_sum(src, seg, n):
    return jax.ops.segment_sum(src, seg, n)
kernel_name = 'mk_decoder_postln_d1_seqx_r8_813bde'

def setup_inputs(seed: int=0):
    np.random.seed(seed)
    _w = jnp.asarray

    def _rec_inputs():
        import jax
        import jax.numpy as jnp
        _rk = jax.random.key(seed)
        x = -0.0002928 + 1 * jax.random.normal(jax.random.fold_in(_rk, 1), (64, 64, 128), jnp.float32)
        _lenS = 64 - jax.random.randint(jax.random.fold_in(_rk, 7), (64,), 0, max(1, 64 // 4) + 1, jnp.int32)
        _lenS2 = 64 - jax.random.randint(jax.random.fold_in(_rk, 8), (64,), 0, max(1, 64 // 4) + 1, jnp.int32)
        _ctx_1024P = jax.random.normal(jax.random.fold_in(_rk, 11), (64, 16, 128), jnp.float32)
        _ctx_1024c = jax.random.dirichlet(jax.random.fold_in(_rk, 511), 0.3 * jnp.ones((16,), jnp.float32), (64, 64))
        _ctx_1024t = jnp.einsum('bsk,bkd->bsd', _ctx_1024c, _ctx_1024P)
        _ctx_1024t = _ctx_1024t * jax.lax.rsqrt(jnp.mean(jnp.square(_ctx_1024t)) + 1e-12) * 0.953939
        ctx_1024 = -1.39393e-06 + 0.999914 * (_ctx_1024t + 0.3 * jax.random.normal(jax.random.fold_in(_rk, 611), (64, 64, 128), jnp.float32))
        _validS = jnp.arange(64)[None, :] < _lenS[:, None]
        _validS2 = jnp.arange(64)[None, :] < _lenS2[:, None]
        _causal = jnp.tril(jnp.ones((64, 64), dtype=bool))
        mask_1x1xSxS2_bf1 = jnp.ones((1, 1, 64, 64), dtype=bool)
        return (x, ctx_1024, mask_1x1xSxS2_bf1)
    x, ctx_1024, mask_1x1xSxS2_bf1 = _rec_inputs()

    def _L0_attn_setup():
        import jax, jax.numpy as jnp
        import numpy as np
        D_MODEL = 128
        HEADS = 16
        SCALE = float(np.sqrt(D_MODEL / HEADS))
        key = jax.random.key(seed)
        ks = jax.random.split(key, 5)
        B, S, D = (4, 256, D_MODEL)
        q = jax.random.normal(ks[0], (B, S, D), dtype=jnp.float32)
        init = 0.02
        wq = jax.random.normal(ks[1], (D, D), dtype=jnp.float32) * init
        wk = jax.random.normal(ks[2], (D, D), dtype=jnp.float32) * init
        wv = jax.random.normal(ks[3], (D, D), dtype=jnp.float32) * init
        wo = jax.random.normal(ks[4], (D, D), dtype=jnp.float32) * init
        return {'q': q, 'wq': wq, 'wk': wk, 'wv': wv, 'wo': wo}
    _L0_attn_all = _L0_attn_setup()
    _L0_attn_in = {k: v for k, v in _L0_attn_all.items() if k in ('wq', 'wk', 'wv', 'wo')}
    del _L0_attn_all

    def _L0_xattn_setup():
        import jax, jax.numpy as jnp
        import numpy as np
        D_MODEL = 128
        H = 16
        D_K = D_MODEL // H
        key = jax.random.key(seed)
        ks = jax.random.split(key, 8)
        B, S = (2, 256)
        q = jax.random.normal(ks[0], (B, S, D_MODEL), dtype=jnp.float32)
        k = jax.random.normal(ks[1], (B, S, D_MODEL), dtype=jnp.float32)
        v = jax.random.normal(ks[2], (B, S, D_MODEL), dtype=jnp.float32)
        mask = jnp.ones((1, 1, S, S), dtype=bool)
        scale = 1.0 / np.sqrt(D_MODEL)
        w_q = jax.random.normal(ks[3], (D_MODEL, D_MODEL), dtype=jnp.float32) * scale
        w_k = jax.random.normal(ks[4], (D_MODEL, D_MODEL), dtype=jnp.float32) * scale
        w_v = jax.random.normal(ks[5], (D_MODEL, D_MODEL), dtype=jnp.float32) * scale
        w_o = jax.random.normal(ks[6], (D_MODEL, D_MODEL), dtype=jnp.float32) * scale
        return {'q': q, 'k': k, 'v': v, 'mask': mask, 'w_q': w_q, 'w_k': w_k, 'w_v': w_v, 'w_o': w_o}
    _L0_xattn_all = _L0_xattn_setup()
    _L0_xattn_in = {k: v for k, v in _L0_xattn_all.items() if k in ('w_q', 'w_k', 'w_v', 'w_o')}
    del _L0_xattn_all

    def _L0_ffn_setup():
        import jax, jax.numpy as jnp
        import numpy as np
        HIDDEN = 128
        NUM_EXPERTS = 8
        TOP_K = 2
        B, S = (2, 256)
        key = jax.random.key(seed)
        k1, k2, k3, k4, k5 = jax.random.split(key, 5)
        d, dff, E = (HIDDEN, 4 * HIDDEN, NUM_EXPERTS)
        x = jax.random.normal(k1, (B, S, d), dtype=jnp.float32)
        W1 = jax.random.normal(k2, (E, d, dff), dtype=jnp.float32) * (1.0 / np.sqrt(d))
        b1 = jax.random.normal(k3, (E, dff), dtype=jnp.float32) * 0.01
        W2 = jax.random.normal(k4, (E, dff, d), dtype=jnp.float32) * (1.0 / np.sqrt(dff))
        b2 = jax.random.normal(k5, (E, d), dtype=jnp.float32) * 0.01
        return {'x': x, 'W1': W1, 'b1': b1, 'W2': W2, 'b2': b2}
    _L0_ffn_all = _L0_ffn_setup()
    _L0_ffn_in = {k: v for k, v in _L0_ffn_all.items() if k in ('W1', 'b1', 'W2', 'b2')}
    del _L0_ffn_all
    return {'x': x, 'ctx_1024': ctx_1024, 'mask_1x1xSxS2_bf1': mask_1x1xSxS2_bf1, 'L0_attn_wq': _L0_attn_in['wq'], 'L0_attn_wk': _L0_attn_in['wk'], 'L0_attn_wv': _L0_attn_in['wv'], 'L0_attn_wo': _L0_attn_in['wo'], 'L0_xattn_w_q': _L0_xattn_in['w_q'], 'L0_xattn_w_k': _L0_xattn_in['w_k'], 'L0_xattn_w_v': _L0_xattn_in['w_v'], 'L0_xattn_w_o': _L0_xattn_in['w_o'], 'L0_ffn_W1': _L0_ffn_in['W1'], 'L0_ffn_b1': _L0_ffn_in['b1'], 'L0_ffn_W2': _L0_ffn_in['W2'], 'L0_ffn_b2': _L0_ffn_in['b2']}

def reference(x, ctx_1024, mask_1x1xSxS2_bf1, L0_attn_wq, L0_attn_wk, L0_attn_wv, L0_attn_wo, L0_xattn_w_q, L0_xattn_w_k, L0_xattn_w_v, L0_xattn_w_o, L0_ffn_W1, L0_ffn_b1, L0_ffn_W2, L0_ffn_b2):
    import jax
    import jax.numpy as jnp

    def _L0_attn_ref(q, wq, wk, wv, wo):
        import jax, jax.numpy as jnp
        import numpy as np
        D_MODEL = 128
        HEADS = 16
        SCALE = float(np.sqrt(D_MODEL / HEADS))
        B, S, D = q.shape
        Q = jnp.einsum('bsd,ed->bse', q, wq)
        K = jnp.einsum('bsd,ed->bse', q, wk)
        V = jnp.einsum('bsd,ed->bse', q, wv)
        scores = jnp.einsum('bqe,bke->bqk', Q, K) / SCALE
        attn = jax.nn.softmax(scores, axis=-1)
        out = jnp.einsum('bqk,bke->bqe', attn, V)
        out = jnp.transpose(out, (0, 2, 1)).reshape(B, S, D)
        return jnp.einsum('bsd,ed->bse', out, wo)

    def _L0_xattn_ref(q, k, v, mask, w_q, w_k, w_v, w_o):
        import jax, jax.numpy as jnp
        import numpy as np
        D_MODEL = 128
        H = 16
        D_K = D_MODEL // H
        B, S, _ = q.shape

        def proj(x, w):
            y = jnp.einsum('bsd,ed->bse', x, w)
            return y.reshape(B, S, H, D_K).transpose(0, 2, 1, 3)
        query, key_, value = (proj(q, w_q), proj(k, w_k), proj(v, w_v))
        scores = jnp.einsum('bhqd,bhkd->bhqk', query, key_) / jnp.sqrt(jnp.asarray(D_K, dtype=query.dtype))
        scores = jnp.where(mask, scores, jnp.asarray(-1000000000.0, dtype=scores.dtype))
        attn = jax.nn.softmax(scores, axis=-1)
        x = jnp.einsum('bhqk,bhkd->bhqd', attn, value)
        x = x.transpose(0, 2, 1, 3).reshape(B, S, D_MODEL)
        return jnp.einsum('bsd,ed->bse', x, w_o)

    def _L0_ffn_ref(x, W1, b1, W2, b2):
        import jax, jax.numpy as jnp
        import numpy as np
        HIDDEN = 128
        NUM_EXPERTS = 8
        TOP_K = 2
        B, S = (2, 256)
        Bm, Sm, d = x.shape
        E = W1.shape[0]
        x_flat = x.reshape(-1, d)
        h = jnp.mod(x_flat[:, :TOP_K].sum(axis=1).astype(jnp.int32), E)
        sel = jnp.stack([h, jnp.mod(h + 1, E)], axis=1)

        def step(acc, params):
            e, W1e, b1e, W2e, b2e = params
            w = jnp.any(sel == e, axis=1).astype(x.dtype) / TOP_K
            y = jnp.maximum(x_flat @ W1e + b1e, 0.0) @ W2e + b2e
            return (acc + w[:, None] * y, None)
        init = jnp.zeros_like(x_flat)
        out_flat, _ = jax.lax.scan(step, init, (jnp.arange(E), W1, b1, W2, b2))
        return out_flat.reshape(Bm, Sm, d)
    x = _layernorm(x + _L0_attn_ref(x, L0_attn_wq, L0_attn_wk, L0_attn_wv, L0_attn_wo), axis=-1)
    x = _layernorm(x + _L0_xattn_ref(x, ctx_1024, ctx_1024, mask_1x1xSxS2_bf1, L0_xattn_w_q, L0_xattn_w_k, L0_xattn_w_v, L0_xattn_w_o), axis=-1)
    x = _layernorm(x + _L0_ffn_ref(x, L0_ffn_W1, L0_ffn_b1, L0_ffn_W2, L0_ffn_b2), axis=-1)
    return x

_drawn_inputs = setup_inputs


def setup_inputs(seed=0):
    import zlib

    import numpy as np

    out = dict(_drawn_inputs(seed))
    spreads = {}
    factors = {'L0_attn_wq': 5.201,
     'L0_attn_wk': 3.523,
     'L0_attn_wv': 2.763,
     'L0_ffn_b1': 8.0,
     'L0_ffn_b2': 8.0}
    for name, (base, spread) in spreads.items():
        noise = np.random.default_rng([zlib.crc32(name.encode()), seed]).standard_normal(out[name].shape)
        drawn = base * np.exp(spread * noise) if base else spread * noise
        out[name] = jnp.asarray(drawn.astype(out[name].dtype))
    for name, factor in factors.items():
        out[name] = (out[name] * factor).astype(out[name].dtype)
    return out
```

```python
from contextlib import ExitStack

import numpy as np
import concourse.bass as bass
from concourse import mybir

F32 = mybir.dt.float32
F16 = mybir.dt.float16
BF16 = mybir.dt.bfloat16
I32 = mybir.dt.int32
U8 = mybir.dt.uint8
ALU = mybir.AluOpType
ACT = mybir.ActivationFunctionType
AX = mybir.AxisListType

P = 128
EPS = 1e-5
ROUND = 12582912.0
PRODUCTS = ((0, 0), (1, 0), (0, 1))


def decoder_layer_kernel(nc, x, ctx, mask, a_wq, a_wk, a_wv, a_wo, c_wq, c_wk, c_wv, c_wo, W1, b1, W2, b2, out):
    B, S, D = x.shape
    H, DK = 16, D // 16
    NE, _, FF = W1.shape
    FC = FF // P
    TG = 4
    BG = TG * P // S
    NG = B * S // (TG * P)
    GT = TG * P
    VW = DK + 1
    NHP = H // 2
    A_SCALE = 1.0 / float(np.sqrt(D // 16))
    C_SCALE = 1.0 / float(np.sqrt(DK))
    N = B * S
    REGION = N + P
    DUMMY = NE * REGION
    ROW = D + 4
    SLOTS = N // P + NE
    assert D == P and S == 64 and TG * P == 512 and NG == NE and SLOTS % 2 == 0

    sorted_rows = nc.dram_tensor("sorted_rows", (DUMMY + P, ROW), F32).ap()

    x_flat = x.rearrange("b s d -> (b s d)")
    ctx_flat = ctx.rearrange("b s d -> (b s d)")
    W1_flat = W1.rearrange("e d f -> (e d f)")
    W2_flat = W2.rearrange("e f d -> (e f d)")
    out_rows = out.rearrange("b s d -> (b s) d")

    with ExitStack() as stack:
        def sb(name, shape, dt=F32):
            return stack.enter_context(nc.sbuf_tensor(name, shape, dt))

        def sem(name):
            return stack.enter_context(nc.semaphore(name))

        ident = sb("ident", [P, P])
        ident_bf = sb("ident_bf", [P, P], BF16)
        ones_bf = sb("ones_bf", [P, P], BF16)
        before = sb("before", [P, P], BF16)
        iota_e = sb("iota_e", [P, NE])
        iota_slot = sb("iota_slot", [P, SLOTS])
        region_e = sb("region_e", [P, NE])
        iota_p = sb("iota_p", [P, 1])
        pad_rows = sb("pad_rows", [P, ROW])
        mask_u8 = sb("mask_u8", [P, S], U8)
        mask_f = sb("mask_f", [P, S])
        mask_two = sb("mask_two", [P, 2, S])
        mask_bias = sb("mask_bias", [P, S], BF16)
        any_key = sb("any_key", [P, 1])
        pick = sb("pick", [P, NHP, 2, S], BF16)
        negmax = sb("negmax", [P, 2, P], BF16)

        w_raw = sb("w_raw", [P, 8, P])
        aqk = sb("aqk", [P, 2, P], F16)
        avT = sb("avT", [P, 2, P], F16)
        aoT = sb("aoT", [P, 2, 2, P], F16)
        cqT = sb("cqT", [P, 2, P], F16)
        ckT = sb("ckT", [P, 2, P], F16)
        cvT = sb("cvT", [P, 2, P], F16)
        coT = sb("coT", [P, 2, P], F16)
        w_wo2 = sb("w_wo2", [P, 2, P])
        w_stage = sb("w_stage", [P, 2, FF])
        w1 = sb("w1", [P, 2, (NE + 1) * FF], F16)
        w2 = sb("w2", [P, 2, (NE + 1) * FF], F16)
        b1_raw = sb("b1_raw", [NE * FC, P])
        b1c = sb("b1c", [P, (NE + 1) * FC])
        b2_all = sb("b2_all", [P, (NE + 1) * D])
        b2_pair = sb("b2_pair", [P, NE * D])

        x_in = sb("x_in", [P, TG, D])
        x_res = sb("x_res", [P, TG, D])
        xT = sb("xT", [P, 2, GT], F16)
        gT = sb("gT", [P, 2, GT], F16)
        av = sb("av", [P, 2, GT], F16)
        a_max = sb("a_max", [P, TG])
        a_shift = sb("a_shift", [P, TG, S])
        a_prob = sb("a_prob", [P, TG, 2, S])
        a_sum = sb("a_sum", [P, TG])
        a_rinv = sb("a_rinv", [P, TG])
        apT = sb("apT", [P, 2, GT], F16)
        a_out = sb("a_out", [P, TG, D])
        a_diag = sb("a_diag", [P, 2, TG, 2, 2, S], F16)
        a_r = sb("a_r", [P, TG, D])
        x1 = sb("x1", [P, NG * GT])

        c_in = sb("c_in", [P, TG, D])
        cT = sb("cT", [P, 2, GT], F16)
        kT = sb("kT", [P, 2, 2, GT // 2], F16)
        k_rows = sb("k_rows", [P, 2, 2, BG // 2, 4, S], F16)
        q_quad = sb("q_quad", [P, 2, 4, GT], F16)
        in_place4 = sb("in_place4", [P, 4, 4])
        in_place = sb("in_place", [P, 4])
        v_pair = sb("v_pair", [P, 2, BG, NHP, 2, VW], F16)
        x1q = sb("x1q", [P, TG, D])
        x1T = sb("x1T", [P, 2, GT], F16)
        qT = sb("qT", [P, 2, GT], F16)
        c_max = sb("c_max", [P, 2, H])
        p_f = sb("p_f", [P, 2, GT])
        p_hl = sb("p_hl", [P, 2, 2, 2, GT], F16)
        c_rinv = sb("c_rinv", [P, H])
        c_out = sb("c_out", [P, TG, D])
        oT = sb("oT", [P, 2, GT], F16)
        c_r = sb("c_r", [P, TG, D])
        x2 = sb("x2", [P, TG, ROW])

        st = sb("st", [P, TG, 6])
        ln = sb("ln", [P, 8, TG])
        ln_i = sb("ln_i", [P, 2, TG], I32)
        rt = sb("rt", [P, 8, TG])
        onehot = sb("onehot", [P, TG, NE])
        onehot_bf = sb("onehot_bf", [P, TG, NE], BF16)
        place = sb("place", [P, TG, NE])
        pos_f = sb("pos_f", [P, TG])
        pos_i = sb("pos_i", [P, TG], I32)
        token_f = sb("token_f", [P, TG])
        base = sb("base", [P, NE])
        count = sb("count", [P, NE])
        pad_f = sb("pad_f", [P, NE])
        pad_i = sb("pad_i", [P, NE], I32)
        tiles_e = sb("tiles_e", [P, 4, NE])
        done_e = sb("done_e", [P, 2, SLOTS, NE])
        slot_f = sb("slot_f", [P, 8, SLOTS])
        slot_row = sb("slot_row", [P, SLOTS], I32)
        slot_w = sb("slot_w", [P, SLOTS], I32)
        slot_b1 = sb("slot_b1", [P, SLOTS], I32)
        slot_b2 = sb("slot_b2", [P, SLOTS], I32)

        xs = sb("xs", [P, 3, ROW])
        xsT = sb("xsT", [P, 2, 2, P], F16)
        h_f = sb("h_f", [P, 2, FF])
        h_hl = sb("h_hl", [P, 2, 2, FF], F16)
        y_r = sb("y_r", [P, 2, D])
        y_t = sb("y_t", [P, 2, D])
        f_st = sb("f_st", [P, 2, 6])
        f_mv = sb("f_mv", [P, 2, 2])
        f_sd = sb("f_sd", [P, 2, 2])
        y_out = sb("y_out", [P, 2, D])
        y_id = sb("y_id", [P, 2, 1], I32)
        eps_t = sb("eps_t", [P, 1])

        psum = [stack.enter_context(nc.psum_tensor(f"psum{i}", [P, 512], F32)) for i in range(8)]
        s_bank, t_bank = psum[0:2], psum[2:4]
        o_bank, m_bank, a_bank, b_bank = psum[4:8]

        names = """sp_passed const_loaded wstage_loaded xin_loaded xres_loaded cin_loaded q_spread k_rows_ready dve_step y_step
            consts_pool consts_dve pe_setup act_setup dve_setup wsplit_hi wsplit_lo
            xT_ps xT_hi xT_lo gT_ps gT_hi gT_lo av_ps av_hi av_lo as_ps as_shifted as_exp as_rinv
            apT_ps apT_hi apT_lo ao_ps ao_scaled adiag_hi adiag_lo ay_ps a_read x1_ready
            cT_ps cT_hi cT_lo kT_ps kT_hi kT_lo v_ps v_hi v_lo x1q_ready x1T_ps x1T_hi x1T_lo
            qT_ps qT_hi qT_lo s_ps max_ready mT_ps nm_hi nm_lo st_ps exp_ready p_hi p_lo pv_ps co_ready
            oT_ps oT_hi oT_lo cy_ps c_read x2_ready onehot_ready rank_ps rank_read pos_ready scattered
            tables_ready wrapped pads_ready pad_written xs_loaded0 xs_loaded1 xs_loaded2 xsT_ps xsT_hi xsT_lo
            h_ps h_relu h_hi h_lo y_ps y_read y_var y_sd y_ready y_written0 y_written1""".split()
        s = {n: sem(n) for n in names}

        def after(eng, name, value):
            if isinstance(value, int) and value <= 0:
                return
            eng.wait_ge(s[name], value)

        def counts(eng, *values):
            return [v if isinstance(v, int) else eng.snap(v) for v in values]

        def passed(eng):
            eng.sem_inc(s["sp_passed"], 1)

        class Steps:
            def __init__(self, eng, name):
                self.eng, self.name, self.start, self.n = eng, name, 0, 0

            def link(self, ins):
                ins.then_inc(s[self.name], 1)
                self.n += 1
                self.eng.wait_ge(s[self.name], self.start + self.n)

        def loop(eng, body, chain=None):
            body(0, 1, None)
            if chain is not None:
                first = chain.n
                trial = chain.per_body
                with eng.Fori(1, NG - 1) as g:
                    chain.start, chain.n = first + (g - 1) * trial, 0
                    body(g, g + 1, g - 1)
                    assert chain.n == trial, chain.n
                chain.start, chain.n = first + (NG - 2) * trial, 0
            else:
                with eng.Fori(1, NG - 1) as g:
                    body(g, g + 1, g - 1)
            body(NG - 1, None, NG - 2)

        def by_parity(ap):
            return ap.rearrange("p (a n v) -> p a n v", a=2, v=DK)

        def even_odd(ap):
            return ap.rearrange("p (n a v) -> p a n v", a=2, v=DK)

        def bc(ap, shape):
            return ap.broadcast_to(shape)

        SETUP_ORDER = (0, 1, 4, 5, 6, 7, 2, 3)
        SETUP_SPLITS = ((0, aqk), (1, avT), (4, cqT), (5, ckT), (6, cvT), (7, coT), (2, aoT[:, 0]), (3, aoT[:, 1]))
        SETUP_PS = len(SETUP_ORDER) + 1
        DVE_SETUP = len(SETUP_SPLITS) + 1
        POOL_CONSTS = 26
        ROUNDS = (SLOTS - 1) // 6
        DVE_BODY = 58

        block = stack.enter_context(nc.Block())

        @block.sync
        def _(sp):
            def tokens(flat, at):
                return flat[bass.ds(at, GT * D)].rearrange("(t p d) -> p t d", t=TG, p=P)

            def load_x(g):
                at, used = counts(sp, g * GT * D, g)
                after(sp, "xT_ps", used)
                passed(sp)
                sp.dma_start(x_in[:], tokens(x_flat, at)).then_inc(s["xin_loaded"], 16)

            def load_res(g):
                at, used = counts(sp, g * GT * D, g)
                after(sp, "a_read", used)
                passed(sp)
                sp.dma_start(x_res[:], tokens(x_flat, at)).then_inc(s["xres_loaded"], 16)

            def load_ctx(g):
                at, used = counts(sp, g * GT * D, g)
                after(sp, "cT_ps", used)
                passed(sp)
                sp.dma_start(c_in[:], tokens(ctx_flat, at)).then_inc(s["cin_loaded"], 16)

            def load_expert(e):
                at, used = counts(sp, e * D * FF, 2 * e)
                after(sp, "wsplit_lo", used)
                passed(sp)
                sp.dma_start(w_stage[:, 0, :], W1_flat[bass.ds(at, D * FF)].rearrange("(p f) -> p f", p=P))\
                    .then_inc(s["wstage_loaded"], 16)
                sp.dma_start(w_stage[:, 1, :].rearrange("p (c d) -> p c d", c=FC),
                             W2_flat[bass.ds(at, D * FF)].rearrange("(c p d) -> p c d", c=FC, p=P))\
                    .then_inc(s["wstage_loaded"], 16)

            def spread_q(g):
                split, used = counts(sp, g + 1, 2 * TG * g)
                sp.wait_ge(s["qT_lo"], split)
                passed(sp)
                after(sp, "st_ps", used)
                for n in range(4):
                    rows = slice(32 * n, 32 * n + 32)
                    sp.dma_start(q_quad[rows, :, n, :], qT[rows]).then_inc(s["q_spread"], 16)

            load_x(0)
            for n, w in enumerate((a_wq, a_wk, a_wv, a_wo, c_wq, c_wk, c_wv, c_wo)):
                sp.dma_start(w_raw[:, n, :], w).then_inc(s["const_loaded"], 16)
            for b in range(2):
                sp.dma_start(mask_u8[b * S:(b + 1) * S, :], mask[0, 0]).then_inc(s["const_loaded"], 16)
            load_ctx(0)
            sp.dma_start(b1_raw[:], b1.rearrange("e (c p) -> (e c) p", p=P)).then_inc(s["const_loaded"], 16)
            load_res(0)
            sp.dma_start(b2_all[:, 0:NE * D], b2.rearrange("e d -> (e d)").partition_broadcast(P)).then_inc(s["const_loaded"], 16)
            sp.dma_start(b2_all[:, NE * D:], b2[0].partition_broadcast(P)).then_inc(s["const_loaded"], 16)
            load_expert(0)
            sp.wait_ge(s["consts_pool"], POOL_CONSTS)

            def body(g, nxt, prev):
                if nxt is not None:
                    load_ctx(nxt)
                    load_x(nxt)
                spread_q(g)
                if nxt is not None:
                    load_res(nxt)
                    load_expert(nxt)

            loop(sp, body)

            sp.wait_ge(s["wsplit_lo"], 2 * NE)
            for w in (w1, w2):
                for i in range(2):
                    sp.dma_start(w[:, i, NE * FF:], w[:, i, 0:FF]).then_inc(s["wrapped"], 16)

            sp.wait_ge(s["tables_ready"], 1)
            sp.wait_ge(s["scattered"], 16 * TG * NG)
            sp.wait_ge(s["pad_written"], 16 * (NE + 1))

            def load_slot(j, k):
                used, = counts(sp, j - 2)
                row = sp.value_load(slot_row[0:1, bass.ds(j, 1)], min_val=0, max_val=DUMMY)
                after(sp, "y_ready", used)
                after(sp, "xsT_ps", used)
                passed(sp)
                sp.dma_start(xs[:, k, :], sorted_rows[bass.ds(row, P), :]).then_inc(s[f"xs_loaded{k}"], 16)

            for j in range(3):
                load_slot(j, j)
            with sp.Fori(1, (SLOTS - 1) // 3) as i:
                for k in range(3):
                    load_slot(3 * i + k, k)
            for j in range((SLOTS - 1) // 3 * 3, SLOTS):
                load_slot(j, j % 3)
            for k in range(2):
                sp.wait_ge(s[f"y_written{k}"], 8 * SLOTS)

        @block.gpsimd
        def _(pool):
            done = [0]

            def const(ins):
                ins.then_inc(s["consts_pool"], 1)
                done[0] += 1
                pool.wait_ge(s["consts_pool"], done[0])

            const(pool.memset(ident[:], 0.0))
            const(pool.memset(ident_bf[:], 0.0))
            const(pool.memset(ones_bf[:], 1.0))
            const(pool.memset(before[:], 0.0))
            const(pool.memset(pick[:], 0.0))
            diag = dict(compare_op=ALU.not_equal, fill=1.0, base=0, pattern=[[-1, P]], channel_multiplier=1)
            const(pool.affine_select(out=ident[:], in_=ident[:], **diag))
            const(pool.affine_select(out=ident_bf[:], in_=ident_bf[:], **diag))
            const(pool.affine_select(out=before[:], in_=before[:], compare_op=ALU.is_ge, fill=1.0, base=0,
                                     pattern=[[-1, P]], channel_multiplier=1))
            for row in (0, 32):
                v = pick[row:row + H]
                const(pool.affine_select(out=v, in_=v, compare_op=ALU.not_equal, fill=1.0, base=0,
                                         pattern=[[-2, NHP], [-1, 2], [0, S]], channel_multiplier=1))
            v = pick[64:128]
            const(pool.affine_select(out=v, in_=v, compare_op=ALU.not_equal, fill=1.0, base=0,
                                     pattern=[[0, NHP], [0, 2], [-1, S]], channel_multiplier=1))
            const(pool.memset(in_place4[:], 1.0))
            for sign in (1, -1):
                const(pool.affine_select(out=in_place4[:], in_=in_place4[:], compare_op=ALU.is_ge, fill=0.0,
                                         base=0 if sign == 1 else DK - 1, pattern=[[-sign * DK, 4], [-sign * 32, 4]],
                                         channel_multiplier=sign))
            exact = dict(allow_small_or_imprecise_dtypes=True)
            const(pool.iota(iota_e[:], [[1, NE]], base=0, channel_multiplier=0, **exact))
            const(pool.iota(region_e[:], [[REGION, NE]], base=0, channel_multiplier=0, **exact))
            const(pool.iota(iota_slot[:], [[1, SLOTS]], base=0, channel_multiplier=0, **exact))
            const(pool.iota(iota_p[:], [[0, 1]], base=0, channel_multiplier=1, **exact))
            const(pool.iota(token_f[:], [[P, TG]], base=-GT, channel_multiplier=1, **exact))
            const(pool.memset(q_quad[:], 0.0))
            const(pool.memset(negmax[:], 0.0))
            const(pool.memset(pad_rows[:], 0.0))
            const(pool.memset(x2[:], 0.0))
            const(pool.iota(pad_rows[:, D:D + 1].bitcast(I32), [[0, 1]], base=N, channel_multiplier=0))
            const(pool.memset(a_prob[:], 0.0))
            const(pool.memset(a_diag[:], 0.0))
            assert done[0] == POOL_CONSTS, done[0]

            def split_low(e):
                for i, w in enumerate((w1, w2)):
                    pool.wait_ge(s["wsplit_hi"], 2 * e + i + 1)
                    cols = bass.ds(e * FF, FF)
                    pool.tensor_tensor(w[:, 1, cols], w_stage[:, i, :], w[:, 0, cols], ALU.subtract)\
                        .then_inc(s["wsplit_lo"], 1)

            def queries(g):
                ready, used = counts(pool, TG * (g + 1), g)
                pool.wait_ge(s["x1_ready"], ready)
                after(pool, "x1T_ps", used)
                pool.tensor_tensor(x1q[:].rearrange("p t d -> p (t d)"), x1[:, bass.ds(g * GT, GT)],
                                   bc(any_key[:, 0:1], [P, GT]), ALU.mult).then_inc(s["x1q_ready"], 1)

            def prob_low(g, t):
                n = TG * g + t
                for u in range(2):
                    pool.wait_ge(s["p_hi"], 2 * n + u + 1)
                    pool.tensor_tensor(p_hl[:, t % 2, u, 1, :], p_f[:, u, :], p_hl[:, t % 2, u, 0, :], ALU.subtract)\
                        .then_inc(s["p_lo"], 1)

            def scatter(g):
                ready, = counts(pool, g + 1)
                pool.wait_ge(s["consts_pool"], POOL_CONSTS)
                pool.wait_ge(s["pos_ready"], ready)
                for t in range(TG):
                    pool.indirect_dma_start(out=sorted_rows, out_offset=bass.IndirectOffsetOnAxis(ap=pos_i[:, t:t + 1], axis=0),
                                            in_=x2[:, t, :], in_offset=None).then_inc(s["scattered"], 16)

            def body(g, nxt, prev):
                queries(g)
                for t in range(TG):
                    prob_low(g, t)
                    if t == 1 and prev is not None:
                        scatter(prev)
                if nxt is not None:
                    split_low(nxt)

            pool.wait_ge(s["consts_dve"], 1)
            split_low(0)
            loop(pool, body)
            scatter(NG - 1)
            pool.wait_ge(s["pads_ready"], 1)
            pool.dma_start(sorted_rows[DUMMY:DUMMY + P, :], pad_rows[:]).then_inc(s["pad_written"], 16)
            for e in range(NE):
                pool.indirect_dma_start(out=sorted_rows, out_offset=bass.IndirectOffsetOnAxis(ap=pad_i[:, e:e + 1], axis=0),
                                        in_=pad_rows[:], in_offset=None).then_inc(s["pad_written"], 16)

            def low_hidden(j, u):
                pool.wait_ge(s["h_hi"], 2 * j + u + 1)
                pool.tensor_tensor(h_hl[:, u, 1, :], h_f[:, u, :], h_hl[:, u, 0, :], ALU.subtract)\
                    .then_inc(s["h_lo"], 1)

            def write_rows(j, k):
                pool.wait_ge(s["pad_written"], 16 * (NE + 1))
                pool.wait_ge(s["y_ready"], j + 1)
                pool.indirect_dma_start(out=out_rows, out_offset=bass.IndirectOffsetOnAxis(ap=y_id[:, k, :], axis=0),
                                        in_=y_out[:, k, :], in_offset=None,
                                        bounds_check=last_token, oob_is_err=False).then_inc(s[f"y_written{k}"], 16)

            last_token = pool.to_reg(N - 1)
            low_hidden(0, 0)
            low_hidden(0, 1)
            for k in range(2):
                low_hidden(k + 1, 0)
                write_rows(k, k)
                low_hidden(k + 1, 1)
            with pool.Fori(1, SLOTS // 2 - 1) as i:
                for k in range(2):
                    low_hidden(2 * i + k + 1, 0)
                    write_rows(2 * i + k, k)
                    low_hidden(2 * i + k + 1, 1)
            low_hidden(SLOTS - 1, 0)
            write_rows(SLOTS - 2, 0)
            low_hidden(SLOTS - 1, 1)
            write_rows(SLOTS - 1, 1)

        @block.tensor
        def _(pe):
            def transposes(dst, src, n, name):
                for t in range(n):
                    ins = pe.transpose(dst[:, t * P:(t + 1) * P], src[:, t, :], ident[:])
                ins.then_inc(s[name], 1)

            def product(dst, lhsT, rhs, last=True, first=True):
                for i, (a, b) in enumerate(PRODUCTS):
                    ins = pe.matmul(dst, lhsT(a), rhs(b), start=first and i == 0, stop=last and i == 2)
                return ins

            pe.wait_ge(s["const_loaded"], 16 * 13)
            pe.wait_ge(s["consts_pool"], POOL_CONSTS)
            pe.matmul(psum[0][:, 0:P], w_raw[:, 0, :], w_raw[:, 1, :], start=True, stop=True).then_inc(s["pe_setup"], 1)
            for i, n in ((1, 2), (4, 4), (5, 5), (6, 6), (7, 7)):
                pe.transpose(psum[i][:, 0:P], w_raw[:, n, :], ident[:]).then_inc(s["pe_setup"], 1)
            pe.wait_ge(s["consts_dve"], 3)
            for h in range(2):
                pe.transpose(psum[2 + h][:, 0:P], w_wo2[:, h, :], ident[:]).then_inc(s["pe_setup"], 1)
            pe.wait_ge(s["act_setup"], 1)
            pe.wait_ge(s["dve_setup"], 1)
            pe.transpose(psum[0][:, 0:S], mask_two[0:S].rearrange("p a k -> p (a k)"), ident[0:S, 0:S])
            pe.transpose(psum[0][:, 128:128 + NE * FC], b1_raw[:], ident[0:NE * FC, 0:NE * FC])\
                .then_inc(s["pe_setup"], 1)
            pe.wait_ge(s["dve_setup"], DVE_SETUP)

            def A_x(g):
                pe.wait_ge(s["xin_loaded"], 16 * (g + 1))
                after(pe, "a_read", g)
                transposes(a_bank, x_in, TG, "xT_ps")

            def A_g(g):
                pe.wait_ge(s["xT_lo"], g + 1)
                product(a_bank[:], lambda i: aqk[:, i, :], lambda i: xT[:, i, :]).then_inc(s["gT_ps"], 1)

            def A_v(g):
                pe.wait_ge(s["gT_lo"], g + 1)
                for t in range(TG):
                    cols = slice(t * P, t * P + P)
                    ins = product(a_bank[:, cols], lambda i: xT[:, i, cols], lambda i: avT[:, i, :])
                ins.then_inc(s["av_ps"], 1)

            def A_s(g):
                pe.wait_ge(s["av_lo"], g + 1)
                for t in range(TG):
                    for i, (a, b) in enumerate(PRODUCTS):
                        for q in range(2):
                            cols = slice(t * P + q * S, t * P + q * S + S)
                            ins = pe.matmul(a_bank[q * S:q * S + S, t * S:t * S + S], gT[:, a, cols], xT[:, b, cols],
                                            start=i == 0, stop=i == 2)
                ins.then_inc(s["as_ps"], 1)

            def A_p(g):
                pe.wait_ge(s["as_exp"], 2 * (g + 1))
                transposes(a_bank, a_prob[:].rearrange("p t b k -> p t (b k)"), TG, "apT_ps")

            def A_o(g):
                pe.wait_ge(s["apT_lo"], g + 1)
                for t in range(TG):
                    cols = slice(t * P, t * P + P)
                    ins = product(a_bank[:, cols], lambda i: apT[:, i, cols], lambda i: av[:, i, cols])
                ins.then_inc(s["ao_ps"], 1)

            def A_y(g):
                pe.wait_ge(s["adiag_lo"], 2 * (g + 1))
                for t in range(TG):
                    for h in range(2):
                        ins = product(a_bank[:, t * P:t * P + P],
                                      lambda i: a_diag[:, i, t, h, :, :].rearrange("p b r -> p (b r)"),
                                      lambda i: aoT[:, h, i, :], first=h == 0, last=h == 1)
                ins.then_inc(s["ay_ps"], 1)

            def K_x(g):
                pe.wait_ge(s["cin_loaded"], 16 * (g + 1))
                after(pe, "c_read", g - 1)
                transposes(b_bank, c_in, TG, "cT_ps")

            def K_k(g):
                pe.wait_ge(s["cT_lo"], g + 1)
                product(b_bank[:], lambda i: ckT[:, i, :], lambda i: cT[:, i, :]).then_inc(s["kT_ps"], 1)

            def K_v(g, u):
                if u == 0:
                    pe.wait_ge(s["kT_lo"], g + 1)
                else:
                    pe.wait_ge(s["v_lo"], 4 * g + 2)
                for b in range(BG // 2):
                    col = (u * BG // 2 + b) * S
                    for i, (m, n) in enumerate(PRODUCTS):
                        for a in range(2):
                            ins = pe.matmul(b_bank[a * S:a * S + S, b * S:b * S + S], cT[:, m, col:col + S],
                                            cvT[:, n, a * S:a * S + S], start=i == 0, stop=i == 2)
                ins.then_inc(s["v_ps"], 1)

            def B_x(g):
                pe.wait_ge(s["x1q_ready"], g + 1)
                pe.wait_ge(s["v_lo"], 4 * (g + 1))
                transposes(b_bank, x1q, TG, "x1T_ps")

            def B_q(g, prev):
                pe.wait_ge(s["x1T_lo"], g + 1)
                if prev is not None:
                    pe.wait_ge(s["oT_lo"], prev + 1)
                product(b_bank[:], lambda i: cqT[:, i, :], lambda i: x1T[:, i, :]).then_inc(s["qT_ps"], 1)

            def T_s(g, t):
                n = TG * g + t
                pe.wait_ge(s["q_spread"], 16 * 4 * (g + 1))
                pe.wait_ge(s["k_rows_ready"], 2 * g + t // 2 + 1)
                for u in range(2):
                    after(pe, "max_ready", 2 * (n - 1) + u + 1 if not isinstance(n, int) or n else 0)
                    for m in range(2):
                        for q in range(2):
                            cols = slice(t * P + q * S, t * P + q * S + S)
                            pe.matmul(s_bank[u][q * S:q * S + S, m * 4 * S:(m + 1) * 4 * S], q_quad[:, 0, 2 * u + m, cols],
                                      k_rows[:, t // 2, 0, 2 * (t % 2) + q].rearrange("p j k -> p (j k)"),
                                      start=m == 0, stop=False, skip_group_check=True)
                    pe.matmul(s_bank[u][:], ident_bf[:], bc(mask_bias[:].unsqueeze(1), [P, NHP, S]),
                              start=False, stop=True, skip_group_check=True).then_inc(s["s_ps"], 1)

            def T_m(g, t):
                n = TG * g + t
                pe.wait_ge(s["max_ready"], 2 * (n + 1))
                after(pe, "nm_lo", n)
                if t == 3:
                    after(pe, "rank_read", g)
                pe.transpose(m_bank[0:H, 0:P], c_max[:, t % 2, :], ident[:]).then_inc(s["mT_ps"], 1)

            def T_t(g, t):
                n = TG * g + t
                pe.wait_ge(s["nm_lo"], n + 1)
                for u in range(2):
                    after(pe, "exp_ready", 2 * (n - 1) + u + 1 if not isinstance(n, int) or n else 0)
                    for hp in range(NHP // 2):
                        pair = u * NHP // 2 + hp
                        pe.matmul(t_bank[u][:, hp * P:hp * P + P], pick[:, pair].rearrange("p a k -> p (a k)"),
                                  negmax[:, t % 2, :], start=hp == 0, stop=False, skip_group_check=True)
                        for q in range(2):
                            cols = slice(t * P + q * S, t * P + q * S + S)
                            for i, (a, b) in enumerate(PRODUCTS):
                                ins = pe.matmul(t_bank[u][:, hp * P + q * S:hp * P + q * S + S],
                                                k_rows[:, t // 2, a, 2 * (t % 2) + q, 2 * (pair % 2):2 * (pair % 2) + 2]
                                                .rearrange("p j k -> p (j k)"), q_quad[:, b, pair // 2, cols],
                                                start=False, stop=i == 2 and hp == NHP // 2 - 1 and q == 1,
                                                skip_group_check=True)
                    ins.then_inc(s["st_ps"], 1)

            def T_v(g, t):
                n = TG * g + t
                after(pe, "co_ready", 2 * n)
                pe.wait_ge(s["v_lo"], 4 * g + 2 * (t // 2) + 2)
                for u in range(2):
                    pe.wait_ge(s["p_lo"], 2 * n + u + 1)
                    for hp in range(NHP // 2):
                        pair = u * NHP // 2 + hp
                        ins = product(o_bank[:, pair * 4 * VW:(pair + 1) * 4 * VW],
                                      lambda i: p_hl[:, t % 2, u, i, hp * P:hp * P + P],
                                      lambda i: v_pair[:, i, 2 * t:2 * t + 2, pair].rearrange("p b a v -> p b (a v)"))
                ins.then_inc(s["pv_ps"], 1)

            def C_o(g, nxt):
                pe.wait_ge(s["co_ready"], 2 * TG * (g + 1))
                if isinstance(nxt, str):
                    pe.wait_ge(s["qT_lo"], g + 1)
                else:
                    pe.wait_ge(s["x1T_lo"], g + 2)
                transposes(b_bank, c_out, TG, "oT_ps")

            def C_y(g, nxt):
                pe.wait_ge(s["oT_lo"], g + 1)
                if not isinstance(nxt, str):
                    pe.wait_ge(s["qT_lo"], g + 2)
                for t in range(TG):
                    cols = slice(t * P, t * P + P)
                    ins = product(b_bank[:, cols], lambda i: oT[:, i, cols], lambda i: coT[:, i, :])
                ins.then_inc(s["cy_ps"], 1)

            def C_rank(g):
                pe.wait_ge(s["onehot_ready"], g + 1)
                pe.wait_ge(s["nm_lo"], TG * (g + 1) + (3 if g_in_body else 0))
                rank = m_bank[:, 0:TG * NE].rearrange("p (t e) -> p t e", t=TG)
                for t in range(TG):
                    pe.matmul(m_bank[:, 64:64 + NE], ones_bf[:], onehot_bf[:, t, :], start=t == 0, stop=t == TG - 1)
                for t in range(TG - 1):
                    pe.matmul(rank[:, t + 1:TG, :], ones_bf[:], bc(onehot_bf[:, t, :].unsqueeze(1), [P, TG - 1 - t, NE]),
                              start=False, stop=False, skip_group_check=True)
                ins = pe.matmul(rank, before[:], onehot_bf[:], start=False, stop=True, skip_group_check=True)
                ins.then_inc(s["rank_ps"], 1)

            g_in_body = True

            def body(g, nxt, prev):
                B_x(g)
                if prev is not None:
                    C_o(prev, g)
                B_q(g, prev)
                T_s(g, 0)
                if prev is not None:
                    C_y(prev, g)
                T_s(g, 1)
                T_m(g, 0)
                if nxt is not None:
                    K_x(nxt)
                T_t(g, 0)
                if nxt is not None:
                    A_x(nxt)
                T_m(g, 1)
                T_s(g, 2)
                if nxt is not None:
                    K_k(nxt)
                T_v(g, 0)
                if nxt is not None:
                    A_g(nxt)
                T_t(g, 1)
                if nxt is not None:
                    A_v(nxt)
                T_m(g, 2)
                T_s(g, 3)
                if prev is not None:
                    C_rank(prev)
                T_v(g, 1)
                if nxt is not None:
                    A_s(nxt)
                T_t(g, 2)
                if nxt is not None:
                    K_v(nxt, 0)
                T_m(g, 3)
                if nxt is not None:
                    A_p(nxt)
                T_v(g, 2)
                if nxt is not None:
                    A_o(nxt)
                T_t(g, 3)
                T_v(g, 3)
                if nxt is not None:
                    A_y(nxt)
                    K_v(nxt, 1)

            A_x(0)
            K_x(0)
            A_g(0)
            K_k(0)
            A_v(0)
            K_v(0, 0)
            A_s(0)
            K_v(0, 1)
            A_p(0)
            A_o(0)
            A_y(0)
            loop(pe, body)
            g_in_body = False
            C_o(NG - 1, "end")
            C_y(NG - 1, "end")
            C_rank(NG - 1)

            x_bank, h_bank, y_bank = psum[7], psum[0:2], psum[2:4]
            pe.wait_ge(s["tables_ready"], 1)
            pe.wait_ge(s["wrapped"], 64)

            def F_x(i, k):
                j = 6 * i + k
                after(pe, "xsT_lo", j)
                pe.wait_ge(s[f"xs_loaded{k % 3}"], 16 * (2 * i + k // 3 + 1))
                pe.transpose(x_bank[:, 0:P], xs[:, k % 3, 0:D], ident[:]).then_inc(s["xsT_ps"], 1)

            def F_h(j, k, u, w):
                if u == 0:
                    pe.wait_ge(s["xsT_lo"], j + 1)
                after(pe, "h_relu", 2 * j + u - 1 if not isinstance(j, int) or j else 0)
                for c in range(FC):
                    ins = product(h_bank[u][:, c * P:c * P + P],
                                  lambda i: w1[:, i, bass.ds(w + (u * FC + c) * P, P)], lambda i: xsT[:, k, i, :])
                ins.then_inc(s["h_ps"], 1)

            def F_y(j, k, u, w):
                pe.wait_ge(s["h_lo"], 2 * j + u + 1)
                if u == 0:
                    after(pe, "y_read", j - 1)
                for c in range(FC):
                    ins = product(y_bank[k][:, 0:D], lambda i: h_hl[:, u, i, c * P:c * P + P],
                                  lambda i: w2[:, i, bass.ds(w + (u * FC + c) * P, P)],
                                  first=u == 0 and c == 0, last=u == 1 and c == FC - 1)
                if u == 1:
                    ins.then_inc(s["y_ps"], 1)

            def weights(j):
                return pe.value_load(slot_w[0:1, bass.ds(j, 1)], min_val=0, max_val=(NE - 1) * FF)

            def F_step(i, k):
                j = 6 * i + k
                w, w_next = weights(j), weights(j + 1)
                F_x(i, k + 1)
                F_y(j, k % 2, 0, w)
                F_h(j + 1, (k + 1) % 2, 0, w_next)
                F_y(j, k % 2, 1, w)
                F_h(j + 1, (k + 1) % 2, 1, w_next)

            F_x(0, 0)
            w = weights(0)
            F_h(0, 0, 0, w)
            F_h(0, 0, 1, w)
            for k in range(6):
                F_step(0, k)
            with pe.Fori(1, ROUNDS) as i:
                for k in range(6):
                    F_step(i, k)
            for k in range(SLOTS - 1 - 6 * ROUNDS):
                F_step(ROUNDS, k)
            w = weights(SLOTS - 1)
            F_y(SLOTS - 1, (SLOTS - 1) % 2, 0, w)
            F_y(SLOTS - 1, (SLOTS - 1) % 2, 1, w)

        @block.scalar
        def _(act):
            def high(dst, src, name, **kw):
                act.activation(dst, src, ACT.Copy, **kw).then_inc(s[name], 1)

            for i, dst in SETUP_SPLITS:
                act.wait_ge(s["pe_setup"], SETUP_ORDER.index(i) + 1)
                high(by_parity(dst[:, 0, :]) if i == 6 else dst[:, 0, :],
                     even_odd(psum[i][:, 0:P]) if i == 6 else psum[i][:, 0:P], "act_setup")
            act.wait_ge(s["pe_setup"], SETUP_PS)
            for k in range(2):
                for q in range(2):
                    high(negmax[64:128, k, q * S:q * S + S], psum[0][64:128, 0:S], "act_setup")
            high(b1c[:, 0:NE * FC], psum[0][:, 128:128 + NE * FC], "act_setup")
            high(b1c[:, NE * FC:], psum[0][:, 128:128 + FC], "act_setup")

            def split_high(e):
                act.wait_ge(s["wstage_loaded"], 32 * (e + 1))
                for i, w in enumerate((w1, w2)):
                    high(w[:, 0, bass.ds(e * FF, FF)], w_stage[:, i, :], "wsplit_hi")

            def plain(name, dst, bank):
                def step(g):
                    act.wait_ge(s[name + "_ps"], g + 1)
                    high(dst[:, 0, :], bank[:], name + "_hi")
                return step

            A_x, A_g, A_v = plain("xT", xT, a_bank), plain("gT", gT, a_bank), plain("av", av, a_bank)
            A_p, K_x = plain("apT", apT, a_bank), plain("cT", cT, b_bank)
            B_x, C_o = plain("x1T", x1T, b_bank), plain("oT", oT, b_bank)

            def A_s(g):
                act.wait_ge(s["as_shifted"], g + 1)
                after(act, "apT_ps", g)
                for b in range(2):
                    rows = slice(b * S, b * S + S)
                    act.activation(a_prob[rows, :, b, :], a_shift[rows], ACT.Exp, scale=A_SCALE).then_inc(s["as_exp"], 1)

            def A_o(g):
                act.wait_ge(s["ao_scaled"], g + 1)
                for b in range(2):
                    rows = slice(b * S, b * S + S)
                    for h in range(2):
                        src = a_out[rows].rearrange("p t (r h) -> p t h r", h=2)[:, :, h, :]
                        ins = act.activation(a_diag[rows, 0, :, h, b, :], src, ACT.Copy)
                    ins.then_inc(s["adiag_hi"], 1)

            def K_k(g):
                act.wait_ge(s["kT_ps"], g + 1)
                after(act, "k_rows_ready", 2 * g)
                high(kT[:, :, 0, :], b_bank[:].rearrange("p (u k) -> p u k", u=2), "kT_hi")

            def K_v(g, u):
                act.wait_ge(s["v_ps"], 2 * g + u + 1)
                after(act, "pv_ps", TG * (g - 1) + 2 * u + 2 if not isinstance(g, int) or g else 0)
                for a in range(2):
                    rows = slice(a * S, a * S + S)
                    src = b_bank[rows, 0:GT // 2].rearrange("p (b n v) -> p b n v", b=BG // 2, v=DK)
                    high(v_pair[rows, 0, u * BG // 2:(u + 1) * BG // 2, :, a, 0:DK], src, "v_hi")

            def B_q(g):
                act.wait_ge(s["qT_ps"], g + 1)
                high(qT[:, 0, :], b_bank[:], "qT_hi", scale=C_SCALE)

            def T_m(g, t):
                act.wait_ge(s["mT_ps"], TG * g + t + 1)
                high(negmax[0:H, t % 2, :], m_bank[0:H, 0:P], "nm_hi", scale=-1.0)

            def T_t(g, t):
                n = TG * g + t
                for u in range(2):
                    act.wait_ge(s["st_ps"], 2 * n + u + 1)
                    after(act, "p_lo", 2 * (n - 1) + u + 1 if not isinstance(n, int) or n else 0)
                    act.activation(p_f[:, u, :], t_bank[u][:], ACT.Exp).then_inc(s["exp_ready"], 1)
                    act.wait_ge(s["exp_ready"], 2 * n + u + 1)
                    after(act, "pv_ps", n - 1)
                    high(p_hl[:, t % 2, u, 0, :], p_f[:, u, :], "p_hi")

            def body(g, nxt, prev):
                B_x(g)
                if prev is not None:
                    C_o(prev)
                B_q(g)
                T_m(g, 0)
                if nxt is not None:
                    K_x(nxt)
                T_t(g, 0)
                if nxt is not None:
                    A_x(nxt)
                T_m(g, 1)
                if nxt is not None:
                    K_k(nxt)
                    A_g(nxt)
                T_t(g, 1)
                if nxt is not None:
                    A_v(nxt)
                T_m(g, 2)
                if nxt is not None:
                    A_s(nxt)
                T_t(g, 2)
                if nxt is not None:
                    K_v(nxt, 0)
                T_m(g, 3)
                if nxt is not None:
                    A_p(nxt)
                    A_o(nxt)
                T_t(g, 3)
                if nxt is not None:
                    K_v(nxt, 1)
                    split_high(nxt)

            A_x(0)
            K_x(0)
            A_g(0)
            K_k(0)
            A_v(0)
            K_v(0, 0)
            A_s(0)
            K_v(0, 1)
            A_p(0)
            A_o(0)
            split_high(0)
            loop(act, body)
            C_o(NG - 1)

            x_bank, h_bank = psum[7], psum[0:2]
            act.wait_ge(s["tables_ready"], 1)

            def F_x(j, k):
                act.wait_ge(s["xsT_ps"], j + 1)
                after(act, "h_ps", 2 * (j - 1))
                high(xsT[:, k, 0, :], x_bank[:, 0:P], "xsT_hi")

            def F_h(j, u, e):
                act.wait_ge(s["h_ps"], 2 * j + u + 1)
                after(act, "h_lo", 2 * j + u - 1 if not isinstance(j, int) or j else 0)
                for c in range(FC):
                    ins = act.activation(h_f[:, u, c * P:c * P + P], h_bank[u][:, c * P:c * P + P], ACT.Relu,
                                         bias=b1c[:, bass.ds(e + u * FC + c, 1)])
                ins.then_inc(s["h_relu"], 1)

            def F_sd(j, k):
                act.wait_ge(s["y_var"], j + 1)
                act.activation(f_sd[:, k, 0:1], f_mv[:, k, 1:2], ACT.Sqrt, bias=eps_t[:, 0:1]).then_inc(s["y_sd"], 1)

            def bias_of(j):
                return act.value_load(slot_b1[0:1, bass.ds(j, 1)], min_val=0, max_val=(NE - 1) * FC)

            def F_step(j, k):
                e = bias_of(j + 1)
                F_x(j + 1, 1 - k)
                F_h(j + 1, 0, e)
                F_h(j + 1, 1, e)
                F_sd(j, k)

            F_x(0, 0)
            e = bias_of(0)
            F_h(0, 0, e)
            F_h(0, 1, e)
            for j in range(2):
                F_step(j, j % 2)
            with act.Fori(1, SLOTS // 2 - 1) as i:
                for k in range(2):
                    F_step(2 * i + k, k)
            F_step(SLOTS - 2, 0)
            F_sd(SLOTS - 1, 1)

        @block.vector
        def _(dve):
            chain = Steps(dve, "dve_step")
            chain.per_body = DVE_BODY
            link = chain.link

            dve.memset(eps_t[:], EPS)
            dve.wait_ge(s["const_loaded"], 16 * 13)
            link(dve.tensor_copy(mask_f[:], mask_u8[:]))
            dve.tensor_reduce(any_key[:], mask_f[:], AX.X, ALU.max).then_inc(s["consts_dve"], 1)
            link(dve.tensor_scalar(mask_two[:], bc(mask_f[:].unsqueeze(1), [P, 2, S]), 1.0, 1e9, ALU.subtract, ALU.mult))
            dve.tensor_copy(mask_bias[:], mask_two[:, 0, :]).then_inc(s["consts_dve"], 1)
            dve.tensor_copy(w_wo2[:].rearrange("p h (a q) -> p h a q", a=2),
                            bc(w_raw[:, 3, :].rearrange("p (h q) -> p h q", h=2).unsqueeze(2), [P, 2, 2, S]))\
                .then_inc(s["consts_dve"], 1)
            dve.wait_ge(s["consts_pool"], POOL_CONSTS)
            link(dve.tensor_reduce(in_place[:], in_place4[:], AX.X, ALU.add))
            link(dve.memset(v_pair[:], 0.0))
            for a in range(2):
                link(dve.memset(v_pair[a * S:a * S + S, 0, :, :, a, DK:VW], 1.0))
            link(dve.tensor_copy(base[:], region_e[:]))
            link(dve.tensor_tensor(b2_pair[:], b2_all[:, 0:NE * D], b2_all[:, D:], ALU.add))
            link(dve.tensor_scalar(b2_pair[:], b2_pair[:], 0.5, None, ALU.mult))
            for n, (i, dst) in enumerate(SETUP_SPLITS):
                dve.wait_ge(s["act_setup"], n + 1)
                if i == 6:
                    ins = dve.tensor_tensor(by_parity(dst[:, 1, :]), even_odd(psum[i][:, 0:P]), by_parity(dst[:, 0, :]),
                                            ALU.subtract)
                else:
                    ins = dve.tensor_tensor(dst[:, 1, :], psum[i][:, 0:P], dst[:, 0, :], ALU.subtract)
                ins.then_inc(s["dve_setup"], 1)
            dve.wait_ge(s["act_setup"], len(SETUP_SPLITS) + 6)
            dve.memset(a_max[:], 0.0).then_inc(s["dve_setup"], 1)

            def low(dst, src, hi, hi_name, count, name):
                dve.wait_ge(s[hi_name], count)
                dve.tensor_tensor(dst, src, hi, ALU.subtract).then_inc(s[name], 1)

            def k_low(g):
                low(kT[:, :, 1, :], b_bank[:].rearrange("p (u k) -> p u k", u=2), kT[:, :, 0, :], "kT_hi", g + 1, "kT_lo")

            def plain(name, dst, bank):
                return lambda g: low(dst[:, 1, :], bank[:], dst[:, 0, :], name + "_hi", g + 1, name + "_lo")

            A_x, A_g, A_v = plain("xT", xT, a_bank), plain("gT", gT, a_bank), plain("av", av, a_bank)
            A_p, K_x, K_k = plain("apT", apT, a_bank), plain("cT", cT, b_bank), k_low
            B_x, C_o = plain("x1T", x1T, b_bank), plain("oT", oT, b_bank)

            def normalise(r, dst, name):
                for t in range(TG):
                    ins = dve.bn_stats(st[:, t, :], r[:, t, :])
                link(ins)
                total, diff, m2, v, mean, y, w, half = (ln[:, i, :] for i in range(8))
                dve.tensor_tensor(total, st[:, :, 1], st[:, :, 4], ALU.add)
                dve.tensor_tensor(m2, st[:, :, 2], st[:, :, 5], ALU.add)
                link(dve.tensor_tensor(diff, st[:, :, 1], st[:, :, 4], ALU.subtract))
                link(dve.tensor_tensor(diff, diff, diff, ALU.mult))
                link(dve.scalar_tensor_tensor(out=m2, in0=diff, scalar=D / 4.0, in1=m2, op0=ALU.mult, op1=ALU.add))
                dve.tensor_scalar(mean, total, 0.5, None, ALU.mult)
                link(dve.tensor_scalar(v, m2, 1.0 / D, EPS, ALU.mult, ALU.add))
                dve.tensor_scalar(half, v, -0.5, None, ALU.mult)
                link(dve.tensor_scalar(ln_i[:, 0, :], v.bitcast(I32), 1, None, ALU.arith_shift_right))
                link(dve.tensor_scalar(ln_i[:, 1, :], ln_i[:, 0, :], -1.0, 1597463007.0, ALU.mult, ALU.add))
                guess = ln_i[:, 1, :].bitcast(F32)
                for k in range(3):
                    y_in = guess if k == 0 else y
                    link(dve.tensor_tensor(w, y_in, y_in, ALU.mult))
                    link(dve.tensor_tensor(w, w, half, ALU.mult))
                    link(dve.scalar_tensor_tensor(out=y, in0=w, scalar=1.5, in1=y_in, op0=ALU.add, op1=ALU.mult))
                for t in range(TG):
                    dve.tensor_scalar(dst(t), r[:, t, :], mean[:, t:t + 1], y[:, t:t + 1], ALU.subtract, ALU.mult)\
                        .then_inc(s[name], 1)

            def A_s(g):
                dve.wait_ge(s["as_ps"], g + 1)
                scores = a_bank[:, 0:TG * S].rearrange("p (t k) -> p t k", t=TG)
                link(dve.tensor_reduce(a_max[:], scores, AX.X, ALU.max))
                dve.tensor_tensor(a_shift[:], scores, bc(a_max[:].unsqueeze(2), [P, TG, S]), ALU.subtract)\
                    .then_inc(s["as_shifted"], 1)

            def A_sum(g):
                dve.wait_ge(s["as_exp"], 2 * (g + 1))
                link(dve.tensor_reduce(a_sum[:], a_prob[:].rearrange("p t b k -> p t (b k)"), AX.X, ALU.add))
                link(dve.reciprocal(a_rinv[:], a_sum[:]))

            def A_o(g):
                dve.wait_ge(s["ao_ps"], g + 1)
                dve.tensor_tensor(a_out[:], a_bank[:].rearrange("p (t d) -> p t d", t=TG),
                                  bc(a_rinv[:].unsqueeze(2), [P, TG, D]), ALU.mult).then_inc(s["ao_scaled"], 1)
                for b in range(2):
                    rows = slice(b * S, b * S + S)
                    dve.wait_ge(s["adiag_hi"], 2 * g + b + 1)
                    for h in range(2):
                        src = a_out[rows].rearrange("p t (r h) -> p t h r", h=2)[:, :, h, :]
                        ins = dve.tensor_tensor(a_diag[rows, 1, :, h, b, :], src, a_diag[rows, 0, :, h, b, :], ALU.subtract)
                    ins.then_inc(s["adiag_lo"], 1)

            def A_y(g):
                dve.wait_ge(s["ay_ps"], g + 1)
                dve.wait_ge(s["xres_loaded"], 16 * (g + 1))
                dve.tensor_tensor(a_r[:], a_bank[:].rearrange("p (t d) -> p t d", t=TG), x_res[:], ALU.add)\
                    .then_inc(s["a_read"], 1)
                dve.wait_ge(s["a_read"], g + 1)
                normalise(a_r, lambda t: x1[:, bass.ds(g * GT + t * D, D)], "x1_ready")

            def K_rows(g, u):
                dve.wait_ge(s["kT_lo"], g + 1)
                after(dve, "st_ps", 2 * TG * (g - 1) + 4 * u + 4 if not isinstance(g, int) or g else 0)
                for j in range(4):
                    ins = dve.tensor_scalar(k_rows[:, u, :, :, j, :].rearrange("p i b k -> p (i b) k"),
                                            kT[:, u].rearrange("p i (b k) -> p (i b) k", k=S),
                                            in_place[:, j:j + 1], None, ALU.mult)
                ins.then_inc(s["k_rows_ready"], 1)

            def K_v(g, u):
                for a in range(2):
                    rows = slice(a * S, a * S + S)
                    src = b_bank[rows, 0:GT // 2].rearrange("p (b n v) -> p b n v", b=BG // 2, v=DK)
                    seq = slice(u * BG // 2, (u + 1) * BG // 2)
                    low(v_pair[rows, 1, seq, :, a, 0:DK], src, v_pair[rows, 0, seq, :, a, 0:DK],
                        "v_hi", 4 * g + 2 * u + a + 1, "v_lo")

            def B_q(g):
                dve.wait_ge(s["qT_hi"], g + 1)
                dve.scalar_tensor_tensor(out=qT[:, 1, :], in0=b_bank[:], scalar=C_SCALE, in1=qT[:, 0, :],
                                         op0=ALU.mult, op1=ALU.subtract).then_inc(s["qT_lo"], 1)

            def T_s(g, t):
                n = TG * g + t
                after(dve, "mT_ps", n - 1)
                for u in range(2):
                    dve.wait_ge(s["s_ps"], 2 * n + u + 1)
                    dve.tensor_reduce(c_max[:, t % 2, u * NHP:(u + 1) * NHP],
                                      s_bank[u][:].rearrange("p (h k) -> p h k", h=NHP), AX.X, ALU.max)\
                        .then_inc(s["max_ready"], 1)

            def T_m(g, t):
                n = TG * g + t
                dve.wait_ge(s["nm_hi"], n + 1)
                dve.scalar_tensor_tensor(out=negmax[32:32 + H, t % 2, :], in0=m_bank[0:H, 0:P], scalar=-1.0,
                                         in1=negmax[0:H, t % 2, :], op0=ALU.mult, op1=ALU.subtract).then_inc(s["nm_lo"], 1)

            def T_v(g, t):
                n = TG * g + t
                dve.wait_ge(s["pv_ps"], n + 1)
                if t == 0:
                    after(dve, "oT_ps", g)
                for b in range(2):
                    rows = slice(b * S, b * S + S)
                    o = o_bank[rows, 0:NHP * 4 * VW].rearrange("p (n b a v) -> p n b a v", b=2, a=2, v=VW)[:, :, b]
                    dve.reciprocal(c_rinv[rows].rearrange("p (n a) -> p n a", a=2), o[:, :, :, DK])\
                        .then_inc(s["dve_step"], 1)
                    chain.n += 1
                dve.wait_ge(s["dve_step"], chain.start + chain.n)
                for b in range(2):
                    rows = slice(b * S, b * S + S)
                    o = o_bank[rows, 0:NHP * 4 * VW].rearrange("p (n b a v) -> p n b a v", b=2, a=2, v=VW)[:, :, b]
                    dve.tensor_tensor(c_out[rows, t, :].rearrange("p (n a v) -> p n a v", a=2, v=DK), o[:, :, :, 0:DK],
                                      bc(c_rinv[rows].rearrange("p (n a) -> p n a", a=2).unsqueeze(3), [S, NHP, 2, DK]),
                                      ALU.mult).then_inc(s["co_ready"], 1)

            def C_y(g):
                dve.wait_ge(s["cy_ps"], g + 1)
                dve.tensor_tensor(c_r[:].rearrange("p t d -> p (t d)"), b_bank[:], x1[:, bass.ds(g * GT, GT)], ALU.add)\
                    .then_inc(s["c_read"], 1)
                dve.wait_ge(s["c_read"], g + 1)
                after(dve, "scattered", 16 * TG * g)
                normalise(c_r, lambda t: x2[:, t, 0:D], "x2_ready")
                link(dve.tensor_scalar(token_f[:], token_f[:], float(GT), None, ALU.add))
                dve.tensor_copy(x2[:, :, D].bitcast(I32), token_f[:]).then_inc(s["x2_ready"], 1)

            def C_route(g):
                dve.wait_ge(s["x2_ready"], (TG + 1) * (g + 1))
                v, mag, near, over, sign, trunc, m8, h = (rt[:, i, :] for i in range(8))
                link(dve.tensor_tensor(v, x2[:, :, 0], x2[:, :, 1], ALU.add))
                link(dve.tensor_scalar(sign, v, 0.0, 2.0, ALU.is_ge, ALU.mult))
                link(dve.scalar_tensor_tensor(out=mag, in0=sign, scalar=-1.0, in1=v, op0=ALU.add, op1=ALU.mult))
                link(dve.tensor_scalar(near, mag, ROUND, ROUND, ALU.add, ALU.subtract))
                link(dve.tensor_tensor(over, near, mag, ALU.is_gt))
                link(dve.tensor_tensor(near, near, over, ALU.subtract))
                link(dve.scalar_tensor_tensor(out=trunc, in0=sign, scalar=-1.0, in1=near, op0=ALU.add, op1=ALU.mult))
                link(dve.tensor_scalar(m8, trunc, 1.0 / NE, -0.4375, ALU.mult, ALU.add))
                link(dve.tensor_scalar(m8, m8, ROUND, ROUND, ALU.add, ALU.subtract))
                link(dve.scalar_tensor_tensor(out=h, in0=m8, scalar=-float(NE), in1=trunc, op0=ALU.mult, op1=ALU.add))
                link(dve.tensor_tensor(onehot[:], bc(iota_e[:].unsqueeze(1), [P, TG, NE]), bc(h.unsqueeze(2), [P, TG, NE]),
                                       ALU.is_equal))
                dve.tensor_copy(onehot_bf[:], onehot[:]).then_inc(s["onehot_ready"], 1)

            def C_rank(g):
                dve.wait_ge(s["rank_ps"], g + 1)
                after(dve, "scattered", 16 * TG * g)
                rank = m_bank[:, 0:TG * NE].rearrange("p (t e) -> p t e", t=TG)
                link(dve.tensor_tensor(place[:], rank, bc(base[:].unsqueeze(1), [P, TG, NE]), ALU.add))
                link(dve.tensor_tensor(place[:], place[:], onehot[:], ALU.mult))
                dve.tensor_tensor(base[:], m_bank[:, 64:64 + NE], base[:], ALU.add).then_inc(s["rank_read"], 1)
                link(dve.tensor_reduce(pos_f[:], place[:], AX.X, ALU.add))
                dve.tensor_copy(pos_i[:], pos_f[:]).then_inc(s["pos_ready"], 1)

            def body(g, nxt, prev):
                B_x(g)
                if prev is not None:
                    C_o(prev)
                B_q(g)
                T_s(g, 0)
                if prev is not None:
                    C_y(prev)
                T_s(g, 1)
                T_m(g, 0)
                if nxt is not None:
                    K_x(nxt)
                    A_x(nxt)
                T_m(g, 1)
                if prev is not None:
                    C_route(prev)
                T_s(g, 2)
                if nxt is not None:
                    K_k(nxt)
                T_v(g, 0)
                if nxt is not None:
                    A_g(nxt)
                    A_v(nxt)
                T_m(g, 2)
                T_s(g, 3)
                if prev is not None:
                    C_rank(prev)
                T_v(g, 1)
                if nxt is not None:
                    A_s(nxt)
                    K_rows(nxt, 0)
                    K_v(nxt, 0)
                T_m(g, 3)
                if nxt is not None:
                    A_sum(nxt)
                    A_p(nxt)
                T_v(g, 2)
                if nxt is not None:
                    A_o(nxt)
                T_v(g, 3)
                if nxt is not None:
                    K_rows(nxt, 1)
                    A_y(nxt)
                    K_v(nxt, 1)

            A_x(0)
            K_x(0)
            A_g(0)
            K_k(0)
            K_rows(0, 0)
            K_rows(0, 1)
            A_v(0)
            K_v(0, 0)
            A_s(0)
            K_v(0, 1)
            A_sum(0)
            A_p(0)
            A_o(0)
            A_y(0)
            loop(dve, body, chain)
            C_o(NG - 1)
            C_y(NG - 1)
            C_route(NG - 1)
            C_rank(NG - 1)

            dve.wait_ge(s["rank_read"], NG)
            link(dve.tensor_scalar(pad_f[:], base[:], iota_p[:, 0:1], None, ALU.add))
            dve.tensor_copy(pad_i[:], pad_f[:]).then_inc(s["pads_ready"], 1)
            link(dve.tensor_tensor(count[:], base[:], region_e[:], ALU.subtract))
            link(dve.tensor_scalar(tiles_e[:, 0, :], count[:], 1.0 / P, (P - 1.0) / P - 0.49609375, ALU.mult, ALU.add))
            link(dve.tensor_scalar(tiles_e[:, 1, :], tiles_e[:, 0, :], ROUND, ROUND, ALU.add, ALU.subtract))
            a = 1
            for step in (1, 2, 4):
                b = 2 if a != 2 else 3
                link(dve.tensor_copy(tiles_e[:, b, 0:step], tiles_e[:, a, 0:step]))
                link(dve.tensor_tensor(tiles_e[:, b, step:NE], tiles_e[:, a, step:NE], tiles_e[:, a, 0:NE - step], ALU.add))
                a = b
            upto = bc(tiles_e[:, a, :].unsqueeze(1), [P, SLOTS, NE])
            link(dve.tensor_tensor(done_e[:, 0], upto, bc(iota_slot[:].unsqueeze(2), [P, SLOTS, NE]), ALU.is_le))
            link(dve.tensor_tensor(done_e[:, 1], done_e[:, 0], upto, ALU.mult))
            expert, first, row, wrow, t4, t5 = (slot_f[:, i, :] for i in range(6))
            dve.tensor_reduce(expert, done_e[:, 0], AX.X, ALU.add)
            link(dve.tensor_reduce(first, done_e[:, 1], AX.X, ALU.max))
            link(dve.tensor_tensor(row, iota_slot[:], first, ALU.subtract))
            link(dve.tensor_scalar(row, row, float(P), None, ALU.mult))
            link(dve.scalar_tensor_tensor(out=row, in0=expert, scalar=float(REGION), in1=row, op0=ALU.mult, op1=ALU.add))
            link(dve.tensor_scalar(row, row, float(DUMMY), None, ALU.min))
            link(dve.tensor_scalar(wrow, expert, NE - 1.0, None, ALU.min))
            dve.tensor_copy(slot_row[:], row)
            dve.tensor_scalar(slot_w[:], wrow, float(FF), None, ALU.mult)
            dve.tensor_scalar(slot_b1[:], wrow, float(FC), None, ALU.mult)
            dve.tensor_scalar(slot_b2[:], wrow, float(D), None, ALU.mult).then_inc(s["tables_ready"], 1)
            dve.wait_ge(s["tables_ready"], 1)

            x_bank, y_bank = psum[7], psum[2:4]
            def F_x(j, k):
                dve.wait_ge(s["xsT_hi"], j + 1)
                dve.tensor_tensor(xsT[:, k, 1, :], x_bank[:, 0:P], xsT[:, k, 0, :], ALU.subtract).then_inc(s["xsT_lo"], 1)

            def F_h(j, u):
                dve.wait_ge(s["h_relu"], 2 * j + u + 1)
                dve.tensor_copy(h_hl[:, u, 0, :], h_f[:, u, :]).then_inc(s["h_hi"], 1)

            def F_out(i, k):
                j = 6 * i + k
                e = dve.value_load(slot_b2[0:1, bass.ds(j, 1)], min_val=0, max_val=(NE - 1) * D)
                dve.wait_ge(s["y_ps"], j + 1)
                dve.wait_ge(s[f"xs_loaded{k % 3}"], 16 * (2 * i + k // 3 + 1))
                dve.scalar_tensor_tensor(out=y_r[:, k % 2, :], in0=y_bank[k % 2][:, 0:D], scalar=0.5, in1=xs[:, k % 3, 0:D],
                                         op0=ALU.mult, op1=ALU.add).then_inc(s["y_read"], 1)
                after(dve, f"y_written{k % 2}", 16 * (3 * i + k // 2))
                dve.wait_ge(s["y_read"], j + 1)
                y_chain.link(dve.tensor_tensor(y_t[:, k % 2, :], y_r[:, k % 2, :], b2_pair[:, bass.ds(e, D)], ALU.add))
                y_chain.link(dve.bn_stats(f_st[:, k % 2, :], y_t[:, k % 2, :]))
                dve.tensor_copy(y_id[:, k % 2, :], xs[:, k % 3, D:D + 1].bitcast(I32))
                dve.bn_aggr(f_mv[:, k % 2, :], f_st[:, k % 2, :]).then_inc(s["y_var"], 1)

            def F_norm(i, k):
                j = 6 * i + k
                dve.wait_ge(s["y_sd"], j + 1)
                y_chain.link(dve.reciprocal(f_sd[:, k % 2, 1:2], f_sd[:, k % 2, 0:1]))
                dve.tensor_scalar(y_out[:, k % 2, :], y_t[:, k % 2, :], f_mv[:, k % 2, 0:1], f_sd[:, k % 2, 1:2],
                                  ALU.subtract, ALU.mult).then_inc(s["y_ready"], 1)

            y_chain = Steps(dve, "y_step")

            def F_step(i, k):
                j = 6 * i + k
                F_x(j + 1, (k + 1) % 2)
                F_h(j + 1, 0)
                F_h(j + 1, 1)
                F_out(i, k)
                F_norm(i, k)

            F_x(0, 0)
            F_h(0, 0)
            F_h(0, 1)
            for k in range(6):
                F_step(0, k)
            per_round = y_chain.n
            with dve.Fori(1, ROUNDS) as i:
                y_chain.start, y_chain.n = i * per_round, 0
                for k in range(6):
                    F_step(i, k)
            y_chain.start, y_chain.n = ROUNDS * per_round, 0
            for k in range(SLOTS - 1 - 6 * ROUNDS):
                F_step(ROUNDS, k)
            F_out(ROUNDS, SLOTS - 1 - 6 * ROUNDS)
            F_norm(ROUNDS, SLOTS - 1 - 6 * ROUNDS)


_INS = ["x", "ctx_1024", "mask_1x1xSxS2_bf1", "L0_attn_wq", "L0_attn_wk", "L0_attn_wv", "L0_attn_wo",
        "L0_xattn_w_q", "L0_xattn_w_k", "L0_xattn_w_v", "L0_xattn_w_o",
        "L0_ffn_W1", "L0_ffn_b1", "L0_ffn_W2", "L0_ffn_b2"]


def kernel(**inputs):
    import concourse.bacc as _bacc
    from concourse.bass_utils import run_bass_kernel_spmd as _run

    nc = _bacc.Bacc("TRN2", target_bir_lowering=False, num_devices=1)
    arrays, args = {}, []
    for name in _INS:
        a = np.ascontiguousarray(inputs[name])
        if a.dtype == np.bool_:
            a = a.view(np.uint8)
        arrays[f"in_{name}"] = a
        args.append(nc.dram_tensor(f"in_{name}", a.shape, mybir.dt.from_np(a.dtype), kind="ExternalInput").ap())
    args.append(nc.dram_tensor("out_dram", arrays["in_x"].shape, F32, kind="ExternalOutput").ap())
    decoder_layer_kernel(nc, *args)
    r = _run(nc, [arrays], core_ids=[0])
    return r.results[0]["out_dram"]
```

```python
from contextlib import ExitStack

import numpy as np
import concourse.bass as bass
from concourse import mybir

F32 = mybir.dt.float32
F16 = mybir.dt.float16
BF16 = mybir.dt.bfloat16
I32 = mybir.dt.int32
U8 = mybir.dt.uint8
ALU = mybir.AluOpType
ACT = mybir.ActivationFunctionType
AX = mybir.AxisListType

P = 128
EPS = 1e-5
ROUND = 12582912.0
PRODUCTS = ((0, 0), (1, 0), (0, 1))


def decoder_layer_kernel(nc, x, ctx, mask, a_wq, a_wk, a_wv, a_wo, c_wq, c_wk, c_wv, c_wo, W1, b1, W2, b2, out):
    B, S, D = x.shape
    H, DK = 16, D // 16
    NE, _, FF = W1.shape
    FC = FF // P
    TG = 4
    BG = TG * P // S
    NG = B * S // (TG * P)
    GT = TG * P
    VW = DK + 1
    NHP = H // 2
    A_SCALE = 1.0 / float(np.sqrt(D // 16))
    C_SCALE = 1.0 / float(np.sqrt(DK))
    N = B * S
    REGION = N + P
    DUMMY = NE * REGION
    ROW = D + 4
    SLOTS = N // P + NE - 1
    UNROLL = 6
    XB, YB = UNROLL, 3
    assert D == P and S == 64 and TG * P == 512 and NG == NE and SLOTS % YB == 0

    sorted_rows = nc.dram_tensor("sorted_rows", (DUMMY + P, ROW), F32).ap()
    sorted_flat = sorted_rows.rearrange("r c -> (r c)")

    x_flat = x.rearrange("b s d -> (b s d)")
    ctx_flat = ctx.rearrange("b s d -> (b s d)")
    W1_flat = W1.rearrange("e d f -> (e d f)")
    W2_flat = W2.rearrange("e f d -> (e f d)")
    out_rows = out.rearrange("b s d -> (b s) d")

    with ExitStack() as stack:
        def sb(name, shape, dt=F32):
            return stack.enter_context(nc.sbuf_tensor(name, shape, dt))

        def sem(name):
            return stack.enter_context(nc.semaphore(name))

        ident = sb("ident", [P, P])
        ident_bf = sb("ident_bf", [P, P], BF16)
        ones_bf = sb("ones_bf", [P, P], BF16)
        before = sb("before", [P, P], BF16)
        iota_e = sb("iota_e", [P, NE])
        iota_slot = sb("iota_slot", [P, SLOTS])
        region_e = sb("region_e", [P, NE])
        pad_rows = sb("pad_rows", [P, ROW])
        mask_u8 = sb("mask_u8", [P, S], U8)
        mask_f = sb("mask_f", [P, S])
        mask_two = sb("mask_two", [P, 2, S])
        mask_bias = sb("mask_bias", [P, S], BF16)
        any_key = sb("any_key", [P, 1])
        pick = sb("pick", [P, NHP, 2, S], BF16)
        negmax = sb("negmax", [P, 2, P], BF16)

        w_raw = sb("w_raw", [P, 8, P])
        aqk = sb("aqk", [P, 2, P], F16)
        avT = sb("avT", [P, 2, P], F16)
        aoT = sb("aoT", [P, 2, 2, P], F16)
        cqT = sb("cqT", [P, 2, P], F16)
        ckT = sb("ckT", [P, 2, P], F16)
        cvT = sb("cvT", [P, 2, P], F16)
        coT = sb("coT", [P, 2, P], F16)
        w_wo2 = sb("w_wo2", [P, 2, P])
        w_stage = sb("w_stage", [P, 2, FF])
        w1 = sb("w1", [P, 2, (NE + 1) * FF], F16)
        w2 = sb("w2", [P, (NE + 1) * FC * 2 * P], F16)
        b1_stage = sb("b1_stage", [FC, (NE + 1) * P])
        b1_rows = sb("b1_rows", [P, (NE + 1) * P], F16)
        b1_ones = sb("b1_ones", [P, FC, P], F16)
        b2_stage = sb("b2_stage", [P, NE * D])
        b2_rows = sb("b2_rows", [P, NE * D], F16)
        ones_h = sb("ones_h", [P, P], F16)

        x_in = sb("x_in", [P, TG, D])
        x_res = sb("x_res", [P, TG, D])
        xT = sb("xT", [P, 2, GT], F16)
        gT = sb("gT", [P, 2, GT], F16)
        av = sb("av", [P, 2, GT], F16)
        a_max = sb("a_max", [P, TG])
        a_shift = sb("a_shift", [P, TG, S])
        a_prob = sb("a_prob", [P, TG, 2, S])
        a_sum = sb("a_sum", [P, TG])
        a_rinv = sb("a_rinv", [P, TG])
        apT = sb("apT", [P, 2, GT], F16)
        a_out = sb("a_out", [P, TG, D])
        a_diag = sb("a_diag", [P, 2, TG, 2, 2, S], F16)
        a_r = sb("a_r", [P, TG, D])
        x1 = sb("x1", [P, NG * GT])

        c_in = sb("c_in", [P, TG, D])
        cT = sb("cT", [P, 2, GT], F16)
        kT = sb("kT", [P, 2, 2, GT // 2], F16)
        k_rows = sb("k_rows", [P, 2, 2, BG // 2, 4, S], F16)
        q_quad = sb("q_quad", [P, 2, 4, GT], F16)
        in_place4 = sb("in_place4", [P, 4, 4])
        in_place = sb("in_place", [P, 4])
        v_pair = sb("v_pair", [P, 2, BG, NHP, 2, VW], F16)
        x1q = sb("x1q", [P, TG, D])
        x1T = sb("x1T", [P, 2, GT], F16)
        qT = sb("qT", [P, 2, GT], F16)
        c_max = sb("c_max", [P, 2, H])
        p_f = sb("p_f", [P, 2, GT])
        p_hl = sb("p_hl", [P, 2, 2, 2, GT], F16)
        c_rinv = sb("c_rinv", [P, H])
        c_out = sb("c_out", [P, TG, D])
        oT = sb("oT", [P, 2, GT], F16)
        c_r = sb("c_r", [P, TG, D])
        x2 = sb("x2", [P, TG, ROW])

        st = sb("st", [P, TG, 6])
        ln = sb("ln", [P, 8, TG])
        ln_i = sb("ln_i", [P, 2, TG], I32)
        rt = sb("rt", [P, 8, TG])
        onehot = sb("onehot", [P, TG, NE])
        onehot_bf = sb("onehot_bf", [P, TG, NE], BF16)
        place = sb("place", [P, TG, NE])
        pos_f = sb("pos_f", [P, TG])
        pos_i = sb("pos_i", [P, TG], I32)
        token_f = sb("token_f", [P, TG])
        base = sb("base", [P, NE])
        count = sb("count", [P, NE])
        pad_f = sb("pad_f", [P, NE])
        pad_i = sb("pad_i", [P, NE], I32)
        tiles_e = sb("tiles_e", [P, 4, NE])
        done_e = sb("done_e", [P, 2, SLOTS, NE])
        slot_f = sb("slot_f", [P, 8, SLOTS])
        slot_row = sb("slot_row", [P, SLOTS], I32)
        slot_d = sb("slot_d", [P, SLOTS], I32)

        xs = sb("xs", [P, XB, ROW])
        xsT = sb("xsT", [P, 2, 2, P], F16)
        h_hl = sb("h_hl", [P, 2, 2, FF], F16)
        y_r = sb("y_r", [P, 2, D])
        f_st = sb("f_st", [P, 2, 6])
        f_mv = sb("f_mv", [P, 2, 2])
        f_sd = sb("f_sd", [P, 2, 2])
        y_out = sb("y_out", [P, YB, D])
        y_id = sb("y_id", [P, YB, 1], I32)
        eps_t = sb("eps_t", [P, 1])

        psum = [stack.enter_context(nc.psum_tensor(f"psum{i}", [P, 512], F32)) for i in range(8)]
        s_bank, t_bank = psum[0:2], psum[2:4]
        o_bank, m_bank, a_bank, b_bank = psum[4:8]

        names = """passed const_loaded wstage_loaded xin_loaded xres_loaded cin_loaded q_spread k_rows_ready dve_step y_step
            consts_pool consts_dve pe_setup act_setup dve_setup wsplit_hi wsplit_lo
            xT_ps xT_hi xT_lo gT_ps gT_hi gT_lo av_ps av_hi av_lo as_ps as_shifted as_exp as_rinv
            apT_ps apT_hi apT_lo ao_ps ao_scaled adiag_hi adiag_lo ay_ps a_read x1_ready
            cT_ps cT_hi cT_lo kT_ps kT_hi kT_lo v_ps v_hi v_lo x1q_ready x1T_ps x1T_hi x1T_lo
            qT_ps qT_hi qT_lo s_ps max_ready mT_ps nm_hi nm_lo st_ps exp_ready p_hi p_lo pv_ps co_ready
            oT_ps oT_hi oT_lo cy_ps c_read x2_ready onehot_ready rank_ps rank_read pos_ready scattered
            tables_ready wrapped pads_ready pad_written b_loaded b_hi b_lo xsT_ps xsT_hi xsT_lo
            h_ps h_hi h_lo y_ps y_read y_var y_sd y_ready""".split()
        names += [f"xs_loaded{k}" for k in range(XB)] + [f"y_written{k}" for k in range(YB)]
        s = {n: sem(n) for n in names}

        def after(eng, name, value):
            if isinstance(value, int) and value <= 0:
                return
            eng.wait_ge(s[name], value)

        def counts(eng, *values):
            return [v if isinstance(v, int) else eng.snap(v) for v in values]

        def passed(eng):
            eng.sem_inc(s["passed"], 1)

        class Steps:
            def __init__(self, eng, name):
                self.eng, self.name, self.start, self.n = eng, name, 0, 0

            def link(self, ins):
                ins.then_inc(s[self.name], 1)
                self.n += 1
                self.eng.wait_ge(s[self.name], self.start + self.n)

        def loop(eng, body, chain=None):
            body(0, 1, None)
            if chain is not None:
                first = chain.n
                trial = chain.per_body
                with eng.Fori(1, NG - 1) as g:
                    chain.start, chain.n = first + (g - 1) * trial, 0
                    body(g, g + 1, g - 1)
                    assert chain.n == trial, chain.n
                chain.start, chain.n = first + (NG - 2) * trial, 0
            else:
                with eng.Fori(1, NG - 1) as g:
                    body(g, g + 1, g - 1)
            body(NG - 1, None, NG - 2)

        def by_parity(ap):
            return ap.rearrange("p (a n v) -> p a n v", a=2, v=DK)

        def even_odd(ap):
            return ap.rearrange("p (n a v) -> p a n v", a=2, v=DK)

        def bc(ap, shape):
            return ap.broadcast_to(shape)

        SETUP_ORDER = (0, 1, 4, 5, 6, 7, 2, 3)
        SETUP_SPLITS = ((0, aqk), (1, avT), (4, cqT), (5, ckT), (6, cvT), (7, coT), (2, aoT[:, 0]), (3, aoT[:, 1]))
        SETUP_PS = len(SETUP_ORDER) + 1
        DVE_SETUP = len(SETUP_SPLITS) + 1
        POOL_CONSTS = 31
        ROUNDS = (SLOTS - 1) // UNROLL
        DVE_BODY = 58

        def expert_w(i, part, e):
            if i == 0:
                return w1[:, part, bass.ds(e * FF, FF)]
            return w2[:, bass.ds(e * FC * 2 * P, FC * 2 * P)].rearrange("p (c a d) -> p c a d", c=FC, a=2)[:, :, part, :]

        def staged(i):
            return w_stage[:, 0, :] if i == 0 else w_stage[:, 1, :].rearrange("p (c d) -> p c d", c=FC)

        def bias_parts():
            return [(b1_rows[32:32 + FC, :], b1_stage[:], b1_rows[0:FC, :]),
                    (b2_rows[32:33, :], b2_stage[0:1, :], b2_rows[0:1, :]),
                    (b2_rows[96:97, :], b2_stage[64:65, :], b2_rows[64:65, :])]

        block = stack.enter_context(nc.Block())

        @block.sync
        def _(sp):
            def tokens(flat, at):
                return flat[bass.ds(at, GT * D)].rearrange("(t p d) -> p t d", t=TG, p=P)

            def load_x(g):
                at, used = counts(sp, g * GT * D, g)
                after(sp, "xT_ps", used)
                passed(sp)
                sp.dma_start(x_in[:], tokens(x_flat, at)).then_inc(s["xin_loaded"], 16)

            def load_res(g):
                at, used = counts(sp, g * GT * D, g)
                after(sp, "a_read", used)
                passed(sp)
                sp.dma_start(x_res[:], tokens(x_flat, at)).then_inc(s["xres_loaded"], 16)

            def load_ctx(g):
                at, used = counts(sp, g * GT * D, g)
                after(sp, "cT_ps", used)
                passed(sp)
                sp.dma_start(c_in[:], tokens(ctx_flat, at)).then_inc(s["cin_loaded"], 16)

            def load_expert(e):
                at, used = counts(sp, e * D * FF, 2 * e)
                after(sp, "wsplit_lo", used)
                passed(sp)
                sp.dma_start(w_stage[:, 0, :], W1_flat[bass.ds(at, D * FF)].rearrange("(p f) -> p f", p=P))\
                    .then_inc(s["wstage_loaded"], 16)
                sp.dma_start(w_stage[:, 1, :].rearrange("p (c d) -> p c d", c=FC),
                             W2_flat[bass.ds(at, D * FF)].rearrange("(c p d) -> p c d", c=FC, p=P))\
                    .then_inc(s["wstage_loaded"], 16)

            def spread_q(g):
                split, used = counts(sp, g + 1, 2 * TG * g)
                sp.wait_ge(s["qT_lo"], split)
                passed(sp)
                after(sp, "st_ps", used)
                for n in range(4):
                    rows = slice(32 * n, 32 * n + 32)
                    sp.dma_start(q_quad[rows, :, n, :], qT[rows]).then_inc(s["q_spread"], 16)

            load_x(0)
            for n, w in enumerate((a_wq, a_wk, a_wv, a_wo, c_wq, c_wk, c_wv, c_wo)):
                sp.dma_start(w_raw[:, n, :], w).then_inc(s["const_loaded"], 16)
            for b in range(2):
                sp.dma_start(mask_u8[b * S:(b + 1) * S, :], mask[0, 0]).then_inc(s["const_loaded"], 16)
            load_ctx(0)
            load_res(0)
            b1_chunks = b1.rearrange("e (c p) -> c e p", p=P)
            sp.dma_start(b1_stage[:, 0:NE * P].rearrange("c (e p) -> c e p", p=P), b1_chunks).then_inc(s["b_loaded"], 16)
            sp.dma_start(b1_stage[:, NE * P:], b1_chunks[:, 0]).then_inc(s["b_loaded"], 16)
            b2_flat = b2.rearrange("e d -> (e d)").unsqueeze(0)
            sp.dma_start(b2_stage[0:1, :], b2_flat).then_inc(s["b_loaded"], 16)
            sp.dma_start(b2_stage[64:65, 0:(NE - 1) * D], b2_flat[:, D:]).then_inc(s["b_loaded"], 16)
            sp.dma_start(b2_stage[64:65, (NE - 1) * D:], b2_flat[:, 0:D]).then_inc(s["b_loaded"], 16)
            load_expert(0)
            sp.wait_ge(s["consts_pool"], POOL_CONSTS)

            def body(g, nxt, prev):
                if nxt is not None:
                    load_ctx(nxt)
                    load_x(nxt)
                spread_q(g)
                if nxt is not None:
                    load_res(nxt)
                    load_expert(nxt)

            loop(sp, body)

            sp.wait_ge(s["wsplit_lo"], 2 * NE)
            for i in range(2):
                sp.dma_start(w1[:, i, NE * FF:], w1[:, i, 0:FF]).then_inc(s["wrapped"], 16)
            sp.dma_start(w2[:, NE * FC * 2 * P:], w2[:, 0:FC * 2 * P]).then_inc(s["wrapped"], 16)

            sp.dma_start(sorted_flat[DUMMY * ROW:].rearrange("(p c) -> p c", p=P), pad_rows[:]).then_inc(s["pad_written"], 16)
            sp.wait_ge(s["pads_ready"], 1)
            for e in range(NE):
                at = sp.value_load(pad_i[0:1, e:e + 1], min_val=0, max_val=(DUMMY - P) * ROW)
                sp.dma_start(sorted_flat[bass.ds(at, P * ROW)].rearrange("(p c) -> p c", p=P), pad_rows[:])\
                    .then_inc(s["pad_written"], 16)

            sp.wait_ge(s["tables_ready"], 1)
            sp.wait_ge(s["scattered"], 16 * TG * NG)
            sp.wait_ge(s["pad_written"], 16 * (NE + 1))

            def load_slot(j, k):
                used, = counts(sp, j - XB + 1)
                at = sp.value_load(slot_row[0:1, bass.ds(j, 1)], min_val=0, max_val=DUMMY * ROW)
                after(sp, "y_var", used)
                passed(sp)
                sp.dma_start(xs[:, k, :], sorted_flat[bass.ds(at, P * ROW)].rearrange("(p c) -> p c", p=P))\
                    .then_inc(s[f"xs_loaded{k}"], 16)

            for j in range(XB):
                load_slot(j, j)
            with sp.Fori(1, SLOTS // XB) as i:
                for k in range(XB):
                    load_slot(XB * i + k, k)
            for j in range(SLOTS // XB * XB, SLOTS):
                load_slot(j, j % XB)
            for k in range(YB):
                sp.wait_ge(s[f"y_written{k}"], 16 * SLOTS // YB)

        @block.gpsimd
        def _(pool):
            done = [0]

            def const(ins):
                ins.then_inc(s["consts_pool"], 1)
                done[0] += 1
                pool.wait_ge(s["consts_pool"], done[0])

            const(pool.memset(ident[:], 0.0))
            const(pool.memset(ident_bf[:], 0.0))
            const(pool.memset(ones_bf[:], 1.0))
            const(pool.memset(before[:], 0.0))
            const(pool.memset(pick[:], 0.0))
            diag = dict(compare_op=ALU.not_equal, fill=1.0, base=0, pattern=[[-1, P]], channel_multiplier=1)
            const(pool.affine_select(out=ident[:], in_=ident[:], **diag))
            const(pool.affine_select(out=ident_bf[:], in_=ident_bf[:], **diag))
            const(pool.affine_select(out=before[:], in_=before[:], compare_op=ALU.is_ge, fill=1.0, base=0,
                                     pattern=[[-1, P]], channel_multiplier=1))
            for row in (0, 32):
                v = pick[row:row + H]
                const(pool.affine_select(out=v, in_=v, compare_op=ALU.not_equal, fill=1.0, base=0,
                                         pattern=[[-2, NHP], [-1, 2], [0, S]], channel_multiplier=1))
            v = pick[64:128]
            const(pool.affine_select(out=v, in_=v, compare_op=ALU.not_equal, fill=1.0, base=0,
                                     pattern=[[0, NHP], [0, 2], [-1, S]], channel_multiplier=1))
            const(pool.memset(in_place4[:], 1.0))
            for sign in (1, -1):
                const(pool.affine_select(out=in_place4[:], in_=in_place4[:], compare_op=ALU.is_ge, fill=0.0,
                                         base=0 if sign == 1 else DK - 1, pattern=[[-sign * DK, 4], [-sign * 32, 4]],
                                         channel_multiplier=sign))
            exact = dict(allow_small_or_imprecise_dtypes=True)
            const(pool.iota(iota_e[:], [[1, NE]], base=0, channel_multiplier=0, **exact))
            const(pool.iota(region_e[:], [[REGION, NE]], base=0, channel_multiplier=0, **exact))
            const(pool.iota(iota_slot[:], [[1, SLOTS]], base=0, channel_multiplier=0, **exact))
            const(pool.iota(token_f[:], [[P, TG]], base=-GT, channel_multiplier=1, **exact))
            const(pool.memset(q_quad[:], 0.0))
            const(pool.memset(negmax[:], 0.0))
            const(pool.memset(pad_rows[:], 0.0))
            const(pool.memset(x2[:], 0.0))
            const(pool.iota(pad_rows[:, D:D + 1].bitcast(I32), [[0, 1]], base=N, channel_multiplier=0))
            const(pool.memset(a_prob[:], 0.0))
            const(pool.memset(a_diag[:], 0.0))
            const(pool.memset(b1_rows[:], 0.0))
            const(pool.memset(b2_rows[:], 0.0))
            const(pool.memset(ones_h[:], 1.0))
            const(pool.memset(b1_ones[:], 0.0))
            for row in (0, 32):
                const(pool.affine_select(out=b1_ones[:], in_=b1_ones[:], compare_op=ALU.not_equal, fill=1.0, base=-row,
                                         pattern=[[-1, FC], [0, P]], channel_multiplier=1))
            assert done[0] == POOL_CONSTS, done[0]

            def split_low(e):
                for i in range(2):
                    pool.wait_ge(s["wsplit_hi"], 2 * e + i + 1)
                    pool.tensor_tensor(expert_w(i, 1, e), staged(i), expert_w(i, 0, e), ALU.subtract)\
                        .then_inc(s["wsplit_lo"], 1)

            def queries(g):
                ready, used = counts(pool, TG * (g + 1), g)
                pool.wait_ge(s["x1_ready"], ready)
                after(pool, "x1T_ps", used)
                pool.tensor_tensor(x1q[:].rearrange("p t d -> p (t d)"), x1[:, bass.ds(g * GT, GT)],
                                   bc(any_key[:, 0:1], [P, GT]), ALU.mult).then_inc(s["x1q_ready"], 1)

            def prob_low(g, t):
                n = TG * g + t
                for u in range(2):
                    pool.wait_ge(s["p_hi"], 2 * n + u + 1)
                    pool.tensor_tensor(p_hl[:, t % 2, u, 1, :], p_f[:, u, :], p_hl[:, t % 2, u, 0, :], ALU.subtract)\
                        .then_inc(s["p_lo"], 1)

            def scatter(g):
                ready, = counts(pool, g + 1)
                pool.wait_ge(s["consts_pool"], POOL_CONSTS)
                pool.wait_ge(s["pos_ready"], ready)
                for t in range(TG):
                    pool.indirect_dma_start(out=sorted_rows, out_offset=bass.IndirectOffsetOnAxis(ap=pos_i[:, t:t + 1], axis=0),
                                            in_=x2[:, t, :], in_offset=None).then_inc(s["scattered"], 16)

            def body(g, nxt, prev):
                queries(g)
                for t in range(TG):
                    prob_low(g, t)
                    if t == 1 and prev is not None:
                        scatter(prev)
                if nxt is not None:
                    split_low(nxt)

            pool.wait_ge(s["consts_dve"], 1)
            for n, (rows, src, hi) in enumerate(bias_parts()):
                pool.wait_ge(s["b_hi"], n + 1)
                pool.tensor_tensor(rows, src, hi, ALU.subtract).then_inc(s["b_lo"], 1)
                pool.wait_ge(s["b_lo"], n + 1)
            split_low(0)
            loop(pool, body)
            scatter(NG - 1)
            def write_rows(j, k):
                pool.wait_ge(s["y_ready"], j + 1)
                passed(pool)
                pool.indirect_dma_start(out=out_rows, out_offset=bass.IndirectOffsetOnAxis(ap=y_id[:, k, :], axis=0),
                                        in_=y_out[:, k, :], in_offset=None,
                                        bounds_check=last_token, oob_is_err=False).then_inc(s[f"y_written{k}"], 16)

            last_token = pool.to_reg(N - 1)
            with pool.Fori(0, SLOTS // YB) as i:
                for k in range(YB):
                    write_rows(YB * i + k, k)

        @block.tensor
        def _(pe):
            def transposes(dst, src, n, name):
                for t in range(n):
                    ins = pe.transpose(dst[:, t * P:(t + 1) * P], src[:, t, :], ident[:])
                ins.then_inc(s[name], 1)

            def product(dst, lhsT, rhs, last=True, first=True):
                for i, (a, b) in enumerate(PRODUCTS):
                    ins = pe.matmul(dst, lhsT(a), rhs(b), start=first and i == 0, stop=last and i == 2)
                return ins

            pe.wait_ge(s["const_loaded"], 16 * 10)
            pe.wait_ge(s["consts_pool"], POOL_CONSTS)
            pe.matmul(psum[0][:, 0:P], w_raw[:, 0, :], w_raw[:, 1, :], start=True, stop=True).then_inc(s["pe_setup"], 1)
            for i, n in ((1, 2), (4, 4), (5, 5), (6, 6), (7, 7)):
                pe.transpose(psum[i][:, 0:P], w_raw[:, n, :], ident[:]).then_inc(s["pe_setup"], 1)
            pe.wait_ge(s["consts_dve"], 3)
            for h in range(2):
                pe.transpose(psum[2 + h][:, 0:P], w_wo2[:, h, :], ident[:]).then_inc(s["pe_setup"], 1)
            pe.wait_ge(s["act_setup"], 1)
            pe.wait_ge(s["dve_setup"], 1)
            pe.transpose(psum[0][:, 0:S], mask_two[0:S].rearrange("p a k -> p (a k)"), ident[0:S, 0:S])\
                .then_inc(s["pe_setup"], 1)
            pe.wait_ge(s["dve_setup"], DVE_SETUP)

            def A_x(g):
                pe.wait_ge(s["xin_loaded"], 16 * (g + 1))
                after(pe, "a_read", g)
                transposes(a_bank, x_in, TG, "xT_ps")

            def A_g(g):
                pe.wait_ge(s["xT_lo"], g + 1)
                product(a_bank[:], lambda i: aqk[:, i, :], lambda i: xT[:, i, :]).then_inc(s["gT_ps"], 1)

            def A_v(g):
                pe.wait_ge(s["gT_lo"], g + 1)
                for t in range(TG):
                    cols = slice(t * P, t * P + P)
                    ins = product(a_bank[:, cols], lambda i: xT[:, i, cols], lambda i: avT[:, i, :])
                ins.then_inc(s["av_ps"], 1)

            def A_s(g):
                pe.wait_ge(s["av_lo"], g + 1)
                for t in range(TG):
                    for i, (a, b) in enumerate(PRODUCTS):
                        for q in range(2):
                            cols = slice(t * P + q * S, t * P + q * S + S)
                            ins = pe.matmul(a_bank[q * S:q * S + S, t * S:t * S + S], gT[:, a, cols], xT[:, b, cols],
                                            start=i == 0, stop=i == 2)
                ins.then_inc(s["as_ps"], 1)

            def A_p(g):
                pe.wait_ge(s["as_exp"], 2 * (g + 1))
                transposes(a_bank, a_prob[:].rearrange("p t b k -> p t (b k)"), TG, "apT_ps")

            def A_o(g):
                pe.wait_ge(s["apT_lo"], g + 1)
                for t in range(TG):
                    cols = slice(t * P, t * P + P)
                    ins = product(a_bank[:, cols], lambda i: apT[:, i, cols], lambda i: av[:, i, cols])
                ins.then_inc(s["ao_ps"], 1)

            def A_y(g):
                pe.wait_ge(s["adiag_lo"], 2 * (g + 1))
                for t in range(TG):
                    for h in range(2):
                        ins = product(a_bank[:, t * P:t * P + P],
                                      lambda i: a_diag[:, i, t, h, :, :].rearrange("p b r -> p (b r)"),
                                      lambda i: aoT[:, h, i, :], first=h == 0, last=h == 1)
                ins.then_inc(s["ay_ps"], 1)

            def K_x(g):
                pe.wait_ge(s["cin_loaded"], 16 * (g + 1))
                after(pe, "c_read", g - 1)
                transposes(b_bank, c_in, TG, "cT_ps")

            def K_k(g):
                pe.wait_ge(s["cT_lo"], g + 1)
                product(b_bank[:], lambda i: ckT[:, i, :], lambda i: cT[:, i, :]).then_inc(s["kT_ps"], 1)

            def K_v(g, u):
                if u == 0:
                    pe.wait_ge(s["kT_lo"], g + 1)
                else:
                    pe.wait_ge(s["v_lo"], 4 * g + 2)
                for b in range(BG // 2):
                    col = (u * BG // 2 + b) * S
                    for i, (m, n) in enumerate(PRODUCTS):
                        for a in range(2):
                            ins = pe.matmul(b_bank[a * S:a * S + S, b * S:b * S + S], cT[:, m, col:col + S],
                                            cvT[:, n, a * S:a * S + S], start=i == 0, stop=i == 2)
                ins.then_inc(s["v_ps"], 1)

            def B_x(g):
                pe.wait_ge(s["x1q_ready"], g + 1)
                pe.wait_ge(s["v_lo"], 4 * (g + 1))
                transposes(b_bank, x1q, TG, "x1T_ps")

            def B_q(g, prev):
                pe.wait_ge(s["x1T_lo"], g + 1)
                if prev is not None:
                    pe.wait_ge(s["oT_lo"], prev + 1)
                product(b_bank[:], lambda i: cqT[:, i, :], lambda i: x1T[:, i, :]).then_inc(s["qT_ps"], 1)

            def T_s(g, t):
                n = TG * g + t
                pe.wait_ge(s["q_spread"], 16 * 4 * (g + 1))
                pe.wait_ge(s["k_rows_ready"], 2 * g + t // 2 + 1)
                for u in range(2):
                    after(pe, "max_ready", 2 * (n - 1) + u + 1 if not isinstance(n, int) or n else 0)
                    for m in range(2):
                        for q in range(2):
                            cols = slice(t * P + q * S, t * P + q * S + S)
                            pe.matmul(s_bank[u][q * S:q * S + S, m * 4 * S:(m + 1) * 4 * S], q_quad[:, 0, 2 * u + m, cols],
                                      k_rows[:, t // 2, 0, 2 * (t % 2) + q].rearrange("p j k -> p (j k)"),
                                      start=m == 0, stop=False, skip_group_check=True)
                    pe.matmul(s_bank[u][:], ident_bf[:], bc(mask_bias[:].unsqueeze(1), [P, NHP, S]),
                              start=False, stop=True, skip_group_check=True).then_inc(s["s_ps"], 1)

            def T_m(g, t):
                n = TG * g + t
                pe.wait_ge(s["max_ready"], 2 * (n + 1))
                after(pe, "nm_lo", n)
                if t == 3:
                    after(pe, "rank_read", g)
                pe.transpose(m_bank[0:H, 0:P], c_max[:, t % 2, :], ident[:]).then_inc(s["mT_ps"], 1)

            def T_t(g, t):
                n = TG * g + t
                pe.wait_ge(s["nm_lo"], n + 1)
                for u in range(2):
                    after(pe, "exp_ready", 2 * (n - 1) + u + 1 if not isinstance(n, int) or n else 0)
                    for hp in range(NHP // 2):
                        pair = u * NHP // 2 + hp
                        pe.matmul(t_bank[u][:, hp * P:hp * P + P], pick[:, pair].rearrange("p a k -> p (a k)"),
                                  negmax[:, t % 2, :], start=hp == 0, stop=False, skip_group_check=True)
                        for q in range(2):
                            cols = slice(t * P + q * S, t * P + q * S + S)
                            for i, (a, b) in enumerate(PRODUCTS):
                                ins = pe.matmul(t_bank[u][:, hp * P + q * S:hp * P + q * S + S],
                                                k_rows[:, t // 2, a, 2 * (t % 2) + q, 2 * (pair % 2):2 * (pair % 2) + 2]
                                                .rearrange("p j k -> p (j k)"), q_quad[:, b, pair // 2, cols],
                                                start=False, stop=i == 2 and hp == NHP // 2 - 1 and q == 1,
                                                skip_group_check=True)
                    ins.then_inc(s["st_ps"], 1)

            def T_v(g, t):
                n = TG * g + t
                after(pe, "co_ready", 2 * n)
                pe.wait_ge(s["v_lo"], 4 * g + 2 * (t // 2) + 2)
                for u in range(2):
                    pe.wait_ge(s["p_lo"], 2 * n + u + 1)
                    for hp in range(NHP // 2):
                        pair = u * NHP // 2 + hp
                        ins = product(o_bank[:, pair * 4 * VW:(pair + 1) * 4 * VW],
                                      lambda i: p_hl[:, t % 2, u, i, hp * P:hp * P + P],
                                      lambda i: v_pair[:, i, 2 * t:2 * t + 2, pair].rearrange("p b a v -> p b (a v)"))
                ins.then_inc(s["pv_ps"], 1)

            def C_o(g, nxt):
                pe.wait_ge(s["co_ready"], 2 * TG * (g + 1))
                if isinstance(nxt, str):
                    pe.wait_ge(s["qT_lo"], g + 1)
                else:
                    pe.wait_ge(s["x1T_lo"], g + 2)
                transposes(b_bank, c_out, TG, "oT_ps")

            def C_y(g, nxt):
                pe.wait_ge(s["oT_lo"], g + 1)
                if not isinstance(nxt, str):
                    pe.wait_ge(s["qT_lo"], g + 2)
                for t in range(TG):
                    cols = slice(t * P, t * P + P)
                    ins = product(b_bank[:, cols], lambda i: oT[:, i, cols], lambda i: coT[:, i, :])
                ins.then_inc(s["cy_ps"], 1)

            def C_rank(g):
                pe.wait_ge(s["onehot_ready"], g + 1)
                pe.wait_ge(s["nm_lo"], TG * (g + 1) + (3 if g_in_body else 0))
                rank = m_bank[:, 0:TG * NE].rearrange("p (t e) -> p t e", t=TG)
                for t in range(TG):
                    pe.matmul(m_bank[:, 64:64 + NE], ones_bf[:], onehot_bf[:, t, :], start=t == 0, stop=t == TG - 1)
                for t in range(TG - 1):
                    pe.matmul(rank[:, t + 1:TG, :], ones_bf[:], bc(onehot_bf[:, t, :].unsqueeze(1), [P, TG - 1 - t, NE]),
                              start=False, stop=False, skip_group_check=True)
                ins = pe.matmul(rank, before[:], onehot_bf[:], start=False, stop=True, skip_group_check=True)
                ins.then_inc(s["rank_ps"], 1)

            g_in_body = True

            def body(g, nxt, prev):
                B_x(g)
                if prev is not None:
                    C_o(prev, g)
                B_q(g, prev)
                T_s(g, 0)
                if prev is not None:
                    C_y(prev, g)
                T_s(g, 1)
                T_m(g, 0)
                if nxt is not None:
                    K_x(nxt)
                T_t(g, 0)
                if nxt is not None:
                    A_x(nxt)
                T_m(g, 1)
                T_s(g, 2)
                if nxt is not None:
                    K_k(nxt)
                T_v(g, 0)
                if nxt is not None:
                    A_g(nxt)
                T_t(g, 1)
                if nxt is not None:
                    A_v(nxt)
                T_m(g, 2)
                T_s(g, 3)
                if prev is not None:
                    C_rank(prev)
                T_v(g, 1)
                if nxt is not None:
                    A_s(nxt)
                T_t(g, 2)
                if nxt is not None:
                    K_v(nxt, 0)
                T_m(g, 3)
                if nxt is not None:
                    A_p(nxt)
                T_v(g, 2)
                if nxt is not None:
                    A_o(nxt)
                T_t(g, 3)
                T_v(g, 3)
                if nxt is not None:
                    A_y(nxt)
                    K_v(nxt, 1)

            A_x(0)
            K_x(0)
            A_g(0)
            K_k(0)
            A_v(0)
            K_v(0, 0)
            A_s(0)
            K_v(0, 1)
            A_p(0)
            A_o(0)
            A_y(0)
            loop(pe, body)
            g_in_body = False
            C_o(NG - 1, "end")
            C_y(NG - 1, "end")
            C_rank(NG - 1)

            x_bank, h_bank, y_bank = psum[6:8], psum[0:2], psum[2:4]
            pe.wait_ge(s["tables_ready"], 1)
            pe.wait_ge(s["wrapped"], 48)
            pe.wait_ge(s["b_lo"], 3)


            def F_x(i, k):
                j = UNROLL * i + k
                pe.wait_ge(s[f"xs_loaded{k % XB}"], 16 * (i + k // XB + 1))
                after(pe, "xsT_lo", j - 1)
                pe.transpose(x_bank[k % 2][:, 0:P], xs[:, k % XB, 0:D], ident[:]).then_inc(s["xsT_ps"], 1)

            def F_h(j, k, u, d):
                if u == 0:
                    pe.wait_ge(s["xsT_hi"], j + 1)
                pe.matmul(h_bank[u][:], b1_rows[:, bass.ds(d, 2 * P)][:, u * P:u * P + P], b1_ones[:].rearrange("p c t -> p (c t)"),
                          start=True, stop=False, skip_group_check=True)
                for a, b in PRODUCTS:
                    if u == 0 and b == 1:
                        pe.wait_ge(s["xsT_lo"], j + 1)
                    for c in range(FC):
                        ins = pe.matmul(h_bank[u][:, c * P:c * P + P], w1[:, a, bass.ds(d * FC + (u * FC + c) * P, P)],
                                        xsT[:, k % 2, b, :], start=False, stop=b == 1 and c == FC - 1, skip_group_check=True)
                ins.then_inc(s["h_ps"], 1)

            def F_y(j, k, u, d):
                both, half = y_bank[k % 2][:, 0:2 * D], y_bank[k % 2][:, 0:D]
                if u == 0:
                    after(pe, "y_read", j - 1)
                pe.wait_ge(s["h_hi"], 2 * j + u + 1)
                at = [d * FC * 2 + (u * FC + c) * 2 * P for c in range(FC)]
                for c in range(FC):
                    pe.matmul(both, h_hl[:, u, 0, c * P:c * P + P], w2[:, bass.ds(at[c], 2 * P)],
                              start=u == 0 and c == 0, stop=False, skip_group_check=True)
                if u == 0:
                    pe.matmul(half, ones_h[:], b2_rows[:, bass.ds(d, D)], start=False, stop=False, skip_group_check=True)
                pe.wait_ge(s["h_lo"], 2 * j + u + 1)
                for c in range(FC):
                    ins = pe.matmul(half, h_hl[:, u, 1, c * P:c * P + P], w2[:, bass.ds(at[c], P)],
                                    start=False, stop=u == 1 and c == FC - 1, skip_group_check=True)
                if u == 1:
                    ins.then_inc(s["y_ps"], 1)

            def expert(j):
                return pe.value_load(slot_d[0:1, bass.ds(j, 1)], min_val=0, max_val=(NE - 1) * D)

            def F_round(i, steps):
                d_next = expert(UNROLL * i)
                for k in range(steps):
                    j = UNROLL * i + k
                    d, d_next = d_next, expert(j + 1)
                    if not isinstance(i, int) or j + 2 < SLOTS:
                        F_x(i, k + 2)
                    F_y(j, k, 0, d)
                    F_h(j + 1, k + 1, 0, d_next)
                    F_y(j, k, 1, d)
                    F_h(j + 1, k + 1, 1, d_next)

            F_x(0, 0)
            F_x(0, 1)
            d = expert(0)
            F_h(0, 0, 0, d)
            F_h(0, 0, 1, d)
            F_round(0, UNROLL)
            with pe.Fori(1, ROUNDS) as i:
                F_round(i, UNROLL)
            F_round(ROUNDS, SLOTS - 1 - UNROLL * ROUNDS)
            d = expert(SLOTS - 1)
            F_y(SLOTS - 1, SLOTS - 1, 0, d)
            F_y(SLOTS - 1, SLOTS - 1, 1, d)

        @block.scalar
        def _(act):
            def high(dst, src, name, **kw):
                act.activation(dst, src, ACT.Copy, **kw).then_inc(s[name], 1)

            for i, dst in SETUP_SPLITS:
                act.wait_ge(s["pe_setup"], SETUP_ORDER.index(i) + 1)
                high(by_parity(dst[:, 0, :]) if i == 6 else dst[:, 0, :],
                     even_odd(psum[i][:, 0:P]) if i == 6 else psum[i][:, 0:P], "act_setup")
            act.wait_ge(s["pe_setup"], SETUP_PS)
            for k in range(2):
                for q in range(2):
                    high(negmax[64:128, k, q * S:q * S + S], psum[0][64:128, 0:S], "act_setup")

            def split_high(e):
                act.wait_ge(s["wstage_loaded"], 32 * (e + 1))
                for i in range(2):
                    high(expert_w(i, 0, e), staged(i), "wsplit_hi")

            def plain(name, dst, bank):
                def step(g):
                    act.wait_ge(s[name + "_ps"], g + 1)
                    high(dst[:, 0, :], bank[:], name + "_hi")
                return step

            A_x, A_g, A_v = plain("xT", xT, a_bank), plain("gT", gT, a_bank), plain("av", av, a_bank)
            A_p, K_x = plain("apT", apT, a_bank), plain("cT", cT, b_bank)
            B_x, C_o = plain("x1T", x1T, b_bank), plain("oT", oT, b_bank)

            def A_s(g):
                act.wait_ge(s["as_shifted"], g + 1)
                after(act, "apT_ps", g)
                for b in range(2):
                    rows = slice(b * S, b * S + S)
                    act.activation(a_prob[rows, :, b, :], a_shift[rows], ACT.Exp, scale=A_SCALE).then_inc(s["as_exp"], 1)

            def A_o(g):
                act.wait_ge(s["ao_scaled"], g + 1)
                for b in range(2):
                    rows = slice(b * S, b * S + S)
                    for h in range(2):
                        src = a_out[rows].rearrange("p t (r h) -> p t h r", h=2)[:, :, h, :]
                        ins = act.activation(a_diag[rows, 0, :, h, b, :], src, ACT.Copy)
                    ins.then_inc(s["adiag_hi"], 1)

            def K_k(g):
                act.wait_ge(s["kT_ps"], g + 1)
                after(act, "k_rows_ready", 2 * g)
                high(kT[:, :, 0, :], b_bank[:].rearrange("p (u k) -> p u k", u=2), "kT_hi")

            def K_v(g, u):
                act.wait_ge(s["v_ps"], 2 * g + u + 1)
                after(act, "pv_ps", TG * (g - 1) + 2 * u + 2 if not isinstance(g, int) or g else 0)
                for a in range(2):
                    rows = slice(a * S, a * S + S)
                    src = b_bank[rows, 0:GT // 2].rearrange("p (b n v) -> p b n v", b=BG // 2, v=DK)
                    high(v_pair[rows, 0, u * BG // 2:(u + 1) * BG // 2, :, a, 0:DK], src, "v_hi")

            def B_q(g):
                act.wait_ge(s["qT_ps"], g + 1)
                high(qT[:, 0, :], b_bank[:], "qT_hi", scale=C_SCALE)

            def T_m(g, t):
                act.wait_ge(s["mT_ps"], TG * g + t + 1)
                high(negmax[0:H, t % 2, :], m_bank[0:H, 0:P], "nm_hi", scale=-1.0)

            def T_t(g, t):
                n = TG * g + t
                for u in range(2):
                    act.wait_ge(s["st_ps"], 2 * n + u + 1)
                    after(act, "p_lo", 2 * (n - 1) + u + 1 if not isinstance(n, int) or n else 0)
                    act.activation(p_f[:, u, :], t_bank[u][:], ACT.Exp).then_inc(s["exp_ready"], 1)
                    act.wait_ge(s["exp_ready"], 2 * n + u + 1)
                    after(act, "pv_ps", n - 1)
                    high(p_hl[:, t % 2, u, 0, :], p_f[:, u, :], "p_hi")

            def body(g, nxt, prev):
                B_x(g)
                if prev is not None:
                    C_o(prev)
                B_q(g)
                T_m(g, 0)
                if nxt is not None:
                    K_x(nxt)
                T_t(g, 0)
                if nxt is not None:
                    A_x(nxt)
                T_m(g, 1)
                if nxt is not None:
                    K_k(nxt)
                    A_g(nxt)
                T_t(g, 1)
                if nxt is not None:
                    A_v(nxt)
                T_m(g, 2)
                if nxt is not None:
                    A_s(nxt)
                T_t(g, 2)
                if nxt is not None:
                    K_v(nxt, 0)
                T_m(g, 3)
                if nxt is not None:
                    A_p(nxt)
                    A_o(nxt)
                T_t(g, 3)
                if nxt is not None:
                    K_v(nxt, 1)
                    split_high(nxt)

            A_x(0)
            K_x(0)
            A_g(0)
            K_k(0)
            A_v(0)
            K_v(0, 0)
            A_s(0)
            K_v(0, 1)
            A_p(0)
            A_o(0)
            act.wait_ge(s["b_loaded"], 16 * 5)
            act.wait_ge(s["consts_pool"], POOL_CONSTS)
            for rows, src, hi in bias_parts():
                high(hi, src, "b_hi")
            split_high(0)
            loop(act, body)
            C_o(NG - 1)


            x_bank, h_bank = psum[6:8], psum[0:2]

            def F_x(j, k):
                act.wait_ge(s["xsT_ps"], j + 1)
                high(xsT[:, k % 2, 0, :], x_bank[k % 2][:, 0:P], "xsT_hi")

            def F_h(j, u):
                act.wait_ge(s["h_ps"], 2 * j + u + 1)
                act.activation(h_hl[:, u, 0, :], h_bank[u][:], ACT.Relu).then_inc(s["h_hi"], 1)

            def F_sd(j, k):
                act.wait_ge(s["y_var"], j + 1)
                act.activation(f_sd[:, k % 2, 0:1], f_mv[:, k % 2, 1:2], ACT.Sqrt, bias=eps_t[:, 0:1]).then_inc(s["y_sd"], 1)

            def F_round(i, steps):
                for k in range(steps):
                    j = UNROLL * i + k
                    if not isinstance(i, int) or j + 2 < SLOTS:
                        F_x(j + 2, k)
                    F_h(j + 1, 0)
                    F_h(j + 1, 1)
                    F_sd(j, k)

            F_x(0, 0)
            F_x(1, 1)
            F_h(0, 0)
            F_h(0, 1)
            F_round(0, UNROLL)
            with act.Fori(1, ROUNDS) as i:
                F_round(i, UNROLL)
            F_round(ROUNDS, SLOTS - 1 - UNROLL * ROUNDS)
            F_sd(SLOTS - 1, SLOTS - 1)

        @block.vector
        def _(dve):
            chain = Steps(dve, "dve_step")
            chain.per_body = DVE_BODY
            link = chain.link

            dve.memset(eps_t[:], EPS)
            dve.wait_ge(s["const_loaded"], 16 * 10)
            link(dve.tensor_copy(mask_f[:], mask_u8[:]))
            dve.tensor_reduce(any_key[:], mask_f[:], AX.X, ALU.max).then_inc(s["consts_dve"], 1)
            link(dve.tensor_scalar(mask_two[:], bc(mask_f[:].unsqueeze(1), [P, 2, S]), 1.0, 1e9, ALU.subtract, ALU.mult))
            dve.tensor_copy(mask_bias[:], mask_two[:, 0, :]).then_inc(s["consts_dve"], 1)
            dve.tensor_copy(w_wo2[:].rearrange("p h (a q) -> p h a q", a=2),
                            bc(w_raw[:, 3, :].rearrange("p (h q) -> p h q", h=2).unsqueeze(2), [P, 2, 2, S]))\
                .then_inc(s["consts_dve"], 1)
            dve.wait_ge(s["consts_pool"], POOL_CONSTS)
            link(dve.tensor_reduce(in_place[:], in_place4[:], AX.X, ALU.add))
            link(dve.memset(v_pair[:], 0.0))
            for a in range(2):
                link(dve.memset(v_pair[a * S:a * S + S, 0, :, :, a, DK:VW], 1.0))
            link(dve.tensor_copy(base[:], region_e[:]))
            for n, (i, dst) in enumerate(SETUP_SPLITS):
                dve.wait_ge(s["act_setup"], n + 1)
                if i == 6:
                    ins = dve.tensor_tensor(by_parity(dst[:, 1, :]), even_odd(psum[i][:, 0:P]), by_parity(dst[:, 0, :]),
                                            ALU.subtract)
                else:
                    ins = dve.tensor_tensor(dst[:, 1, :], psum[i][:, 0:P], dst[:, 0, :], ALU.subtract)
                ins.then_inc(s["dve_setup"], 1)
            dve.wait_ge(s["act_setup"], len(SETUP_SPLITS) + 4)
            dve.memset(a_max[:], 0.0).then_inc(s["dve_setup"], 1)

            def low(dst, src, hi, hi_name, count, name):
                dve.wait_ge(s[hi_name], count)
                dve.tensor_tensor(dst, src, hi, ALU.subtract).then_inc(s[name], 1)

            def k_low(g):
                low(kT[:, :, 1, :], b_bank[:].rearrange("p (u k) -> p u k", u=2), kT[:, :, 0, :], "kT_hi", g + 1, "kT_lo")

            def plain(name, dst, bank):
                return lambda g: low(dst[:, 1, :], bank[:], dst[:, 0, :], name + "_hi", g + 1, name + "_lo")

            A_x, A_g, A_v = plain("xT", xT, a_bank), plain("gT", gT, a_bank), plain("av", av, a_bank)
            A_p, K_x, K_k = plain("apT", apT, a_bank), plain("cT", cT, b_bank), k_low
            B_x, C_o = plain("x1T", x1T, b_bank), plain("oT", oT, b_bank)

            def normalise(r, dst, name):
                for t in range(TG):
                    ins = dve.bn_stats(st[:, t, :], r[:, t, :])
                link(ins)
                total, diff, m2, v, mean, y, w, half = (ln[:, i, :] for i in range(8))
                dve.tensor_tensor(total, st[:, :, 1], st[:, :, 4], ALU.add)
                dve.tensor_tensor(m2, st[:, :, 2], st[:, :, 5], ALU.add)
                link(dve.tensor_tensor(diff, st[:, :, 1], st[:, :, 4], ALU.subtract))
                link(dve.tensor_tensor(diff, diff, diff, ALU.mult))
                link(dve.scalar_tensor_tensor(out=m2, in0=diff, scalar=D / 4.0, in1=m2, op0=ALU.mult, op1=ALU.add))
                dve.tensor_scalar(mean, total, 0.5, None, ALU.mult)
                link(dve.tensor_scalar(v, m2, 1.0 / D, EPS, ALU.mult, ALU.add))
                dve.tensor_scalar(half, v, -0.5, None, ALU.mult)
                link(dve.tensor_scalar(ln_i[:, 0, :], v.bitcast(I32), 1, None, ALU.arith_shift_right))
                link(dve.tensor_scalar(ln_i[:, 1, :], ln_i[:, 0, :], -1.0, 1597463007.0, ALU.mult, ALU.add))
                guess = ln_i[:, 1, :].bitcast(F32)
                for k in range(3):
                    y_in = guess if k == 0 else y
                    link(dve.tensor_tensor(w, y_in, y_in, ALU.mult))
                    link(dve.tensor_tensor(w, w, half, ALU.mult))
                    link(dve.scalar_tensor_tensor(out=y, in0=w, scalar=1.5, in1=y_in, op0=ALU.add, op1=ALU.mult))
                for t in range(TG):
                    dve.tensor_scalar(dst(t), r[:, t, :], mean[:, t:t + 1], y[:, t:t + 1], ALU.subtract, ALU.mult)\
                        .then_inc(s[name], 1)

            def A_s(g):
                dve.wait_ge(s["as_ps"], g + 1)
                scores = a_bank[:, 0:TG * S].rearrange("p (t k) -> p t k", t=TG)
                link(dve.tensor_reduce(a_max[:], scores, AX.X, ALU.max))
                dve.tensor_tensor(a_shift[:], scores, bc(a_max[:].unsqueeze(2), [P, TG, S]), ALU.subtract)\
                    .then_inc(s["as_shifted"], 1)

            def A_sum(g):
                dve.wait_ge(s["as_exp"], 2 * (g + 1))
                link(dve.tensor_reduce(a_sum[:], a_prob[:].rearrange("p t b k -> p t (b k)"), AX.X, ALU.add))
                link(dve.reciprocal(a_rinv[:], a_sum[:]))

            def A_o(g):
                dve.wait_ge(s["ao_ps"], g + 1)
                dve.tensor_tensor(a_out[:], a_bank[:].rearrange("p (t d) -> p t d", t=TG),
                                  bc(a_rinv[:].unsqueeze(2), [P, TG, D]), ALU.mult).then_inc(s["ao_scaled"], 1)
                for b in range(2):
                    rows = slice(b * S, b * S + S)
                    dve.wait_ge(s["adiag_hi"], 2 * g + b + 1)
                    for h in range(2):
                        src = a_out[rows].rearrange("p t (r h) -> p t h r", h=2)[:, :, h, :]
                        ins = dve.tensor_tensor(a_diag[rows, 1, :, h, b, :], src, a_diag[rows, 0, :, h, b, :], ALU.subtract)
                    ins.then_inc(s["adiag_lo"], 1)

            def A_y(g):
                dve.wait_ge(s["ay_ps"], g + 1)
                dve.wait_ge(s["xres_loaded"], 16 * (g + 1))
                dve.tensor_tensor(a_r[:], a_bank[:].rearrange("p (t d) -> p t d", t=TG), x_res[:], ALU.add)\
                    .then_inc(s["a_read"], 1)
                dve.wait_ge(s["a_read"], g + 1)
                normalise(a_r, lambda t: x1[:, bass.ds(g * GT + t * D, D)], "x1_ready")

            def K_rows(g, u):
                dve.wait_ge(s["kT_lo"], g + 1)
                after(dve, "st_ps", 2 * TG * (g - 1) + 4 * u + 4 if not isinstance(g, int) or g else 0)
                for j in range(4):
                    ins = dve.tensor_scalar(k_rows[:, u, :, :, j, :].rearrange("p i b k -> p (i b) k"),
                                            kT[:, u].rearrange("p i (b k) -> p (i b) k", k=S),
                                            in_place[:, j:j + 1], None, ALU.mult)
                ins.then_inc(s["k_rows_ready"], 1)

            def K_v(g, u):
                for a in range(2):
                    rows = slice(a * S, a * S + S)
                    src = b_bank[rows, 0:GT // 2].rearrange("p (b n v) -> p b n v", b=BG // 2, v=DK)
                    seq = slice(u * BG // 2, (u + 1) * BG // 2)
                    low(v_pair[rows, 1, seq, :, a, 0:DK], src, v_pair[rows, 0, seq, :, a, 0:DK],
                        "v_hi", 4 * g + 2 * u + a + 1, "v_lo")

            def B_q(g):
                dve.wait_ge(s["qT_hi"], g + 1)
                dve.scalar_tensor_tensor(out=qT[:, 1, :], in0=b_bank[:], scalar=C_SCALE, in1=qT[:, 0, :],
                                         op0=ALU.mult, op1=ALU.subtract).then_inc(s["qT_lo"], 1)

            def T_s(g, t):
                n = TG * g + t
                after(dve, "mT_ps", n - 1)
                for u in range(2):
                    dve.wait_ge(s["s_ps"], 2 * n + u + 1)
                    dve.tensor_reduce(c_max[:, t % 2, u * NHP:(u + 1) * NHP],
                                      s_bank[u][:].rearrange("p (h k) -> p h k", h=NHP), AX.X, ALU.max)\
                        .then_inc(s["max_ready"], 1)

            def T_m(g, t):
                n = TG * g + t
                dve.wait_ge(s["nm_hi"], n + 1)
                dve.scalar_tensor_tensor(out=negmax[32:32 + H, t % 2, :], in0=m_bank[0:H, 0:P], scalar=-1.0,
                                         in1=negmax[0:H, t % 2, :], op0=ALU.mult, op1=ALU.subtract).then_inc(s["nm_lo"], 1)

            def T_v(g, t):
                n = TG * g + t
                dve.wait_ge(s["pv_ps"], n + 1)
                if t == 0:
                    after(dve, "oT_ps", g)
                for b in range(2):
                    rows = slice(b * S, b * S + S)
                    o = o_bank[rows, 0:NHP * 4 * VW].rearrange("p (n b a v) -> p n b a v", b=2, a=2, v=VW)[:, :, b]
                    dve.reciprocal(c_rinv[rows].rearrange("p (n a) -> p n a", a=2), o[:, :, :, DK])\
                        .then_inc(s["dve_step"], 1)
                    chain.n += 1
                dve.wait_ge(s["dve_step"], chain.start + chain.n)
                for b in range(2):
                    rows = slice(b * S, b * S + S)
                    o = o_bank[rows, 0:NHP * 4 * VW].rearrange("p (n b a v) -> p n b a v", b=2, a=2, v=VW)[:, :, b]
                    dve.tensor_tensor(c_out[rows, t, :].rearrange("p (n a v) -> p n a v", a=2, v=DK), o[:, :, :, 0:DK],
                                      bc(c_rinv[rows].rearrange("p (n a) -> p n a", a=2).unsqueeze(3), [S, NHP, 2, DK]),
                                      ALU.mult).then_inc(s["co_ready"], 1)

            def C_y(g):
                dve.wait_ge(s["cy_ps"], g + 1)
                dve.tensor_tensor(c_r[:].rearrange("p t d -> p (t d)"), b_bank[:], x1[:, bass.ds(g * GT, GT)], ALU.add)\
                    .then_inc(s["c_read"], 1)
                dve.wait_ge(s["c_read"], g + 1)
                after(dve, "scattered", 16 * TG * g)
                normalise(c_r, lambda t: x2[:, t, 0:D], "x2_ready")
                link(dve.tensor_scalar(token_f[:], token_f[:], float(GT), None, ALU.add))
                dve.tensor_copy(x2[:, :, D].bitcast(I32), token_f[:]).then_inc(s["x2_ready"], 1)

            def C_route(g):
                dve.wait_ge(s["x2_ready"], (TG + 1) * (g + 1))
                v, mag, near, over, sign, trunc, m8, h = (rt[:, i, :] for i in range(8))
                link(dve.tensor_tensor(v, x2[:, :, 0], x2[:, :, 1], ALU.add))
                link(dve.tensor_scalar(sign, v, 0.0, 2.0, ALU.is_ge, ALU.mult))
                link(dve.scalar_tensor_tensor(out=mag, in0=sign, scalar=-1.0, in1=v, op0=ALU.add, op1=ALU.mult))
                link(dve.tensor_scalar(near, mag, ROUND, ROUND, ALU.add, ALU.subtract))
                link(dve.tensor_tensor(over, near, mag, ALU.is_gt))
                link(dve.tensor_tensor(near, near, over, ALU.subtract))
                link(dve.scalar_tensor_tensor(out=trunc, in0=sign, scalar=-1.0, in1=near, op0=ALU.add, op1=ALU.mult))
                link(dve.tensor_scalar(m8, trunc, 1.0 / NE, -0.4375, ALU.mult, ALU.add))
                link(dve.tensor_scalar(m8, m8, ROUND, ROUND, ALU.add, ALU.subtract))
                link(dve.scalar_tensor_tensor(out=h, in0=m8, scalar=-float(NE), in1=trunc, op0=ALU.mult, op1=ALU.add))
                link(dve.tensor_tensor(onehot[:], bc(iota_e[:].unsqueeze(1), [P, TG, NE]), bc(h.unsqueeze(2), [P, TG, NE]),
                                       ALU.is_equal))
                dve.tensor_copy(onehot_bf[:], onehot[:]).then_inc(s["onehot_ready"], 1)

            def C_rank(g):
                dve.wait_ge(s["rank_ps"], g + 1)
                after(dve, "scattered", 16 * TG * g)
                rank = m_bank[:, 0:TG * NE].rearrange("p (t e) -> p t e", t=TG)
                link(dve.tensor_tensor(place[:], rank, bc(base[:].unsqueeze(1), [P, TG, NE]), ALU.add))
                link(dve.tensor_tensor(place[:], place[:], onehot[:], ALU.mult))
                dve.tensor_tensor(base[:], m_bank[:, 64:64 + NE], base[:], ALU.add).then_inc(s["rank_read"], 1)
                link(dve.tensor_reduce(pos_f[:], place[:], AX.X, ALU.add))
                dve.tensor_copy(pos_i[:], pos_f[:]).then_inc(s["pos_ready"], 1)

            def body(g, nxt, prev):
                B_x(g)
                if prev is not None:
                    C_o(prev)
                B_q(g)
                T_s(g, 0)
                if prev is not None:
                    C_y(prev)
                T_s(g, 1)
                T_m(g, 0)
                if nxt is not None:
                    K_x(nxt)
                    A_x(nxt)
                T_m(g, 1)
                if prev is not None:
                    C_route(prev)
                T_s(g, 2)
                if nxt is not None:
                    K_k(nxt)
                T_v(g, 0)
                if nxt is not None:
                    A_g(nxt)
                    A_v(nxt)
                T_m(g, 2)
                T_s(g, 3)
                if prev is not None:
                    C_rank(prev)
                T_v(g, 1)
                if nxt is not None:
                    A_s(nxt)
                    K_rows(nxt, 0)
                    K_v(nxt, 0)
                T_m(g, 3)
                if nxt is not None:
                    A_sum(nxt)
                    A_p(nxt)
                T_v(g, 2)
                if nxt is not None:
                    A_o(nxt)
                T_v(g, 3)
                if nxt is not None:
                    K_rows(nxt, 1)
                    A_y(nxt)
                    K_v(nxt, 1)

            A_x(0)
            K_x(0)
            A_g(0)
            K_k(0)
            K_rows(0, 0)
            K_rows(0, 1)
            A_v(0)
            K_v(0, 0)
            A_s(0)
            K_v(0, 1)
            A_sum(0)
            A_p(0)
            A_o(0)
            A_y(0)
            loop(dve, body, chain)
            C_o(NG - 1)
            C_y(NG - 1)
            C_route(NG - 1)
            C_rank(NG - 1)

            dve.wait_ge(s["rank_read"], NG)
            link(dve.tensor_scalar(pad_f[:], base[:], float(ROW), None, ALU.mult))
            dve.tensor_copy(pad_i[:], pad_f[:]).then_inc(s["pads_ready"], 1)
            link(dve.tensor_tensor(count[:], base[:], region_e[:], ALU.subtract))
            link(dve.tensor_scalar(tiles_e[:, 0, :], count[:], 1.0 / P, (P - 1.0) / P - 0.49609375, ALU.mult, ALU.add))
            link(dve.tensor_scalar(tiles_e[:, 1, :], tiles_e[:, 0, :], ROUND, ROUND, ALU.add, ALU.subtract))
            a = 1
            for step in (1, 2, 4):
                b = 2 if a != 2 else 3
                link(dve.tensor_copy(tiles_e[:, b, 0:step], tiles_e[:, a, 0:step]))
                link(dve.tensor_tensor(tiles_e[:, b, step:NE], tiles_e[:, a, step:NE], tiles_e[:, a, 0:NE - step], ALU.add))
                a = b
            upto = bc(tiles_e[:, a, :].unsqueeze(1), [P, SLOTS, NE])
            link(dve.tensor_tensor(done_e[:, 0], upto, bc(iota_slot[:].unsqueeze(2), [P, SLOTS, NE]), ALU.is_le))
            link(dve.tensor_tensor(done_e[:, 1], done_e[:, 0], upto, ALU.mult))
            expert, first, row, wrow, t4, t5 = (slot_f[:, i, :] for i in range(6))
            dve.tensor_reduce(expert, done_e[:, 0], AX.X, ALU.add)
            link(dve.tensor_reduce(first, done_e[:, 1], AX.X, ALU.max))
            link(dve.tensor_tensor(row, iota_slot[:], first, ALU.subtract))
            link(dve.tensor_scalar(row, row, float(P), None, ALU.mult))
            link(dve.scalar_tensor_tensor(out=row, in0=expert, scalar=float(REGION), in1=row, op0=ALU.mult, op1=ALU.add))
            link(dve.tensor_scalar(row, row, float(DUMMY), None, ALU.min))
            link(dve.tensor_scalar(wrow, expert, NE - 1.0, None, ALU.min))
            dve.tensor_scalar(slot_row[:], row, float(ROW), None, ALU.mult)
            dve.tensor_scalar(slot_d[:], wrow, float(D), None, ALU.mult).then_inc(s["tables_ready"], 1)

            x_bank, h_bank, y_bank = psum[6:8], psum[0:2], psum[2:4]
            y_chain = Steps(dve, "y_step")

            def F_x(j, k):
                low(xsT[:, k % 2, 1, :], x_bank[k % 2][:, 0:P], xsT[:, k % 2, 0, :], "xsT_hi", j + 1, "xsT_lo")

            def F_h(j, u):
                dve.wait_ge(s["h_hi"], 2 * j + u + 1)
                dve.scalar_tensor_tensor(out=h_hl[:, u, 1, :], in0=h_bank[u][:], scalar=0.0, in1=h_hl[:, u, 0, :],
                                         op0=ALU.max, op1=ALU.subtract).then_inc(s["h_lo"], 1)

            def F_out(j, k, written):
                dve.wait_ge(s["y_ps"], j + 1)
                y_chain.link(dve.scalar_tensor_tensor(out=y_r[:, k % 2, :], in0=y_bank[k % 2][:, 0:D], scalar=0.5,
                                                      in1=xs[:, k % XB, 0:D], op0=ALU.mult, op1=ALU.add))
                dve.scalar_tensor_tensor(out=y_r[:, k % 2, :], in0=y_bank[k % 2][:, D:2 * D], scalar=0.5,
                                         in1=y_r[:, k % 2, :], op0=ALU.mult, op1=ALU.add).then_inc(s["y_read"], 1)
                dve.wait_ge(s["y_read"], j + 1)
                y_chain.link(dve.bn_stats(f_st[:, k % 2, :], y_r[:, k % 2, :]))
                after(dve, f"y_written{k % YB}", written)
                dve.tensor_copy(y_id[:, k % YB, :], xs[:, k % XB, D:D + 1].bitcast(I32))
                dve.bn_aggr(f_mv[:, k % 2, :], f_st[:, k % 2, :]).then_inc(s["y_var"], 1)

            def F_norm(j, k):
                dve.wait_ge(s["y_sd"], j + 1)
                y_chain.link(dve.reciprocal(f_sd[:, k % 2, 1:2], f_sd[:, k % 2, 0:1]))
                dve.tensor_scalar(y_out[:, k % YB, :], y_r[:, k % 2, :], f_mv[:, k % 2, 0:1], f_sd[:, k % 2, 1:2],
                                  ALU.subtract, ALU.mult).then_inc(s["y_ready"], 1)

            def F_round(i, steps):
                for k in range(steps):
                    j = UNROLL * i + k
                    if not isinstance(i, int) or j + 2 < SLOTS:
                        F_x(j + 2, k)
                    if not isinstance(i, int) or j > 0:
                        F_norm(j - 1, k + UNROLL - 1)
                    F_h(j + 1, 0)
                    F_out(j, k, 16 * (UNROLL // YB * i + k // YB))
                    F_h(j + 1, 1)

            F_x(0, 0)
            F_x(1, 1)
            F_h(0, 0)
            F_h(0, 1)
            F_round(0, UNROLL)
            first_round = y_chain.n
            with dve.Fori(1, ROUNDS) as i:
                y_chain.start, y_chain.n = first_round + (i - 1) * 3 * UNROLL, 0
                F_round(i, UNROLL)
                assert y_chain.n == 3 * UNROLL
            y_chain.start, y_chain.n = first_round + (ROUNDS - 1) * 3 * UNROLL, 0
            F_round(ROUNDS, SLOTS - 1 - UNROLL * ROUNDS)
            last = SLOTS - 1
            F_norm(last - 1, last - 1)
            F_out(last, last, 16 * (last // YB))
            F_norm(last, last)


_INS = ["x", "ctx_1024", "mask_1x1xSxS2_bf1", "L0_attn_wq", "L0_attn_wk", "L0_attn_wv", "L0_attn_wo",
        "L0_xattn_w_q", "L0_xattn_w_k", "L0_xattn_w_v", "L0_xattn_w_o",
        "L0_ffn_W1", "L0_ffn_b1", "L0_ffn_W2", "L0_ffn_b2"]


def kernel(**inputs):
    import concourse.bacc as _bacc
    from concourse.bass_utils import run_bass_kernel_spmd as _run

    nc = _bacc.Bacc("TRN2", target_bir_lowering=False, num_devices=1)
    arrays, args = {}, []
    for name in _INS:
        a = np.ascontiguousarray(inputs[name])
        if a.dtype == np.bool_:
            a = a.view(np.uint8)
        arrays[f"in_{name}"] = a
        args.append(nc.dram_tensor(f"in_{name}", a.shape, mybir.dt.from_np(a.dtype), kind="ExternalInput").ap())
    args.append(nc.dram_tensor("out_dram", arrays["in_x"].shape, F32, kind="ExternalOutput").ap())
    decoder_layer_kernel(nc, *args)
    r = _run(nc, [arrays], core_ids=[0])
    return r.results[0]["out_dram"]
```

```python
from contextlib import ExitStack

import numpy as np
import concourse.bass as bass
from concourse import mybir

F32 = mybir.dt.float32
F16 = mybir.dt.float16
BF16 = mybir.dt.bfloat16
I32 = mybir.dt.int32
U8 = mybir.dt.uint8
ALU = mybir.AluOpType
ACT = mybir.ActivationFunctionType
AX = mybir.AxisListType

P = 128
EPS = 1e-5
ROUND = 12582912.0
PRODUCTS = ((0, 0), (1, 0), (0, 1))


def decoder_layer_kernel(nc, x, ctx, mask, a_wq, a_wk, a_wv, a_wo, c_wq, c_wk, c_wv, c_wo, W1, b1, W2, b2, out):
    B, S, D = x.shape
    H, DK = 16, D // 16
    NE, _, FF = W1.shape
    FC = FF // P
    TG = 4
    BG = TG * P // S
    NG = B * S // (TG * P)
    GT = TG * P
    VW = DK + 1
    NHP = H // 2
    A_SCALE = 1.0 / float(np.sqrt(D // 16))
    C_SCALE = 1.0 / float(np.sqrt(DK))
    N = B * S
    REGION = N + P
    DUMMY = NE * REGION
    ROW = D + 4
    SLOTS = N // P + NE - 1
    UNROLL = 6
    XB, YB = UNROLL, 3
    assert D == P and S == 64 and TG * P == 512 and NG == NE and SLOTS % YB == 0

    sorted_rows = nc.dram_tensor("sorted_rows", (DUMMY + P, ROW), F32).ap()
    sorted_flat = sorted_rows.rearrange("r c -> (r c)")

    x_flat = x.rearrange("b s d -> (b s d)")
    ctx_flat = ctx.rearrange("b s d -> (b s d)")
    W1_flat = W1.rearrange("e d f -> (e d f)")
    W2_flat = W2.rearrange("e f d -> (e f d)")
    out_rows = out.rearrange("b s d -> (b s) d")

    with ExitStack() as stack:
        def sb(name, shape, dt=F32):
            return stack.enter_context(nc.sbuf_tensor(name, shape, dt))

        def sem(name):
            return stack.enter_context(nc.semaphore(name))

        ident = sb("ident", [P, P])
        ident_bf = sb("ident_bf", [P, P], BF16)
        ones_bf = sb("ones_bf", [P, P], BF16)
        before = sb("before", [P, P], BF16)
        iota_e = sb("iota_e", [P, NE])
        iota_slot = sb("iota_slot", [P, SLOTS])
        region_e = sb("region_e", [P, NE])
        pad_rows = sb("pad_rows", [P, ROW])
        mask_u8 = sb("mask_u8", [P, S], U8)
        mask_f = sb("mask_f", [P, S])
        mask_two = sb("mask_two", [P, 2, S])
        mask_bias = sb("mask_bias", [P, S], BF16)
        any_key = sb("any_key", [P, 1])
        pick = sb("pick", [P, NHP, 2, S], BF16)
        negmax = sb("negmax", [P, 2, P], BF16)

        w_raw = sb("w_raw", [P, 8, P])
        aqk = sb("aqk", [P, 2, P], F16)
        avT = sb("avT", [P, 2, P], F16)
        aoT = sb("aoT", [P, 2, 2, P], F16)
        cqT = sb("cqT", [P, 2, P], F16)
        ckT = sb("ckT", [P, 2, P], F16)
        cvT = sb("cvT", [P, 2, P], F16)
        coT = sb("coT", [P, 2, P], F16)
        w_wo2 = sb("w_wo2", [P, 2, P])
        w_stage = sb("w_stage", [P, 2, FF])
        w1 = [[sb(f"w1_{('hi', 'lo')[a]}{c}", [P, (NE + 1) * P], F16) for c in range(FC)] for a in range(2)]
        w2 = [sb(f"w2_{c}", [P, (NE + 1) * 2 * P], F16) for c in range(FC)]
        b1_stage = sb("b1_stage", [FC, (NE + 1) * P])
        b1_rows = sb("b1_rows", [P, (NE + 1) * P], F16)
        b1_ones = sb("b1_ones", [P, FC, P], F16)
        b2_stage = sb("b2_stage", [P, NE * D])
        b2_rows = sb("b2_rows", [P, NE * D], F16)
        ones_h = sb("ones_h", [P, P], F16)

        x_in = sb("x_in", [P, TG, D])
        x_res = sb("x_res", [P, TG, D])
        xT = sb("xT", [P, 2, GT], F16)
        gT = sb("gT", [P, 2, GT], F16)
        av = sb("av", [P, 2, GT], F16)
        a_max = sb("a_max", [P, TG])
        a_shift = sb("a_shift", [P, TG, S])
        a_prob = sb("a_prob", [P, TG, 2, S])
        a_sum = sb("a_sum", [P, TG])
        a_rinv = sb("a_rinv", [P, TG])
        apT = sb("apT", [P, 2, GT], F16)
        a_out = sb("a_out", [P, TG, D])
        a_diag = sb("a_diag", [P, 2, TG, 2, 2, S], F16)
        a_r = sb("a_r", [P, TG, D])
        x1 = sb("x1", [P, NG * GT])

        c_in = sb("c_in", [P, TG, D])
        cT = sb("cT", [P, 2, GT], F16)
        kT = sb("kT", [P, 2, 2, GT // 2], F16)
        k_rows = sb("k_rows", [P, 2, 2, BG // 2, 4, S], F16)
        q_quad = sb("q_quad", [P, 2, 4, GT], F16)
        in_place4 = sb("in_place4", [P, 4, 4])
        in_place = sb("in_place", [P, 4])
        v_pair = sb("v_pair", [P, 2, BG, NHP, 2, VW], F16)
        x1q = sb("x1q", [P, TG, D])
        x1T = sb("x1T", [P, 2, GT], F16)
        qT = sb("qT", [P, 2, GT], F16)
        c_max = sb("c_max", [P, 2, H])
        p_f = sb("p_f", [P, 2, GT])
        p_hl = sb("p_hl", [P, 2, 2, 2, GT], F16)
        c_rinv = sb("c_rinv", [P, H])
        c_out = sb("c_out", [P, TG, D])
        oT = sb("oT", [P, 2, GT], F16)
        c_r = sb("c_r", [P, TG, D])
        x2 = sb("x2", [P, TG, ROW])

        st = sb("st", [P, 2 * TG, 6])
        ln = sb("ln", [P, 8, 2 * TG])
        ln_i = sb("ln_i", [P, 2, 2 * TG], I32)
        three_halves = sb("three_halves", [P, 2 * TG])
        rt = sb("rt", [P, 8, TG])
        onehot = sb("onehot", [P, TG, NE])
        onehot_bf = sb("onehot_bf", [P, TG, NE], BF16)
        place = sb("place", [P, TG, NE])
        pos_f = sb("pos_f", [P, TG])
        pos_i = sb("pos_i", [P, TG], I32)
        token_f = sb("token_f", [P, TG])
        base = sb("base", [P, NE])
        count = sb("count", [P, NE])
        pad_f = sb("pad_f", [P, NE])
        pad_i = sb("pad_i", [P, NE], I32)
        tiles_e = sb("tiles_e", [P, 4, NE])
        done_e = sb("done_e", [P, 2, SLOTS, NE])
        slot_f = sb("slot_f", [P, 8, SLOTS])
        slot_row = sb("slot_row", [P, SLOTS], I32)
        slot_d = sb("slot_d", [P, SLOTS], I32)

        xs = sb("xs", [P, XB, ROW])
        xsT = sb("xsT", [P, 2, 2, P], F16)
        h_hl = sb("h_hl", [P, 2, 2, FF], F16)
        y_r = sb("y_r", [P, 2, D])
        f_st = sb("f_st", [P, 2, 6])
        f_mv = sb("f_mv", [P, 2, 2])
        f_sd = sb("f_sd", [P, 2, 2])
        y_out = sb("y_out", [P, YB, D])
        y_id = sb("y_id", [P, YB, 1], I32)
        eps_t = sb("eps_t", [P, 1])

        psum = [stack.enter_context(nc.psum_tensor(f"psum{i}", [P, 512], F32)) for i in range(8)]
        s_bank, t_bank = psum[0:2], psum[2:4]
        o_bank, m_bank, a_bank, b_bank = psum[4:8]

        names = """passed const_loaded wstage_loaded xin_loaded xres_loaded cin_loaded q_spread in_place_ready k_rows0_ready k_rows1_ready dve_step y_step
            consts_pool consts_dve zeroed pe_setup act_setup dve_setup wsplit_hi wsplit_lo
            xT_ps xT_hi xT_lo gT_ps gT_hi gT_lo av_ps av_hi av_lo as_ps as_shifted as_exp as_rinv
            apT_ps apT_hi apT_lo ao_ps ao_scaled adiag_hi adiag_lo ay_ps a_read x1_ready
            cT_ps cT_hi cT_lo kT_ps kT_hi kT_lo v_ps v_hi v_lo x1q_ready x1T_ps x1T_hi x1T_lo
            qT_ps qT_hi qT_lo s_ps max_ready mT_ps nm_hi nm_lo st_ps exp_ready p_hi p_lo pv_ps co_ready
            oT_ps oT_hi oT_lo cy_ps c_read x2_ready onehot_ready rank_ps rank_read pos_ready scattered
            ln_started newton_step newton_done tables_ready pads_ready pad_written b_loaded b_hi b_lo xsT_ps xsT_hi xsT_lo
            h_ps h_hi h_lo y_ps y_read y_var y_sd y_ready""".split()
        names += [f"xs_loaded{k}" for k in range(XB)] + [f"y_written{k}" for k in range(YB)]
        s = {n: sem(n) for n in names}

        def after(eng, name, value):
            if isinstance(value, int) and value <= 0:
                return
            eng.wait_ge(s[name], value)

        def counts(eng, *values):
            return [v if isinstance(v, int) else eng.snap(v) for v in values]

        def passed(eng):
            eng.sem_inc(s["passed"], 1)

        class Steps:
            def __init__(self, eng, name):
                self.eng, self.name, self.start, self.n = eng, name, 0, 0

            def link(self, ins):
                ins.then_inc(s[self.name], 1)
                self.n += 1
                self.eng.wait_ge(s[self.name], self.start + self.n)

        def real(g):
            return g is not None and (not isinstance(g, int) or 0 <= g < NG)

        def loop(eng, body, last_body, chain=None, steps=0):
            body(0)
            body(1)
            if chain is not None:
                first = chain.n
                with eng.Fori(2, NG - 2) as g:
                    chain.start, chain.n = first + (g - 2) * steps, 0
                    body(g)
                    assert chain.n == steps, chain.n
                chain.start, chain.n = first + (NG - 4) * steps, 0
            else:
                with eng.Fori(2, NG - 2) as g:
                    body(g)
            body(NG - 2)
            last_body(NG - 1)

        def by_parity(ap):
            return ap.rearrange("p (a n v) -> p a n v", a=2, v=DK)

        def even_odd(ap):
            return ap.rearrange("p (n a v) -> p a n v", a=2, v=DK)

        def bc(ap, shape):
            return ap.broadcast_to(shape)

        SETUP = ((0, aqk), (1, avT), (4, cqT), (5, ckT), (7, coT), (2, aoT[:, 0]), (3, aoT[:, 1]), (1, cvT))
        DVE_SETUP = len(SETUP) + 1
        IDENT_READY, SMALL_READY, POOL_CONSTS = 2, 9, 22
        ROUNDS = (SLOTS - 1) // UNROLL
        ZEROED = 14
        DVE_BODY = 28
        NEWTON_STEPS = 12

        def expert_w(i, part, e, c):
            return w1[part][c][:, bass.ds(e * P, P)] if i == 0 else w2[c][:, bass.ds(e * 2 * P, 2 * P)][:, part * P:part * P + P]

        def staged(i, c):
            return w_stage[:, i, c * P:c * P + P]

        def write_padding(eng, experts):
            for e in experts:
                at = eng.value_load(pad_i[0:1, e:e + 1], min_val=0, max_val=(DUMMY - P) * ROW)
                eng.dma_start(sorted_flat[bass.ds(at, P * ROW)].rearrange("(p c) -> p c", p=P), pad_rows[:])\
                    .then_inc(s["pad_written"], 16)

        def newton_steps(eng, link, cols):
            y, w, half = (ln[:, i, cols] for i in (5, 6, 7))
            for k in range(3):
                y_in = ln_i[:, 1, cols].bitcast(F32) if k == 0 else y
                link(eng.tensor_tensor(w, y_in, y_in, ALU.mult))
                link(eng.tensor_tensor(w, w, half, ALU.mult))
                link(eng.tensor_tensor(w, w, three_halves[:, cols], ALU.add))
                link(eng.tensor_tensor(y, w, y_in, ALU.mult))
            return eng.tensor_tensor(ln[:, 3, cols], ln[:, 4, cols], y, ALU.mult)

        def ln_columns(a, c):
            return slice(0 if real(a) else TG, 2 * TG if real(c) else TG)

        def bias_parts():
            return [(b1_rows[32:32 + FC, :], b1_stage[:], b1_rows[0:FC, :]),
                    (b2_rows[32:33, :], b2_stage[0:1, :], b2_rows[0:1, :]),
                    (b2_rows[96:97, :], b2_stage[64:65, :], b2_rows[64:65, :])]

        block = stack.enter_context(nc.Block())

        @block.sync
        def _(sp):
            def tokens(flat, at):
                return flat[bass.ds(at, GT * D)].rearrange("(t p d) -> p t d", t=TG, p=P)

            def load_x(g):
                at, used = counts(sp, g * GT * D, g)
                after(sp, "xT_ps", used)
                passed(sp)
                sp.dma_start(x_in[:], tokens(x_flat, at)).then_inc(s["xin_loaded"], 16)

            def load_res(g):
                at, used = counts(sp, g * GT * D, g)
                after(sp, "a_read", used)
                passed(sp)
                sp.dma_start(x_res[:], tokens(x_flat, at)).then_inc(s["xres_loaded"], 16)

            def load_ctx(g):
                at, used = counts(sp, g * GT * D, g)
                after(sp, "cT_ps", used)
                passed(sp)
                sp.dma_start(c_in[:], tokens(ctx_flat, at)).then_inc(s["cin_loaded"], 16)

            def load_expert(e):
                at, used = counts(sp, e * D * FF, 2 * e + 2 if real(e - 1) else 0)
                after(sp, "wsplit_lo", used)
                passed(sp)
                sp.dma_start(w_stage[:, 0, :], W1_flat[bass.ds(at, D * FF)].rearrange("(p f) -> p f", p=P))\
                    .then_inc(s["wstage_loaded"], 16)
                sp.dma_start(w_stage[:, 1, :].rearrange("p (c d) -> p c d", c=FC),
                             W2_flat[bass.ds(at, D * FF)].rearrange("(c p d) -> p c d", c=FC, p=P))\
                    .then_inc(s["wstage_loaded"], 16)

            def spread_q(g):
                split, used = counts(sp, g + 1, 2 * TG * g)
                sp.wait_ge(s["qT_lo"], split)
                passed(sp)
                after(sp, "st_ps", used)
                for n in range(4):
                    rows = slice(32 * n, 32 * n + 32)
                    sp.dma_start(q_quad[rows, :, n, :], qT[rows]).then_inc(s["q_spread"], 16)

            load_x(0)
            for n, w in enumerate((a_wq, a_wk, a_wv, a_wo, c_wq, c_wk, c_wv, c_wo)):
                sp.dma_start(w_raw[:, n, :], w).then_inc(s["const_loaded"], 16)
            for b in range(2):
                sp.dma_start(mask_u8[b * S:(b + 1) * S, :], mask[0, 0]).then_inc(s["const_loaded"], 16)
            load_ctx(0)
            load_res(0)
            b1_chunks = b1.rearrange("e (c p) -> c e p", p=P)
            sp.dma_start(b1_stage[:, 0:NE * P].rearrange("c (e p) -> c e p", p=P), b1_chunks).then_inc(s["b_loaded"], 16)
            sp.dma_start(b1_stage[:, NE * P:], b1_chunks[:, 0]).then_inc(s["b_loaded"], 16)
            b2_flat = b2.rearrange("e d -> (e d)").unsqueeze(0)
            sp.dma_start(b2_stage[0:1, :], b2_flat).then_inc(s["b_loaded"], 16)
            sp.dma_start(b2_stage[64:65, 0:(NE - 1) * D], b2_flat[:, D:]).then_inc(s["b_loaded"], 16)
            sp.dma_start(b2_stage[64:65, (NE - 1) * D:], b2_flat[:, 0:D]).then_inc(s["b_loaded"], 16)
            load_expert(0)
            sp.wait_ge(s["zeroed"], ZEROED)

            load_x(1)
            load_ctx(1)
            load_res(1)
            load_x(2)
            spread_q(0)
            load_res(2)

            def body(g):
                if real(g + 3):
                    load_x(g + 3)
                if real(g + 2):
                    load_ctx(g + 2)
                if real(g + 1):
                    load_expert(g + 1)
                    spread_q(g + 1)
                if real(g + 3):
                    load_res(g + 3)

            with sp.Fori(0, NG - 3) as g:
                body(g)
            for g in range(NG - 3, NG):
                body(g)

            sp.dma_start(sorted_flat[DUMMY * ROW:].rearrange("(p c) -> p c", p=P), pad_rows[:]).then_inc(s["pad_written"], 16)
            sp.wait_ge(s["pads_ready"], 1)
            write_padding(sp, range(0, NE, 2))

            sp.wait_ge(s["tables_ready"], 1)
            sp.wait_ge(s["scattered"], 16 * TG * NG)
            sp.wait_ge(s["pad_written"], 16 * (NE + 1))

            def load_slot(j, k):
                used, = counts(sp, j - XB + 1)
                at = sp.value_load(slot_row[0:1, bass.ds(j, 1)], min_val=0, max_val=DUMMY * ROW)
                after(sp, "y_var", used)
                passed(sp)
                sp.dma_start(xs[:, k, :], sorted_flat[bass.ds(at, P * ROW)].rearrange("(p c) -> p c", p=P))\
                    .then_inc(s[f"xs_loaded{k}"], 16)

            for j in range(XB):
                load_slot(j, j)
            with sp.Fori(1, SLOTS // XB) as i:
                for k in range(XB):
                    load_slot(XB * i + k, k)
            for j in range(SLOTS // XB * XB, SLOTS):
                load_slot(j, j % XB)
            for k in range(YB):
                sp.wait_ge(s[f"y_written{k}"], 16 * SLOTS // YB)

        @block.gpsimd
        def _(pool):
            done = [0]

            def const(ins):
                ins.then_inc(s["consts_pool"], 1)
                done[0] += 1
                pool.wait_ge(s["consts_pool"], done[0])

            diag = dict(compare_op=ALU.not_equal, fill=1.0, base=0, pattern=[[-1, P]], channel_multiplier=1)
            exact = dict(allow_small_or_imprecise_dtypes=True)
            const(pool.memset(ident[:], 0.0))
            const(pool.affine_select(out=ident[:], in_=ident[:], **diag))
            assert done[0] == IDENT_READY
            const(pool.memset(in_place4[:], 1.0))
            for sign in (1, -1):
                const(pool.affine_select(out=in_place4[:], in_=in_place4[:], compare_op=ALU.is_ge, fill=0.0,
                                         base=0 if sign == 1 else DK - 1, pattern=[[-sign * DK, 4], [-sign * 32, 4]],
                                         channel_multiplier=sign))
            const(pool.iota(iota_e[:], [[1, NE]], base=0, channel_multiplier=0, **exact))
            const(pool.iota(region_e[:], [[REGION, NE]], base=0, channel_multiplier=0, **exact))
            const(pool.iota(iota_slot[:], [[1, SLOTS]], base=0, channel_multiplier=0, **exact))
            const(pool.iota(token_f[:], [[P, TG]], base=-GT, channel_multiplier=1, **exact))
            assert done[0] == SMALL_READY
            const(pool.memset(before[:], 0.0))
            const(pool.memset(ident_bf[:], 0.0))
            const(pool.affine_select(out=ident_bf[:], in_=ident_bf[:], **diag))
            const(pool.affine_select(out=before[:], in_=before[:], compare_op=ALU.is_ge, fill=1.0, base=0,
                                     pattern=[[-1, P]], channel_multiplier=1))
            pool.wait_ge(s["zeroed"], ZEROED)
            for row in (0, 32):
                v = pick[row:row + H]
                const(pool.affine_select(out=v, in_=v, compare_op=ALU.not_equal, fill=1.0, base=0,
                                         pattern=[[-2, NHP], [-1, 2], [0, S]], channel_multiplier=1))
            v = pick[64:128]
            const(pool.affine_select(out=v, in_=v, compare_op=ALU.not_equal, fill=1.0, base=0,
                                     pattern=[[0, NHP], [0, 2], [-1, S]], channel_multiplier=1))
            const(pool.iota(pad_rows[:, D:D + 1].bitcast(I32), [[0, 1]], base=N, channel_multiplier=0))
            for row in (0, 32):
                const(pool.affine_select(out=b1_ones[:], in_=b1_ones[:], compare_op=ALU.not_equal, fill=1.0, base=-row,
                                         pattern=[[-1, FC], [0, P]], channel_multiplier=1))
            const(pool.memset(v_pair[:], 0.0))
            for a in range(2):
                const(pool.memset(v_pair[a * S:a * S + S, 0, :, :, a, DK:VW], 1.0))
            assert done[0] == POOL_CONSTS, done[0]

            def split_low(e, n):
                for i in range(2):
                    pool.wait_ge(s["wsplit_hi"], 2 * n + i + 1)
                    for c in range(FC):
                        ins = pool.tensor_tensor(expert_w(i, 1, e, c), staged(i, c), expert_w(i, 0, e, c), ALU.subtract)
                    ins.then_inc(s["wsplit_lo"], 1)

            def queries(g):
                ready, used = counts(pool, TG * (g + 1), g)
                pool.wait_ge(s["x1_ready"], ready)
                after(pool, "x1T_ps", used)
                pool.tensor_tensor(x1q[:].rearrange("p t d -> p (t d)"), x1[:, bass.ds(g * GT, GT)],
                                   bc(any_key[:, 0:1], [P, GT]), ALU.mult).then_inc(s["x1q_ready"], 1)

            def prob_low(g, t):
                n = TG * g + t
                for u in range(2):
                    pool.wait_ge(s["p_hi"], 2 * n + u + 1)
                    pool.tensor_tensor(p_hl[:, t % 2, u, 1, :], p_f[:, u, :], p_hl[:, t % 2, u, 0, :], ALU.subtract)\
                        .then_inc(s["p_lo"], 1)

            def scatter(g):
                ready, = counts(pool, g + 1)
                pool.wait_ge(s["pos_ready"], ready)
                passed(pool)
                for t in range(TG):
                    pool.indirect_dma_start(out=sorted_rows, out_offset=bass.IndirectOffsetOnAxis(ap=pos_i[:, t:t + 1], axis=0),
                                            in_=x2[:, t, :], in_offset=None).then_inc(s["scattered"], 16)

            chain = Steps(pool, "newton_step")

            def newton(n, a, c):
                pool.wait_ge(s["ln_started"], n)
                newton_steps(pool, chain.link, ln_columns(a, c)).then_inc(s["newton_done"], 1)

            def body(g):
                prob_low(g, 0)
                if real(g + 1):
                    queries(g + 1)
                prob_low(g, 1)
                prob_low(g, 2)
                prob_low(g, 3)
                if real(g - 2):
                    scatter(g - 2)
                if real(g + 2) or real(g - 1):
                    newton(g + 3, g + 2, g - 1)
                if real(g + 1):
                    split_low(g + 1, g + 2)

            newton(1, 0, None)
            queries(0)
            pool.wait_ge(s["x1q_ready"], 1)
            for n, (rows, src, hi) in enumerate(bias_parts()):
                pool.wait_ge(s["b_hi"], n + 1)
                pool.tensor_tensor(rows, src, hi, ALU.subtract).then_inc(s["b_lo"], 1)
                pool.wait_ge(s["b_lo"], n + 1)
            split_low(0, 0)
            split_low(NE, 1)
            newton(2, 1, None)
            def last_body(g):
                prob_low(g, 0)
                newton(NG + 2, None, g - 1)
                prob_low(g, 1)
                scatter(g - 2)
                prob_low(g, 2)
                prob_low(g, 3)
                scatter(g - 1)

            loop(pool, body, last_body, chain, NEWTON_STEPS)
            scatter(NG - 1)

            def write_rows(j, k):
                pool.wait_ge(s["y_ready"], j + 1)
                passed(pool)
                pool.indirect_dma_start(out=out_rows, out_offset=bass.IndirectOffsetOnAxis(ap=y_id[:, k, :], axis=0),
                                        in_=y_out[:, k, :], in_offset=None,
                                        bounds_check=last_token, oob_is_err=False).then_inc(s[f"y_written{k}"], 16)

            last_token = pool.to_reg(N - 1)
            with pool.Fori(0, SLOTS // YB) as i:
                for k in range(YB):
                    write_rows(YB * i + k, k)

        @block.tensor
        def _(pe):
            def transposes(dst, src, n, name):
                for t in range(n):
                    ins = pe.transpose(dst[:, t * P:(t + 1) * P], src[:, t, :], ident[:])
                ins.then_inc(s[name], 1)

            def product(dst, lhsT, rhs, last=True, first=True):
                for i, (a, b) in enumerate(PRODUCTS):
                    ins = pe.matmul(dst, lhsT(a), rhs(b), start=first and i == 0, stop=last and i == 2)
                return ins

            def A_x(g):
                pe.wait_ge(s["xin_loaded"], 16 * (g + 1))
                after(pe, "a_read", g)
                transposes(a_bank, x_in, TG, "xT_ps")

            def A_g(g):
                pe.wait_ge(s["xT_lo"], g + 1)
                product(a_bank[:], lambda i: aqk[:, i, :], lambda i: xT[:, i, :]).then_inc(s["gT_ps"], 1)

            def A_v(g):
                pe.wait_ge(s["gT_lo"], g + 1)
                for t in range(TG):
                    cols = slice(t * P, t * P + P)
                    ins = product(a_bank[:, cols], lambda i: xT[:, i, cols], lambda i: avT[:, i, :])
                ins.then_inc(s["av_ps"], 1)

            def A_s(g):
                pe.wait_ge(s["av_lo"], g + 1)
                for t in range(TG):
                    for i, (a, b) in enumerate(PRODUCTS):
                        for q in range(2):
                            cols = slice(t * P + q * S, t * P + q * S + S)
                            ins = pe.matmul(a_bank[q * S:q * S + S, t * S:t * S + S], gT[:, a, cols], xT[:, b, cols],
                                            start=i == 0, stop=i == 2)
                ins.then_inc(s["as_ps"], 1)

            def A_p(g):
                pe.wait_ge(s["as_exp"], 2 * (g + 1))
                transposes(a_bank, a_prob[:].rearrange("p t b k -> p t (b k)"), TG, "apT_ps")

            def A_o(g):
                pe.wait_ge(s["apT_lo"], g + 1)
                for t in range(TG):
                    cols = slice(t * P, t * P + P)
                    ins = product(a_bank[:, cols], lambda i: apT[:, i, cols], lambda i: av[:, i, cols])
                ins.then_inc(s["ao_ps"], 1)

            def A_y(g):
                pe.wait_ge(s["adiag_lo"], 2 * (g + 1))
                for t in range(TG):
                    for h in range(2):
                        ins = product(a_bank[:, t * P:t * P + P],
                                      lambda i: a_diag[:, i, t, h, :, :].rearrange("p b r -> p (b r)"),
                                      lambda i: aoT[:, h, i, :], first=h == 0, last=h == 1)
                ins.then_inc(s["ay_ps"], 1)

            def K_x(g):
                pe.wait_ge(s["cin_loaded"], 16 * (g + 1))
                if real(g - 2):
                    pe.wait_ge(s["c_read"], g - 1)
                elif real(g - 1):
                    pe.wait_ge(s["v_lo"], 4 * g)
                transposes(b_bank, c_in, TG, "cT_ps")

            def K_k(g):
                pe.wait_ge(s["cT_lo"], g + 1)
                product(b_bank[:], lambda i: ckT[:, i, :], lambda i: cT[:, i, :]).then_inc(s["kT_ps"], 1)

            def K_v(g, u):
                if u == 0:
                    pe.wait_ge(s["qT_lo"], g + 1)
                else:
                    pe.wait_ge(s["v_lo"], 4 * g + 2)
                for b in range(BG // 2):
                    col = (u * BG // 2 + b) * S
                    for i, (m, n) in enumerate(PRODUCTS):
                        for a in range(2):
                            ins = pe.matmul(b_bank[a * S:a * S + S, b * S:b * S + S], cT[:, m, col:col + S],
                                            cvT[:, n, a * S:a * S + S], start=i == 0, stop=i == 2)
                ins.then_inc(s["v_ps"], 1)

            def B_x(g):
                pe.wait_ge(s["x1q_ready"], g + 1)
                pe.wait_ge(s["kT_lo"], g + 1)
                transposes(b_bank, x1q, TG, "x1T_ps")

            def B_q(g):
                pe.wait_ge(s["x1T_lo"], g + 1)
                product(b_bank[:], lambda i: cqT[:, i, :], lambda i: x1T[:, i, :]).then_inc(s["qT_ps"], 1)

            def T_s(g, t):
                n = TG * g + t
                pe.wait_ge(s["q_spread"], 16 * 4 * (g + 1))
                pe.wait_ge(s[f"k_rows{t // 2}_ready"], g + 1)
                for u in range(2):
                    after(pe, "max_ready", 2 * (n - 1) + u + 1 if not isinstance(n, int) or n else 0)
                    for m in range(2):
                        for q in range(2):
                            cols = slice(t * P + q * S, t * P + q * S + S)
                            pe.matmul(s_bank[u][q * S:q * S + S, m * 4 * S:(m + 1) * 4 * S], q_quad[:, 0, 2 * u + m, cols],
                                      k_rows[:, t // 2, 0, 2 * (t % 2) + q].rearrange("p j k -> p (j k)"),
                                      start=m == 0, stop=False, skip_group_check=True)
                    pe.matmul(s_bank[u][:], ident_bf[:], bc(mask_bias[:].unsqueeze(1), [P, NHP, S]),
                              start=False, stop=True, skip_group_check=True).then_inc(s["s_ps"], 1)

            def T_m(g, t):
                n = TG * g + t
                pe.wait_ge(s["max_ready"], 2 * (n + 1))
                after(pe, "nm_lo", n)
                if t == 0:
                    after(pe, "rank_read", g - 2)
                pe.transpose(m_bank[0:H, 0:P], c_max[:, t % 2, :], ident[:]).then_inc(s["mT_ps"], 1)

            def T_t(g, t):
                n = TG * g + t
                pe.wait_ge(s["nm_lo"], n + 1)
                for u in range(2):
                    after(pe, "exp_ready", 2 * (n - 1) + u + 1 if not isinstance(n, int) or n else 0)
                    for hp in range(NHP // 2):
                        pair = u * NHP // 2 + hp
                        pe.matmul(t_bank[u][:, hp * P:hp * P + P], pick[:, pair].rearrange("p a k -> p (a k)"),
                                  negmax[:, t % 2, :], start=hp == 0, stop=False, skip_group_check=True)
                        for q in range(2):
                            cols = slice(t * P + q * S, t * P + q * S + S)
                            for i, (a, b) in enumerate(PRODUCTS):
                                ins = pe.matmul(t_bank[u][:, hp * P + q * S:hp * P + q * S + S],
                                                k_rows[:, t // 2, a, 2 * (t % 2) + q, 2 * (pair % 2):2 * (pair % 2) + 2]
                                                .rearrange("p j k -> p (j k)"), q_quad[:, b, pair // 2, cols],
                                                start=False, stop=i == 2 and hp == NHP // 2 - 1 and q == 1,
                                                skip_group_check=True)
                    ins.then_inc(s["st_ps"], 1)

            def T_v(g, t):
                n = TG * g + t
                after(pe, "co_ready", 2 * n)
                pe.wait_ge(s["v_lo"], 4 * g + 2 * (t // 2) + 2)
                for a, bs in ((0, (0, 1)), (1, (0,))):
                    for u in range(2):
                        pe.wait_ge(s[("p_hi", "p_lo")[a]], 2 * n + u + 1)
                        for hp in range(NHP // 2):
                            pair = u * NHP // 2 + hp
                            for b in bs:
                                ins = pe.matmul(o_bank[:, pair * 4 * VW:(pair + 1) * 4 * VW],
                                                p_hl[:, t % 2, u, a, hp * P:hp * P + P],
                                                v_pair[:, b, 2 * t:2 * t + 2, pair].rearrange("p b a v -> p b (a v)"),
                                                start=a + u + hp + b == 0, stop=a * u == 1 and hp == NHP // 2 - 1,
                                                skip_group_check=True)
                ins.then_inc(s["pv_ps"], 1)

            def C_o(g):
                pe.wait_ge(s["co_ready"], 2 * TG * (g + 1))
                if real(g + 1):
                    pe.wait_ge(s["v_lo"], 4 * (g + 2))
                transposes(b_bank, c_out, TG, "oT_ps")

            def C_y(g):
                pe.wait_ge(s["oT_lo"], g + 1)
                for t in range(TG):
                    cols = slice(t * P, t * P + P)
                    ins = product(b_bank[:, cols], lambda i: oT[:, i, cols], lambda i: coT[:, i, :])
                ins.then_inc(s["cy_ps"], 1)

            def C_rank(g, read):
                pe.wait_ge(s["onehot_ready"], g + 1)
                pe.wait_ge(s["nm_lo"], read)
                after(pe, "rank_read", g)
                rank = m_bank[:, 0:TG * NE].rearrange("p (t e) -> p t e", t=TG)
                for t in range(TG):
                    pe.matmul(m_bank[:, 64:64 + NE], ones_bf[:], onehot_bf[:, t, :], start=t == 0, stop=t == TG - 1)
                for t in range(TG - 1):
                    pe.matmul(rank[:, t + 1:TG, :], ones_bf[:], bc(onehot_bf[:, t, :].unsqueeze(1), [P, TG - 1 - t, NE]),
                              start=False, stop=False, skip_group_check=True)
                ins = pe.matmul(rank, before[:], onehot_bf[:], start=False, stop=True, skip_group_check=True)
                ins.then_inc(s["rank_ps"], 1)

            def body(g):
                nxt, far, prev = g + 1, g + 2, g - 1
                T_s(g, 0)
                if real(prev):
                    C_o(prev)
                T_m(g, 0)
                T_s(g, 1)
                if real(far):
                    A_x(far)
                if real(prev):
                    C_y(prev)
                T_m(g, 1)
                T_t(g, 0)
                T_s(g, 2)
                if real(far):
                    A_g(far)
                T_m(g, 2)
                T_t(g, 1)
                if real(nxt):
                    K_x(nxt)
                T_s(g, 3)
                T_v(g, 0)
                T_m(g, 3)
                if real(far):
                    A_v(far)
                if real(nxt):
                    K_k(nxt)
                T_t(g, 2)
                T_v(g, 1)
                if real(nxt):
                    B_x(nxt)
                if real(g - 2):
                    C_rank(g - 2, TG * (g + 1))
                if real(far):
                    A_s(far)
                T_t(g, 3)
                T_v(g, 2)
                if real(far):
                    A_p(far)
                if real(nxt):
                    B_q(nxt)
                if real(far):
                    A_o(far)
                T_v(g, 3)
                if real(nxt):
                    K_v(nxt, 0)
                if real(far):
                    A_y(far)
                if real(nxt):
                    K_v(nxt, 1)

            def weight(n, raw):
                pe.transpose(psum[SETUP[n][0]][:, 0:P], raw, ident[:]).then_inc(s["pe_setup"], 1)

            pe.wait_ge(s["consts_pool"], IDENT_READY)
            A_x(0)
            pe.wait_ge(s["const_loaded"], 16 * 10)
            pe.matmul(psum[0][:, 0:P], w_raw[:, 0, :], w_raw[:, 1, :], start=True, stop=True).then_inc(s["pe_setup"], 1)
            weight(1, w_raw[:, 2, :])
            weight(2, w_raw[:, 4, :])
            weight(3, w_raw[:, 5, :])
            pe.wait_ge(s["dve_setup"], 1)
            A_g(0)
            weight(4, w_raw[:, 7, :])
            pe.wait_ge(s["consts_dve"], 3)
            weight(5, w_wo2[:, 0, :])
            weight(6, w_wo2[:, 1, :])
            pe.wait_ge(s["dve_setup"], 2)
            A_v(0)
            weight(7, w_raw[:, 6, :])
            pe.transpose(psum[0][:, 0:S], mask_two[0:S].rearrange("p a k -> p (a k)"), ident[0:S, 0:S])\
                .then_inc(s["pe_setup"], 1)
            A_s(0)
            A_p(0)
            pe.wait_ge(s["dve_setup"], DVE_SETUP)
            K_x(0)
            A_o(0)
            K_k(0)
            A_y(0)
            A_x(1)
            A_g(1)
            B_x(0)
            A_v(1)
            B_q(0)
            A_s(1)
            K_v(0, 0)
            A_p(1)
            K_v(0, 1)
            A_o(1)
            A_y(1)
            def last_body(g):
                T_s(g, 0)
                C_o(g - 1)
                T_m(g, 0)
                T_s(g, 1)
                T_m(g, 1)
                T_t(g, 0)
                C_y(g - 1)
                T_s(g, 2)
                T_m(g, 2)
                T_t(g, 1)
                T_s(g, 3)
                C_rank(g - 2, TG * g + 3)
                T_v(g, 0)
                pe.wait_ge(s["rank_read"], g - 1)
                T_m(g, 3)
                T_t(g, 2)
                T_v(g, 1)
                T_t(g, 3)
                C_rank(g - 1, TG * NG)
                T_v(g, 2)
                T_v(g, 3)

            pe.wait_ge(s["consts_pool"], POOL_CONSTS)
            pe.wait_ge(s["zeroed"], ZEROED)
            loop(pe, body, last_body)
            C_o(NG - 1)
            C_y(NG - 1)
            C_rank(NG - 1, TG * NG)

            x_bank, h_bank, y_bank = psum[6:8], psum[0:2], psum[2:4]
            pe.wait_ge(s["tables_ready"], 1)
            pe.wait_ge(s["wsplit_lo"], 2 * (NE + 1))
            pe.wait_ge(s["b_lo"], 3)


            def F_x(i, k):
                j = UNROLL * i + k
                pe.wait_ge(s[f"xs_loaded{k % XB}"], 16 * (i + k // XB + 1))
                after(pe, "xsT_lo", j - 1)
                pe.transpose(x_bank[k % 2][:, 0:P], xs[:, k % XB, 0:D], ident[:]).then_inc(s["xsT_ps"], 1)

            def F_h(j, k, u, d):
                if u == 0:
                    pe.wait_ge(s["xsT_hi"], j + 1)
                pe.matmul(h_bank[u][:], b1_rows[:, bass.ds(d + u * P, P)], b1_ones[:].rearrange("p c t -> p (c t)"),
                          start=True, stop=False, skip_group_check=True)
                for a, b in PRODUCTS:
                    if u == 0 and b == 1:
                        pe.wait_ge(s["xsT_lo"], j + 1)
                    for c in range(FC):
                        ins = pe.matmul(h_bank[u][:, c * P:c * P + P], w1[a][c][:, bass.ds(d + u * P, P)],
                                        xsT[:, k % 2, b, :], start=False, stop=b == 1 and c == FC - 1, skip_group_check=True)
                ins.then_inc(s["h_ps"], 1)

            def F_y(j, k, u, d):
                both, half = y_bank[k % 2][:, 0:2 * D], y_bank[k % 2][:, 0:D]
                if u == 0:
                    after(pe, "y_read", j - 1)
                pe.wait_ge(s["h_hi"], 2 * j + u + 1)
                at = d * 2 + u * 2 * P
                for c in range(FC):
                    pe.matmul(both, h_hl[:, u, 0, c * P:c * P + P], w2[c][:, bass.ds(at, 2 * P)],
                              start=u == 0 and c == 0, stop=False, skip_group_check=True)
                if u == 0:
                    pe.matmul(half, ones_h[:], b2_rows[:, bass.ds(d, D)], start=False, stop=False, skip_group_check=True)
                pe.wait_ge(s["h_lo"], 2 * j + u + 1)
                for c in range(FC):
                    ins = pe.matmul(half, h_hl[:, u, 1, c * P:c * P + P], w2[c][:, bass.ds(at, P)],
                                    start=False, stop=u == 1 and c == FC - 1, skip_group_check=True)
                if u == 1:
                    ins.then_inc(s["y_ps"], 1)

            slot_regs = [pe.alloc_register(f"slot_expert{k}") for k in range(UNROLL + 1)]

            def experts(j, n):
                pe.load(slot_regs[:n], slot_d[0:1, bass.ds(j, n)])
                return [pe.snap(reg, min_val=0, max_val=(NE - 1) * D) for reg in slot_regs[:n]]

            def F_round(i, steps):
                d = experts(UNROLL * i, steps + 1)
                for k in range(steps):
                    j = UNROLL * i + k
                    if not isinstance(i, int) or j + 2 < SLOTS:
                        F_x(i, k + 2)
                    F_y(j, k, 0, d[k])
                    F_h(j + 1, k + 1, 0, d[k + 1])
                    F_y(j, k, 1, d[k])
                    F_h(j + 1, k + 1, 1, d[k + 1])

            F_x(0, 0)
            F_x(0, 1)
            d, = experts(0, 1)
            F_h(0, 0, 0, d)
            F_h(0, 0, 1, d)
            F_round(0, UNROLL)
            with pe.Fori(1, ROUNDS) as i:
                F_round(i, UNROLL)
            F_round(ROUNDS, SLOTS - 1 - UNROLL * ROUNDS)
            d, = experts(SLOTS - 1, 1)
            F_y(SLOTS - 1, SLOTS - 1, 0, d)
            F_y(SLOTS - 1, SLOTS - 1, 1, d)

        @block.scalar
        def _(act):
            def high(dst, src, name, **kw):
                act.activation(dst, src, ACT.Copy, **kw).then_inc(s[name], 1)

            act.wait_ge(s["zeroed"], ZEROED)
            def setup(first, last):
                for n in range(first, last):
                    act.wait_ge(s["pe_setup"], n + 1)
                    bank, dst = SETUP[n]
                    high(by_parity(dst[:, 0, :]) if n == 7 else dst[:, 0, :],
                         even_odd(psum[bank][:, 0:P]) if n == 7 else psum[bank][:, 0:P], "act_setup")

            def split_high(e, loaded):
                act.wait_ge(s["wstage_loaded"], 32 * loaded)
                for i in range(2):
                    for c in range(FC):
                        ins = act.activation(expert_w(i, 0, e, c), staged(i, c), ACT.Copy)
                    ins.then_inc(s["wsplit_hi"], 1)

            def plain(name, dst, bank):
                def step(g):
                    act.wait_ge(s[name + "_ps"], g + 1)
                    high(dst[:, 0, :], bank[:], name + "_hi")
                return step

            A_x, A_g, A_v = plain("xT", xT, a_bank), plain("gT", gT, a_bank), plain("av", av, a_bank)
            A_p, K_x = plain("apT", apT, a_bank), plain("cT", cT, b_bank)
            B_x, C_o = plain("x1T", x1T, b_bank), plain("oT", oT, b_bank)

            def A_s(g):
                act.wait_ge(s["as_shifted"], g + 1)
                after(act, "apT_ps", g)
                for b in range(2):
                    rows = slice(b * S, b * S + S)
                    act.activation(a_prob[rows, :, b, :], a_shift[rows], ACT.Exp, scale=A_SCALE).then_inc(s["as_exp"], 1)

            def A_o(g):
                act.wait_ge(s["ao_scaled"], g + 1)
                for b in range(2):
                    rows = slice(b * S, b * S + S)
                    for h in range(2):
                        src = a_out[rows].rearrange("p t (r h) -> p t h r", h=2)[:, :, h, :]
                        ins = act.activation(a_diag[rows, 0, :, h, b, :], src, ACT.Copy)
                    ins.then_inc(s["adiag_hi"], 1)

            def K_k(g):
                act.wait_ge(s["kT_ps"], g + 1)
                after(act, "k_rows0_ready", g)
                high(kT[:, :, 0, :], b_bank[:].rearrange("p (u k) -> p u k", u=2), "kT_hi")

            def K_rows(g):
                act.wait_ge(s["kT_lo"], g + 1)
                after(act, "st_ps", 2 * TG * g)
                for j in range(4):
                    ins = act.activation(k_rows[:, 1, :, :, j, :].rearrange("p i b k -> p (i b) k"),
                                         kT[:, 1].rearrange("p i (b k) -> p (i b) k", k=S), ACT.Identity,
                                         scale=in_place[:, j:j + 1])
                ins.then_inc(s["k_rows1_ready"], 1)

            def norms_finish(n, a, c):
                act.wait_ge(s["newton_done"], n)
                if real(c):
                    after(act, "scattered", 16 * TG * c)
                passed(act)
                for g, r, first, name in ((a, a_r, 0, "x1_ready"), (c, c_r, TG, "x2_ready")):
                    if real(g):
                        for t in range(TG):
                            m = first + t
                            dst = x1[:, bass.ds(g * GT + t * D, D)] if first == 0 else x2[:, t, 0:D]
                            act.activation(dst, r[:, t, :], ACT.Identity, bias=ln[:, 3, m:m + 1],
                                           scale=ln[:, 5, m:m + 1]).then_inc(s[name], 1)

            def K_v(g, u):
                act.wait_ge(s["v_ps"], 2 * g + u + 1)
                after(act, "pv_ps", TG * (g - 1) + 2 * u + 2 if not isinstance(g, int) or g else 0)
                for a in range(2):
                    rows = slice(a * S, a * S + S)
                    src = b_bank[rows, 0:GT // 2].rearrange("p (b n v) -> p b n v", b=BG // 2, v=DK)
                    high(v_pair[rows, 0, u * BG // 2:(u + 1) * BG // 2, :, a, 0:DK], src, "v_hi")

            def B_q(g):
                act.wait_ge(s["qT_ps"], g + 1)
                high(qT[:, 0, :], b_bank[:], "qT_hi", scale=C_SCALE)

            def T_m(g, t):
                act.wait_ge(s["mT_ps"], TG * g + t + 1)
                high(negmax[0:H, t % 2, :], m_bank[0:H, 0:P], "nm_hi", scale=-1.0)

            def T_t(g, t):
                n = TG * g + t
                for u in range(2):
                    act.wait_ge(s["st_ps"], 2 * n + u + 1)
                    after(act, "p_lo", 2 * (n - 1) + u + 1 if not isinstance(n, int) or n else 0)
                    act.activation(p_f[:, u, :], t_bank[u][:], ACT.Exp).then_inc(s["exp_ready"], 1)
                    act.wait_ge(s["exp_ready"], 2 * n + u + 1)
                    after(act, "pv_ps", n - 1)
                    high(p_hl[:, t % 2, u, 0, :], p_f[:, u, :], "p_hi")

            def body(g):
                nxt, far, prev = g + 1, g + 2, g - 1
                if real(prev):
                    C_o(prev)
                T_m(g, 0)
                if real(far):
                    A_x(far)
                if real(nxt) or real(g - 2):
                    norms_finish(g + 2, nxt, g - 2)
                T_m(g, 1)
                T_t(g, 0)
                if real(far):
                    A_g(far)
                T_m(g, 2)
                T_t(g, 1)
                if real(nxt):
                    K_x(nxt)
                T_m(g, 3)
                if real(far):
                    A_v(far)
                if real(nxt):
                    K_k(nxt)
                T_t(g, 2)
                if real(nxt):
                    B_x(nxt)
                if real(far):
                    A_s(far)
                T_t(g, 3)
                if real(far):
                    A_p(far)
                if real(nxt):
                    B_q(nxt)
                if real(far):
                    A_o(far)
                if real(nxt):
                    K_v(nxt, 0)
                    K_rows(nxt)
                    K_v(nxt, 1)
                    split_high(nxt, g + 2)

            A_x(0)
            setup(0, 4)
            A_g(0)
            setup(4, 7)
            A_v(0)
            setup(7, 8)
            act.wait_ge(s["pe_setup"], len(SETUP) + 1)
            for k in range(2):
                for q in range(2):
                    high(negmax[64:128, k, q * S:q * S + S], psum[0][64:128, 0:S], "act_setup")
            A_s(0)
            A_p(0)
            K_x(0)
            A_o(0)
            K_k(0)
            A_x(1)
            act.wait_ge(s["in_place_ready"], 1)
            K_rows(0)
            A_g(1)
            norms_finish(1, 0, None)
            B_x(0)
            A_v(1)
            B_q(0)
            A_s(1)
            act.wait_ge(s["consts_pool"], POOL_CONSTS)
            K_v(0, 0)
            A_p(1)
            K_v(0, 1)
            A_o(1)
            act.wait_ge(s["b_loaded"], 16 * 5)
            for rows, src, hi in bias_parts():
                high(hi, src, "b_hi")
            split_high(0, 1)
            split_high(NE, 1)
            def last_body(g):
                C_o(g - 1)
                T_m(g, 0)
                norms_finish(g + 2, None, g - 2)
                T_m(g, 1)
                T_t(g, 0)
                T_m(g, 2)
                T_t(g, 1)
                T_m(g, 3)
                T_t(g, 2)
                norms_finish(NG + 2, None, g - 1)
                T_t(g, 3)

            loop(act, body, last_body)
            C_o(NG - 1)
            norms_finish(NG + 3, None, NG - 1)
            act.wait_ge(s["pads_ready"], 1)
            write_padding(act, range(1, NE, 2))


            x_bank, h_bank = psum[6:8], psum[0:2]

            def F_x(j, k):
                act.wait_ge(s["xsT_ps"], j + 1)
                high(xsT[:, k % 2, 0, :], x_bank[k % 2][:, 0:P], "xsT_hi")

            def F_h(j, u):
                act.wait_ge(s["h_ps"], 2 * j + u + 1)
                act.activation(h_hl[:, u, 0, :], h_bank[u][:], ACT.Relu).then_inc(s["h_hi"], 1)

            def F_sd(j, k):
                act.wait_ge(s["y_var"], j + 1)
                act.activation(f_sd[:, k % 2, 0:1], f_mv[:, k % 2, 1:2], ACT.Sqrt, bias=eps_t[:, 0:1]).then_inc(s["y_sd"], 1)

            def F_round(i, steps):
                for k in range(steps):
                    j = UNROLL * i + k
                    if not isinstance(i, int) or j + 2 < SLOTS:
                        F_x(j + 2, k)
                    F_h(j + 1, 0)
                    F_h(j + 1, 1)
                    F_sd(j, k)

            F_x(0, 0)
            F_x(1, 1)
            F_h(0, 0)
            F_h(0, 1)
            F_round(0, UNROLL)
            with act.Fori(1, ROUNDS) as i:
                F_round(i, UNROLL)
            F_round(ROUNDS, SLOTS - 1 - UNROLL * ROUNDS)
            F_sd(SLOTS - 1, SLOTS - 1)

        @block.vector
        def _(dve):
            chain = Steps(dve, "dve_step")
            link = chain.link

            for tensor, value in ((eps_t, EPS), (negmax, 0.0), (pick, 0.0), (b1_ones, 0.0), (a_prob, 0.0), (a_diag, 0.0),
                                  (q_quad, 0.0), (pad_rows, 0.0), (b1_rows, 0.0), (b2_rows, 0.0), (ones_bf, 1.0),
                                  (ones_h, 1.0), (three_halves, 1.5), (x2, 0.0)):
                dve.memset(tensor[:], value).then_inc(s["zeroed"], 1)
            def setup(first, last):
                for n in range(first, last):
                    dve.wait_ge(s["act_setup"], n + 1)
                    bank, dst = SETUP[n]
                    if n == 7:
                        ins = dve.tensor_tensor(by_parity(dst[:, 1, :]), even_odd(psum[bank][:, 0:P]), by_parity(dst[:, 0, :]),
                                                ALU.subtract)
                    else:
                        ins = dve.tensor_tensor(dst[:, 1, :], psum[bank][:, 0:P], dst[:, 0, :], ALU.subtract)
                    ins.then_inc(s["dve_setup"], 1)

            def low(dst, src, hi, hi_name, count, name):
                dve.wait_ge(s[hi_name], count)
                dve.tensor_tensor(dst, src, hi, ALU.subtract).then_inc(s[name], 1)

            def k_low(g):
                low(kT[:, :, 1, :], b_bank[:].rearrange("p (u k) -> p u k", u=2), kT[:, :, 0, :], "kT_hi", g + 1, "kT_lo")

            def plain(name, dst, bank):
                return lambda g: low(dst[:, 1, :], bank[:], dst[:, 0, :], name + "_hi", g + 1, name + "_lo")

            A_x, A_g, A_v = plain("xT", xT, a_bank), plain("gT", gT, a_bank), plain("av", av, a_bank)
            A_p, K_x, K_k = plain("apT", apT, a_bank), plain("cT", cT, b_bank), k_low
            B_x, C_o = plain("x1T", x1T, b_bank), plain("oT", oT, b_bank)

            def norms_start(a, c):
                cols = ln_columns(a, c)
                after(dve, "x1_ready", TG * a if real(a) else 0)
                after(dve, "x2_ready", TG * c if real(c) else 0)
                for g, read, r, first in ((a, "a_read", a_r, 0), (c, "c_read", c_r, TG)):
                    if real(g):
                        dve.wait_ge(s[read], g + 1)
                        for t in range(TG):
                            ins = dve.bn_stats(st[:, first + t, :], r[:, t, :])
                link(ins)
                total, diff, m2, v, negmean, y, w, half = (ln[:, i, cols] for i in range(8))
                dve.tensor_tensor(total, st[:, cols, 1], st[:, cols, 4], ALU.add)
                dve.tensor_tensor(m2, st[:, cols, 2], st[:, cols, 5], ALU.add)
                link(dve.tensor_tensor(diff, st[:, cols, 1], st[:, cols, 4], ALU.subtract))
                link(dve.tensor_tensor(diff, diff, diff, ALU.mult))
                link(dve.scalar_tensor_tensor(out=m2, in0=diff, scalar=D / 4.0, in1=m2, op0=ALU.mult, op1=ALU.add))
                dve.tensor_scalar(negmean, total, -0.5, None, ALU.mult)
                link(dve.tensor_scalar(v, m2, 1.0 / D, EPS, ALU.mult, ALU.add))
                dve.tensor_scalar(half, v, -0.5, None, ALU.mult)
                link(dve.tensor_scalar(ln_i[:, 0, cols], v.bitcast(I32), 1, None, ALU.arith_shift_right))
                dve.tensor_scalar(ln_i[:, 1, cols], ln_i[:, 0, cols], -1.0, 1597463007.0, ALU.mult, ALU.add)\
                    .then_inc(s["ln_started"], 1)

            def A_s(g):
                dve.wait_ge(s["as_ps"], g + 1)
                scores = a_bank[:, 0:TG * S].rearrange("p (t k) -> p t k", t=TG)
                link(dve.tensor_reduce(a_max[:], scores, AX.X, ALU.max))
                dve.tensor_tensor(a_shift[:], scores, bc(a_max[:].unsqueeze(2), [P, TG, S]), ALU.subtract)\
                    .then_inc(s["as_shifted"], 1)

            def A_sum(g):
                dve.wait_ge(s["as_exp"], 2 * (g + 1))
                link(dve.tensor_reduce(a_sum[:], a_prob[:].rearrange("p t b k -> p t (b k)"), AX.X, ALU.add))
                link(dve.reciprocal(a_rinv[:], a_sum[:]))

            def A_o(g):
                dve.wait_ge(s["ao_ps"], g + 1)
                dve.tensor_tensor(a_out[:], a_bank[:].rearrange("p (t d) -> p t d", t=TG),
                                  bc(a_rinv[:].unsqueeze(2), [P, TG, D]), ALU.mult).then_inc(s["ao_scaled"], 1)
                for b in range(2):
                    rows = slice(b * S, b * S + S)
                    dve.wait_ge(s["adiag_hi"], 2 * g + b + 1)
                    for h in range(2):
                        src = a_out[rows].rearrange("p t (r h) -> p t h r", h=2)[:, :, h, :]
                        ins = dve.tensor_tensor(a_diag[rows, 1, :, h, b, :], src, a_diag[rows, 0, :, h, b, :], ALU.subtract)
                    ins.then_inc(s["adiag_lo"], 1)

            def A_y(g):
                dve.wait_ge(s["ay_ps"], g + 1)
                dve.wait_ge(s["xres_loaded"], 16 * (g + 1))
                after(dve, "x1_ready", TG * g)
                dve.tensor_tensor(a_r[:], a_bank[:].rearrange("p (t d) -> p t d", t=TG), x_res[:], ALU.add)\
                    .then_inc(s["a_read"], 1)

            def K_rows(g):
                dve.wait_ge(s["kT_lo"], g + 1)
                after(dve, "st_ps", 2 * TG * (g - 1) + 4)
                for j in range(4):
                    ins = dve.tensor_scalar(k_rows[:, 0, :, :, j, :].rearrange("p i b k -> p (i b) k"),
                                            kT[:, 0].rearrange("p i (b k) -> p (i b) k", k=S),
                                            in_place[:, j:j + 1], None, ALU.mult)
                ins.then_inc(s["k_rows0_ready"], 1)

            def K_v(g, u):
                for a in range(2):
                    rows = slice(a * S, a * S + S)
                    src = b_bank[rows, 0:GT // 2].rearrange("p (b n v) -> p b n v", b=BG // 2, v=DK)
                    seq = slice(u * BG // 2, (u + 1) * BG // 2)
                    low(v_pair[rows, 1, seq, :, a, 0:DK], src, v_pair[rows, 0, seq, :, a, 0:DK],
                        "v_hi", 4 * g + 2 * u + a + 1, "v_lo")

            def B_q(g):
                dve.wait_ge(s["qT_hi"], g + 1)
                dve.scalar_tensor_tensor(out=qT[:, 1, :], in0=b_bank[:], scalar=C_SCALE, in1=qT[:, 0, :],
                                         op0=ALU.mult, op1=ALU.subtract).then_inc(s["qT_lo"], 1)

            def T_s(g, t):
                n = TG * g + t
                after(dve, "mT_ps", n - 1)
                for u in range(2):
                    dve.wait_ge(s["s_ps"], 2 * n + u + 1)
                    dve.tensor_reduce(c_max[:, t % 2, u * NHP:(u + 1) * NHP],
                                      s_bank[u][:].rearrange("p (h k) -> p h k", h=NHP), AX.X, ALU.max)\
                        .then_inc(s["max_ready"], 1)

            def T_m(g, t):
                n = TG * g + t
                dve.wait_ge(s["nm_hi"], n + 1)
                dve.scalar_tensor_tensor(out=negmax[32:32 + H, t % 2, :], in0=m_bank[0:H, 0:P], scalar=-1.0,
                                         in1=negmax[0:H, t % 2, :], op0=ALU.mult, op1=ALU.subtract).then_inc(s["nm_lo"], 1)

            def T_v(g, t):
                n = TG * g + t
                dve.wait_ge(s["pv_ps"], n + 1)
                if t == 0:
                    after(dve, "oT_ps", g)
                sums = o_bank[:, 0:NHP * 4 * VW].rearrange("p (n b a v) -> p n b a v", b=2, a=2, v=VW)[:, :, 0, :, DK]
                link(dve.reciprocal(c_rinv[:].rearrange("p (n a) -> p n a", a=2), sums))
                for b in range(2):
                    rows = slice(b * S, b * S + S)
                    o = o_bank[rows, 0:NHP * 4 * VW].rearrange("p (n b a v) -> p n b a v", b=2, a=2, v=VW)[:, :, b]
                    dve.tensor_tensor(c_out[rows, t, :].rearrange("p (n a v) -> p n a v", a=2, v=DK), o[:, :, :, 0:DK],
                                      bc(c_rinv[rows].rearrange("p (n a) -> p n a", a=2).unsqueeze(3), [S, NHP, 2, DK]),
                                      ALU.mult).then_inc(s["co_ready"], 1)

            def C_y(g):
                dve.wait_ge(s["cy_ps"], g + 1)
                after(dve, "x2_ready", TG * g)
                dve.tensor_tensor(c_r[:].rearrange("p t d -> p (t d)"), b_bank[:], x1[:, bass.ds(g * GT, GT)], ALU.add)\
                    .then_inc(s["c_read"], 1)

            def C_route(g):
                after(dve, "scattered", 16 * TG * g)
                link(dve.tensor_scalar(token_f[:], token_f[:], float(GT), None, ALU.add))
                dve.tensor_copy(x2[:, :, D].bitcast(I32), token_f[:])
                dve.wait_ge(s["x2_ready"], TG * (g + 1))
                v, mag, near, over, sign, trunc, m8, h = (rt[:, i, :] for i in range(8))
                link(dve.tensor_tensor(v, x2[:, :, 0], x2[:, :, 1], ALU.add))
                link(dve.tensor_scalar(sign, v, 0.0, 2.0, ALU.is_ge, ALU.mult))
                link(dve.scalar_tensor_tensor(out=mag, in0=sign, scalar=-1.0, in1=v, op0=ALU.add, op1=ALU.mult))
                link(dve.tensor_scalar(near, mag, ROUND, ROUND, ALU.add, ALU.subtract))
                link(dve.tensor_tensor(over, near, mag, ALU.is_gt))
                link(dve.tensor_tensor(near, near, over, ALU.subtract))
                link(dve.scalar_tensor_tensor(out=trunc, in0=sign, scalar=-1.0, in1=near, op0=ALU.add, op1=ALU.mult))
                link(dve.tensor_scalar(m8, trunc, 1.0 / NE, -0.4375, ALU.mult, ALU.add))
                link(dve.tensor_scalar(m8, m8, ROUND, ROUND, ALU.add, ALU.subtract))
                link(dve.scalar_tensor_tensor(out=h, in0=m8, scalar=-float(NE), in1=trunc, op0=ALU.mult, op1=ALU.add))
                link(dve.tensor_tensor(onehot[:], bc(iota_e[:].unsqueeze(1), [P, TG, NE]), bc(h.unsqueeze(2), [P, TG, NE]),
                                       ALU.is_equal))
                dve.tensor_copy(onehot_bf[:], onehot[:]).then_inc(s["onehot_ready"], 1)

            def C_rank(g):
                dve.wait_ge(s["rank_ps"], g + 1)
                after(dve, "scattered", 16 * TG * g)
                rank = m_bank[:, 0:TG * NE].rearrange("p (t e) -> p t e", t=TG)
                link(dve.tensor_tensor(place[:], rank, bc(base[:].unsqueeze(1), [P, TG, NE]), ALU.add))
                link(dve.tensor_tensor(place[:], place[:], onehot[:], ALU.mult))
                dve.tensor_tensor(base[:], m_bank[:, 64:64 + NE], base[:], ALU.add).then_inc(s["rank_read"], 1)
                link(dve.tensor_reduce(pos_f[:], place[:], AX.X, ALU.add))
                dve.tensor_copy(pos_i[:], pos_f[:]).then_inc(s["pos_ready"], 1)

            def body(g):
                nxt, far, prev = g + 1, g + 2, g - 1
                T_s(g, 0)
                T_m(g, 0)
                if real(prev):
                    C_o(prev)
                T_s(g, 1)
                if real(far):
                    A_x(far)
                if real(prev):
                    C_y(prev)
                T_s(g, 2)
                T_m(g, 1)
                if real(far):
                    A_g(far)
                if real(g - 2):
                    C_route(g - 2)
                T_m(g, 2)
                T_s(g, 3)
                if real(nxt):
                    K_x(nxt)
                T_v(g, 0)
                if real(far):
                    A_v(far)
                T_m(g, 3)
                if real(nxt):
                    K_k(nxt)
                T_v(g, 1)
                if real(far):
                    A_s(far)
                if real(nxt):
                    B_x(nxt)
                    K_rows(nxt)
                if real(far):
                    A_sum(far)
                T_v(g, 2)
                if real(far):
                    A_p(far)
                if real(g - 2):
                    C_rank(g - 2)
                if real(nxt):
                    B_q(nxt)
                if real(far):
                    A_o(far)
                T_v(g, 3)
                if real(nxt):
                    K_v(nxt, 0)
                if real(far):
                    A_y(far)
                if real(far) or real(prev):
                    norms_start(far, prev)
                if real(nxt):
                    K_v(nxt, 1)

            A_x(0)
            dve.wait_ge(s["const_loaded"], 16 * 10)
            link(dve.tensor_copy(mask_f[:], mask_u8[:]))
            dve.tensor_reduce(any_key[:], mask_f[:], AX.X, ALU.max).then_inc(s["consts_dve"], 1)
            link(dve.tensor_scalar(mask_two[:], bc(mask_f[:].unsqueeze(1), [P, 2, S]), 1.0, 1e9, ALU.subtract, ALU.mult))
            dve.tensor_copy(mask_bias[:], mask_two[:, 0, :]).then_inc(s["consts_dve"], 1)
            dve.tensor_copy(w_wo2[:].rearrange("p h (a q) -> p h a q", a=2),
                            bc(w_raw[:, 3, :].rearrange("p (h q) -> p h q", h=2).unsqueeze(2), [P, 2, 2, S]))\
                .then_inc(s["consts_dve"], 1)
            setup(0, 4)
            A_g(0)
            setup(4, 7)
            A_v(0)
            setup(7, 8)
            dve.wait_ge(s["act_setup"], len(SETUP) + 4)
            dve.memset(a_max[:], 0.0).then_inc(s["dve_setup"], 1)
            dve.wait_ge(s["dve_setup"], DVE_SETUP)
            A_s(0)
            A_sum(0)
            A_p(0)
            K_x(0)
            A_o(0)
            A_y(0)
            norms_start(0, None)
            dve.wait_ge(s["consts_pool"], SMALL_READY)
            dve.tensor_reduce(in_place[:], in_place4[:], AX.X, ALU.add).then_inc(s["in_place_ready"], 1)
            dve.wait_ge(s["in_place_ready"], 1)
            link(dve.tensor_copy(base[:], region_e[:]))
            K_k(0)
            K_rows(0)
            A_x(1)
            A_g(1)
            B_x(0)
            A_v(1)
            B_q(0)
            A_s(1)
            K_v(0, 0)
            A_sum(1)
            A_p(1)
            K_v(0, 1)
            A_o(1)
            A_y(1)
            norms_start(1, None)
            def last_body(g):
                T_s(g, 0)
                C_o(g - 1)
                T_m(g, 0)
                T_s(g, 1)
                T_m(g, 1)
                C_y(g - 1)
                T_s(g, 2)
                norms_start(None, g - 1)
                T_m(g, 2)
                C_route(g - 2)
                T_s(g, 3)
                C_rank(g - 2)
                T_v(g, 0)
                T_m(g, 3)
                T_v(g, 1)
                C_route(g - 1)
                C_rank(g - 1)
                T_v(g, 2)
                T_v(g, 3)

            loop(dve, body, last_body, chain, DVE_BODY)
            C_o(NG - 1)
            C_y(NG - 1)
            norms_start(None, NG - 1)
            dve.wait_ge(s["ln_started"], NG + 3)
            newton_steps(dve, link, ln_columns(None, NG - 1)).then_inc(s["newton_done"], 1)
            C_route(NG - 1)
            C_rank(NG - 1)

            dve.wait_ge(s["rank_read"], NG)
            link(dve.tensor_scalar(pad_f[:], base[:], float(ROW), None, ALU.mult))
            dve.tensor_copy(pad_i[:], pad_f[:]).then_inc(s["pads_ready"], 1)
            link(dve.tensor_tensor(count[:], base[:], region_e[:], ALU.subtract))
            link(dve.tensor_scalar(tiles_e[:, 0, :], count[:], 1.0 / P, (P - 1.0) / P - 0.49609375, ALU.mult, ALU.add))
            link(dve.tensor_scalar(tiles_e[:, 1, :], tiles_e[:, 0, :], ROUND, ROUND, ALU.add, ALU.subtract))
            a = 1
            for step in (1, 2, 4):
                b = 2 if a != 2 else 3
                link(dve.tensor_copy(tiles_e[:, b, 0:step], tiles_e[:, a, 0:step]))
                link(dve.tensor_tensor(tiles_e[:, b, step:NE], tiles_e[:, a, step:NE], tiles_e[:, a, 0:NE - step], ALU.add))
                a = b
            upto = bc(tiles_e[:, a, :].unsqueeze(1), [P, SLOTS, NE])
            link(dve.tensor_tensor(done_e[:, 0], upto, bc(iota_slot[:].unsqueeze(2), [P, SLOTS, NE]), ALU.is_le))
            link(dve.tensor_tensor(done_e[:, 1], done_e[:, 0], upto, ALU.mult))
            expert, first, row, wrow, t4, t5 = (slot_f[:, i, :] for i in range(6))
            dve.tensor_reduce(expert, done_e[:, 0], AX.X, ALU.add)
            link(dve.tensor_reduce(first, done_e[:, 1], AX.X, ALU.max))
            link(dve.tensor_tensor(row, iota_slot[:], first, ALU.subtract))
            link(dve.tensor_scalar(row, row, float(P), None, ALU.mult))
            link(dve.scalar_tensor_tensor(out=row, in0=expert, scalar=float(REGION), in1=row, op0=ALU.mult, op1=ALU.add))
            link(dve.tensor_scalar(row, row, float(DUMMY), None, ALU.min))
            link(dve.tensor_scalar(wrow, expert, NE - 1.0, None, ALU.min))
            dve.tensor_scalar(slot_row[:], row, float(ROW), None, ALU.mult)
            dve.tensor_scalar(slot_d[:], wrow, float(D), None, ALU.mult).then_inc(s["tables_ready"], 1)

            x_bank, h_bank, y_bank = psum[6:8], psum[0:2], psum[2:4]
            y_chain = Steps(dve, "y_step")

            def F_x(j, k):
                low(xsT[:, k % 2, 1, :], x_bank[k % 2][:, 0:P], xsT[:, k % 2, 0, :], "xsT_hi", j + 1, "xsT_lo")

            def F_h(j, u):
                dve.wait_ge(s["h_hi"], 2 * j + u + 1)
                dve.scalar_tensor_tensor(out=h_hl[:, u, 1, :], in0=h_bank[u][:], scalar=0.0, in1=h_hl[:, u, 0, :],
                                         op0=ALU.max, op1=ALU.subtract).then_inc(s["h_lo"], 1)

            def F_out(j, k, written):
                dve.wait_ge(s["y_ps"], j + 1)
                y_chain.link(dve.scalar_tensor_tensor(out=y_r[:, k % 2, :], in0=y_bank[k % 2][:, 0:D], scalar=0.5,
                                                      in1=xs[:, k % XB, 0:D], op0=ALU.mult, op1=ALU.add))
                dve.scalar_tensor_tensor(out=y_r[:, k % 2, :], in0=y_bank[k % 2][:, D:2 * D], scalar=0.5,
                                         in1=y_r[:, k % 2, :], op0=ALU.mult, op1=ALU.add).then_inc(s["y_read"], 1)
                dve.wait_ge(s["y_read"], j + 1)
                y_chain.link(dve.bn_stats(f_st[:, k % 2, :], y_r[:, k % 2, :]))
                after(dve, f"y_written{k % YB}", written)
                dve.tensor_copy(y_id[:, k % YB, :], xs[:, k % XB, D:D + 1].bitcast(I32))
                dve.bn_aggr(f_mv[:, k % 2, :], f_st[:, k % 2, :]).then_inc(s["y_var"], 1)

            def F_norm(j, k):
                dve.wait_ge(s["y_sd"], j + 1)
                y_chain.link(dve.reciprocal(f_sd[:, k % 2, 1:2], f_sd[:, k % 2, 0:1]))
                dve.tensor_scalar(y_out[:, k % YB, :], y_r[:, k % 2, :], f_mv[:, k % 2, 0:1], f_sd[:, k % 2, 1:2],
                                  ALU.subtract, ALU.mult).then_inc(s["y_ready"], 1)

            def F_round(i, steps):
                for k in range(steps):
                    j = UNROLL * i + k
                    if not isinstance(i, int) or j + 2 < SLOTS:
                        F_x(j + 2, k)
                    if not isinstance(i, int) or j > 0:
                        F_norm(j - 1, k + UNROLL - 1)
                    F_h(j + 1, 0)
                    F_out(j, k, 16 * (UNROLL // YB * i + k // YB))
                    F_h(j + 1, 1)

            F_x(0, 0)
            F_x(1, 1)
            F_h(0, 0)
            F_h(0, 1)
            F_round(0, UNROLL)
            first_round = y_chain.n
            with dve.Fori(1, ROUNDS) as i:
                y_chain.start, y_chain.n = first_round + (i - 1) * 3 * UNROLL, 0
                F_round(i, UNROLL)
                assert y_chain.n == 3 * UNROLL
            y_chain.start, y_chain.n = first_round + (ROUNDS - 1) * 3 * UNROLL, 0
            F_round(ROUNDS, SLOTS - 1 - UNROLL * ROUNDS)
            last = SLOTS - 1
            F_norm(last - 1, last - 1)
            F_out(last, last, 16 * (last // YB))
            F_norm(last, last)


_INS = ["x", "ctx_1024", "mask_1x1xSxS2_bf1", "L0_attn_wq", "L0_attn_wk", "L0_attn_wv", "L0_attn_wo",
        "L0_xattn_w_q", "L0_xattn_w_k", "L0_xattn_w_v", "L0_xattn_w_o",
        "L0_ffn_W1", "L0_ffn_b1", "L0_ffn_W2", "L0_ffn_b2"]


def kernel(**inputs):
    import concourse.bacc as _bacc
    from concourse.bass_utils import run_bass_kernel_spmd as _run

    nc = _bacc.Bacc("TRN2", target_bir_lowering=False, num_devices=1)
    arrays, args = {}, []
    for name in _INS:
        a = np.ascontiguousarray(inputs[name])
        if a.dtype == np.bool_:
            a = a.view(np.uint8)
        arrays[f"in_{name}"] = a
        args.append(nc.dram_tensor(f"in_{name}", a.shape, mybir.dt.from_np(a.dtype), kind="ExternalInput").ap())
    args.append(nc.dram_tensor("out_dram", arrays["in_x"].shape, F32, kind="ExternalOutput").ap())
    decoder_layer_kernel(nc, *args)
    r = _run(nc, [arrays], core_ids=[0])
    return r.results[0]["out_dram"]
```
